# Optimizing a Trainium2 kernel written in Bass

```python
import numpy as np
import jax
import jax.numpy as jnp

def _softmax(x, axis=-1):
    return jax.nn.softmax(x, axis=axis)

def _gelu(x):
    return jax.nn.gelu(x, approximate=True)

def _silu(x):
    return jax.nn.silu(x)

def _sigmoid(x):
    return jax.nn.sigmoid(x)

def _layernorm(x, axis=-1, eps=1e-05):
    m = jnp.mean(x, axis=axis, keepdims=True)
    v = jnp.var(x, axis=axis, keepdims=True)
    return (x - m) / jnp.sqrt(v + eps)

def _scatter_add(tgt, idx, src, axis=0):
    return tgt.at[idx].add(src)

def _segment_sum(src, seg, n):
    return jax.ops.segment_sum(src, seg, n)
kernel_name = 'mk_decoder_postln_d1_seqx_r4_79042a'

def setup_inputs(seed: int=0):
    np.random.seed(seed)
    _w = jnp.asarray

    def _rec_inputs():
        import jax
        import jax.numpy as jnp
        _rk = jax.random.key(seed)
        x = -0.000125 + 0.9999 * jax.random.normal(jax.random.fold_in(_rk, 1), (2, 512, 1024), jnp.float32)
        _lenS = 512 - jax.random.randint(jax.random.fold_in(_rk, 7), (2,), 0, max(1, 512 // 4) + 1, jnp.int32)
        _lenS2 = 1024 - jax.random.randint(jax.random.fold_in(_rk, 8), (2,), 0, max(1, 1024 // 4) + 1, jnp.int32)
        _ctx_4096P = jax.random.normal(jax.random.fold_in(_rk, 11), (2, 16, 1024), jnp.float32)
        _ctx_4096c = jax.random.dirichlet(jax.random.fold_in(_rk, 511), 0.3 * jnp.ones((16,), jnp.float32), (2, 1024))
        _ctx_4096t = jnp.einsum('bsk,bkd->bsd', _ctx_4096c, _ctx_4096P)
        _ctx_4096t = _ctx_4096t * jax.lax.rsqrt(jnp.mean(jnp.square(_ctx_4096t)) + 1e-12) * 0.953939
        ctx_4096 = -5.72187e-05 + 0.999849 * (_ctx_4096t + 0.3 * jax.random.normal(jax.random.fold_in(_rk, 611), (2, 1024, 1024), jnp.float32))
        return (x, ctx_4096)
    x, ctx_4096 = _rec_inputs()

    def _L0_attn_setup():
        import jax, jax.numpy as jnp
        import numpy as np
        HEADS = 32
        key = jax.random.key(seed)
        ks = jax.random.split(key, 5)
        H = 1024
        B, S = (2, 512)
        w_scale = 1.0 / np.sqrt(H)
        return {'x': jax.random.normal(ks[0], (B, S, H), dtype=jnp.float32), 'attn_qkvw': jax.random.normal(ks[1], (H, 3 * H), dtype=jnp.float32) * w_scale, 'attn_qkvb': jax.random.normal(ks[2], (3 * H,), dtype=jnp.float32) * 0.02, 'attn_ow': jax.random.normal(ks[3], (H, H), dtype=jnp.float32) * w_scale, 'attn_ob': jax.random.normal(ks[4], (H,), dtype=jnp.float32) * 0.02}
    _L0_attn_all = _L0_attn_setup()
    _L0_attn_in = {k: v for k, v in _L0_attn_all.items() if k in ('attn_qkvw', 'attn_qkvb', 'attn_ow', 'attn_ob')}
    del _L0_attn_all

    def _L0_xattn_setup():
        import jax, jax.numpy as jnp
        import numpy as np
        QMIN = 0.0
        QMAX = 255.0

        def fake_quant(x, scale, zp):
            s = scale.reshape(())
            z = zp.reshape(())
            q = jnp.clip(jnp.round(x / s + z), QMIN, QMAX)
            return (q - z) * s
        key = jax.random.key(seed)
        k1, k2 = jax.random.split(key)
        B, M, K, N = (4, 512, 1024, 1024)
        x1 = jax.random.normal(k1, (B, M, K), dtype=jnp.float32)
        x2 = jax.random.normal(k2, (B, K, N), dtype=jnp.float32)
        x1_scale = jnp.full((1,), 8.0 / 255.0, dtype=jnp.float32)
        x1_zp = jnp.full((1,), 128.0, dtype=jnp.float32)
        x2_scale = jnp.full((1,), 8.0 / 255.0, dtype=jnp.float32)
        x2_zp = jnp.full((1,), 128.0, dtype=jnp.float32)
        return {'x1': x1, 'x2': x2, 'x1_scale': x1_scale, 'x1_zp': x1_zp, 'x2_scale': x2_scale, 'x2_zp': x2_zp}
    _L0_xattn_all = _L0_xattn_setup()
    _L0_xattn_in = {k: v for k, v in _L0_xattn_all.items() if k in ('x1_scale', 'x1_zp', 'x2_scale', 'x2_zp')}
    del _L0_xattn_all

    def _L0_ffn_setup():
        import jax, jax.numpy as jnp
        import numpy as np
        R = 16
        NUM_EXPERTS = 8
        TOP_K = 2
        LORA_ALPHA = 32
        SCALING = LORA_ALPHA / R
        key = jax.random.key(seed)
        ks = jax.random.split(key, 6)
        d_in, d_out = (1024, 1024)
        x = jax.random.normal(ks[0], (4, 512, d_in), dtype=jnp.float32)
        W_base = jax.random.normal(ks[1], (d_out, d_in), dtype=jnp.float32) * 0.02
        b_base = jax.random.normal(ks[2], (d_out,), dtype=jnp.float32) * 0.02
        W_router = jax.random.normal(ks[3], (NUM_EXPERTS, d_in), dtype=jnp.float32) * 0.01
        A = jax.random.normal(ks[4], (NUM_EXPERTS, R, d_in), dtype=jnp.float32) * 0.02
        B = jax.random.normal(ks[5], (NUM_EXPERTS, d_out, R), dtype=jnp.float32) * 0.02
        return {'x': x, 'W_base': W_base, 'b_base': b_base, 'W_router': W_router, 'A': A, 'B': B}
    _L0_ffn_all = _L0_ffn_setup()
    _L0_ffn_in = {k: v for k, v in _L0_ffn_all.items() if k in ('W_base', 'b_base', 'W_router', 'A', 'B')}
    del _L0_ffn_all
    return {'x': x, 'ctx_4096': ctx_4096, 'L0_attn_attn_qkvw': _L0_attn_in['attn_qkvw'], 'L0_attn_attn_qkvb': _L0_attn_in['attn_qkvb'], 'L0_attn_attn_ow': _L0_attn_in['attn_ow'], 'L0_attn_attn_ob': _L0_attn_in['attn_ob'], 'L0_xattn_x1_scale': _L0_xattn_in['x1_scale'], 'L0_xattn_x1_zp': _L0_xattn_in['x1_zp'], 'L0_xattn_x2_scale': _L0_xattn_in['x2_scale'], 'L0_xattn_x2_zp': _L0_xattn_in['x2_zp'], 'L0_ffn_W_base': _L0_ffn_in['W_base'], 'L0_ffn_b_base': _L0_ffn_in['b_base'], 'L0_ffn_W_router': _L0_ffn_in['W_router'], 'L0_ffn_A': _L0_ffn_in['A'], 'L0_ffn_B': _L0_ffn_in['B']}

def reference(x, ctx_4096, L0_attn_attn_qkvw, L0_attn_attn_qkvb, L0_attn_attn_ow, L0_attn_attn_ob, L0_xattn_x1_scale, L0_xattn_x1_zp, L0_xattn_x2_scale, L0_xattn_x2_zp, L0_ffn_W_base, L0_ffn_b_base, L0_ffn_W_router, L0_ffn_A, L0_ffn_B):
    import jax
    import jax.numpy as jnp

    def _L0_attn_ref(x, attn_qkvw, attn_qkvb, attn_ow, attn_ob):
        import jax, jax.numpy as jnp
        import numpy as np
        HEADS = 32
        B, S, H = x.shape
        hd = H // HEADS
        scale = 1.0 / np.sqrt(hd)
        qkv = x @ attn_qkvw + attn_qkvb
        qkv = qkv.reshape(B, S, 3, HEADS, hd)
        q = jnp.transpose(qkv[:, :, 0], (0, 2, 1, 3))
        k = jnp.transpose(qkv[:, :, 1], (0, 2, 1, 3))
        v = jnp.transpose(qkv[:, :, 2], (0, 2, 1, 3))
        scores = jnp.einsum('bhqd,bhkd->bhqk', q, k) * scale
        probs = jax.nn.softmax(scores, axis=-1)
        ctx = jnp.einsum('bhqk,bhkd->bhqd', probs, v)
        ctx = jnp.transpose(ctx, (0, 2, 1, 3)).reshape(B, S, H)
        return ctx @ attn_ow + attn_ob

    def _L0_xattn_ref(x1, x2, x1_scale, x1_zp, x2_scale, x2_zp):
        import jax, jax.numpy as jnp
        import numpy as np
        QMIN = 0.0
        QMAX = 255.0

        def fake_quant(x, scale, zp):
            s = scale.reshape(())
            z = zp.reshape(())
            q = jnp.clip(jnp.round(x / s + z), QMIN, QMAX)
            return (q - z) * s
        q1 = fake_quant(x1, x1_scale, x1_zp)
        q2 = fake_quant(x2, x2_scale, x2_zp)
        return jnp.matmul(q1, q2)

    def _L0_ffn_ref(x, W_base, b_base, W_router, A, B):
        import jax, jax.numpy as jnp
        import numpy as np
        R = 16
        NUM_EXPERTS = 8
        TOP_K = 2
        LORA_ALPHA = 32
        SCALING = LORA_ALPHA / R
        orig_shape = x.shape
        d_in = x.shape[-1]
        x_flat = x.reshape(-1, d_in)
        logits = x_flat @ W_router.T
        probs = jax.nn.softmax(logits, axis=-1)
        topk_probs, topk_idx = jax.lax.top_k(probs, TOP_K)
        topk_probs = topk_probs / jnp.sum(topk_probs, axis=-1, keepdims=True)
        onehot = jax.nn.one_hot(topk_idx, NUM_EXPERTS, dtype=x.dtype)
        combine = jnp.einsum('nk,nke->ne', topk_probs, onehot)
        h = jnp.einsum('nd,erd->ner', x_flat, A)
        hw = h * combine[:, :, None]
        expert_out = jnp.einsum('ner,eor->no', hw, B) * SCALING
        base_out = x_flat @ W_base.T + b_base
        out = base_out + expert_out
        return out.reshape(*orig_shape[:-1], W_base.shape[0])
    x = _layernorm(x + _L0_attn_ref(x, L0_attn_attn_qkvw, L0_attn_attn_qkvb, L0_attn_attn_ow, L0_attn_attn_ob), axis=-1)
    x = _layernorm(x + _L0_xattn_ref(x, ctx_4096, L0_xattn_x1_scale, L0_xattn_x1_zp, L0_xattn_x2_scale, L0_xattn_x2_zp), axis=-1)
    x = _layernorm(x + _L0_ffn_ref(x, L0_ffn_W_base, L0_ffn_b_base, L0_ffn_W_router, L0_ffn_A, L0_ffn_B), axis=-1)
    return x

_drawn_inputs = setup_inputs


def setup_inputs(seed=0):
    import zlib

    import numpy as np

    out = dict(_drawn_inputs(seed))
    spreads = {}
    factors = {'L0_ffn_b_base': 3.319}
    for name, (base, spread) in spreads.items():
        noise = np.random.default_rng([zlib.crc32(name.encode()), seed]).standard_normal(out[name].shape)
        drawn = base * np.exp(spread * noise) if base else spread * noise
        out[name] = jnp.asarray(drawn.astype(out[name].dtype))
    for name, factor in factors.items():
        out[name] = (out[name] * factor).astype(out[name].dtype)
    return out
```

```python
import concourse.bass as bass
from concourse import mybir
from concourse.alu_op_type import AluOpType as ALU
from contextlib import ExitStack


def decoder_layer(nc, xT, x, wqkv, qkvb, ow, ob, ctx_in, scales, wbT, bb, art, bt, out):
    f32, f32r, bf16, u32 = mybir.dt.float32, mybir.dt.float32r, mybir.dt.bfloat16, mybir.dt.uint32
    ACT = mybir.ActivationFunctionType
    AX = mybir.AxisListType.X

    P = 128
    H = x.shape[1]
    TOK = x.shape[0]
    NB = ctx_in.shape[0]
    S = TOK // NB
    KT = H // P
    HD = 32
    HPG = P // HD
    G = H // P
    QT = S // P
    NS = HPG * QT
    UNITS = G * NB
    SM_SCALE = float(HD) ** -0.5
    NE = 8
    ER = art.shape[2] - NE
    R = ER // NE
    SCALING = 32.0 / R
    EPS = 1e-5
    QMAX = 255.0
    MAGIC = 1.5 * 2.0 ** 23
    PACK_HI2, PACK_LO, SHIFT = HD, 2 * HD, 3 * HD
    NT = TOK // P
    PACK_INC = 6 * 16

    es = ExitStack()
    with es:
        KB = 1024
        base = 16512

        def at(name, off, shape, dt):
            return nc.alloc_sbuf_tensor_at(name, shape, dt, offset=base + int(off * KB))

        big_hi = at("big_hi", 0, [P, KT, H], f32r)
        big_lo = at("big_lo", 32, [P, KT, H], f32r)
        w_hi = at("w_hi", 64, [P, 3, KT, P], f32r)
        w_lo = at("w_lo", 76, [P, 3, KT, P], f32r)
        w_raw = at("w_raw", 88, [P, 3, KT, P], f32)
        q_hi = at("q_hi", 100, [P, S], f32r)
        q_lo = at("q_lo", 102, [P, S], f32r)
        k_hi = at("k_hi", 104, [P, S], f32r)
        k_lo = at("k_lo", 106, [P, S], f32r)
        qp = at("qp", 108, [P, 2, HPG, S], f32r)
        kp = at("kp", 124, [P, 2, HPG, S], f32r)
        probs = at("probs", 140, [P, HPG, QT, S], f32)
        x_raw = at("x_raw", 140, [P, KT, TOK], f32)
        v_nat = at("v_nat", 172, [P, 2, QT, P], f32)
        vT = at("vT", 176, [P, S], f32)
        psumk = at("psumk", 178, [P, HPG, S], f32)
        recip = at("recip", 186, [P, S], f32)
        ctxs = at("ctxs", 188, [P, S], f32)
        ident = at("ident", 190, [P, P], f32)
        identb = at("identb", 190.5, [P, P], bf16)
        m_row = at("m_row", 190.75, [NS, 2, P], f32r)
        ones = at("ones", 191.75, [P, HD], f32)
        bias = at("bias", 191.875, [P, G, 3], f32)
        wst = at("wst", 192, [P, 2, H], f32)
        ob_sb = at("ob_sb", 200, [P, H], f32)
        c_q = at("c_q", 204, [P, H], bf16)
        m_col = at("m_col", 206, [P, NS], f32)
        sc = at("sc", 206.0625, [P, 12], f32)
        consts = at("consts", 206.125, [P, 4], f32)
        onesb = at("onesb", 206.15625, [P, P], bf16)
        iota = at("iota", 206.40625, [P, NE], f32)
        st = at("st", 206.4375, [P, 2, 2, 6], f32)
        mv = at("mv", 206.53125, [P, 2, 4], f32)
        kcol = at("kcol", 206.5625, [P, 2], f32)
        rt = at("rt", 206.59375, [P, 40], f32)
        ridx = at("ridx", 206.75, [P, NE], u32)
        c2 = at("c2", 64, [P, NB, KT, H], bf16)
        c1T = at("c1T", 96, [P, 2, KT, P], bf16)
        cx_hi = at("cx_hi", 108, [P, 2, KT, P], f32r)
        cx_lo = at("cx_lo", 116, [P, 2, KT, P], f32r)
        corr = at("corr", 124, [P, NB, H], f32)
        x1s = at("x1s", 140, [P, 2, H], f32)
        qtmp = at("qtmp", 148, [P, 2, H], f32)
        cx_raw = at("cx_raw", 172, [P, 2, KT, P], f32)
        xres = at("xres", 180, [P, 2, H], f32)
        c1 = at("c1", 188, [P, H], bf16)
        x2s = at("x2s", 156, [P, 2, H], f32)
        r3 = at("r3", 164, [P, 2, H], f32)
        art_sb = at("art_sb", 108, [P, KT, ER + NE], f32)
        bt_hi = at("bt_hi", 113, [P, H], f32r)
        bt_lo = at("bt_lo", 117, [P, H], f32r)
        x2T = at("x2T", 64, [P, KT, P], f32)
        x2T_hi = at("x2T_hi", 68, [P, 2, KT, P], f32r)
        x2T_lo = at("x2T_lo", 76, [P, 2, KT, P], f32r)
        hw = at("hw", 84, [P, ER], f32)
        hwT_hi = at("hwT_hi", 84.5, [P, P], f32r)
        hwT_lo = at("hwT_lo", 85, [P, P], f32r)
        xb = at("xb", 180, [P, 2, H], f32)
        bt_raw = at("bt_raw", 172, [P, H], f32)
        bb_sb = at("bb_sb", 176, [P, H], f32)

        banks = [es.enter_context(nc.psum_tensor(f"bank{i}", [P, 512], f32)) for i in range(8)]
        wide = None
        del wide
        PROJ0, PROJ1, MAX0, ST0, CTX, LSUM = 0, 1, 2, 4, 6, 7

        ctx_d = nc.dram_tensor("ctx_scratch", [H, TOK], f32).ap()
        c2_d = nc.dram_tensor("c2_scratch", [NB * KT, P, H], bf16).ap()
        x2_d = nc.dram_tensor("x2_scratch", [TOK, H], f32).ap()
        ctx_v = ctx_d.rearrange("(k p) t -> p k t", p=P)
        ctx_tiles = ctx_in.rearrange("b (k p) n -> (b k) p n", p=P)

        names = """x_hi_ok x_lo_ok const_in w_in w_hi_ok w_split proj_done hi_ok lo_ok vT_ok vt_mm v_ok
        max_mm rowmax m_mm m_hi_ok m_ok shift_in st_mm exp_ok pool_sum psum_ok pv_mm l_mm recip_ok ctx_ok
        ctx_out const_ok idb_ok ctxq_in ctxq_1 ctxq_2 ctxq_ok c2_out ow_hi ow_lo
        c2_in cs_mm corr_ok sc_ok
        cx_hi_ok cx_lo_ok xr_ok a_mm r1_ok st1 mv1 ve1 rstd1 nm1 x1_ok qp1 qp2 c1_ok tr_mm c1T_ok
        rs_mm b_mm k1 kc_ok x1c_ok t_ok r2_ok st2 mv2 ve2 rstd2 nm2 x2_ok
        bt_in bt_hi_ok bt_ok art_in wb_hi wb_lo xt_mm xt_ok xthi_ok xtlo_ok h_mm rv1 rv2 rv3 re_ok
        rw1 rw2 rw3 rw4 rw5 comb_ok hw_ok hwt_mm hwthi_ok hwtlo_ok c_mm xb_ok r3_ok st3 mv3 ve3 rstd3 nm3
        o_ok passed minus_ok""".split()
        sem = {n: es.enter_context(nc.semaphore(n)) for n in names}
        x_in = [es.enter_context(nc.semaphore(f"x_in{k}")) for k in range(KT)]
        by_parity = {n: [es.enter_context(nc.semaphore(f"{n}_{q}")) for q in range(2)]
                     for n in ("ow_in", "wb_in", "a_in", "xr_in", "x2_in", "x2_out", "o_out")}
        packed = [es.enter_context(nc.semaphore(f"packed{j}")) for j in range(HPG)]
        block = es.enter_context(nc.Block())

        def steps_of(eng, step):
            step(0, 0, 0)
            step(1, 1, 0)
            step(2, 0, 1)
            step(3, 1, 1)
            with eng.Fori(2, G - 1) as g:
                step(2 * g, 0, g)
                step(2 * g + 1, 1, g)
            for s in range(UNITS - 2, UNITS + 2):
                step(s, s % 2, s // 2)

        def stages(s):
            if not isinstance(s, int):
                return True, True, True
            return s < UNITS, 1 <= s <= UNITS, s >= 2

        def wait_alone(eng, semaphore, value):
            eng.wait_ge(semaphore, value)
            eng.sem_inc(sem["passed"], 1)

        def bank(i, lo=0, hi=512):
            return banks[i][:, lo:hi]

        @block.sync
        def _(sp):
            wq_v = wqkv.rearrange("g p a k c -> g p (a k c)")
            for k in range(KT):
                sp.dma_start(x_raw[:, k, :], xT[k * P:(k + 1) * P, :]).then_inc(x_in[k], 16)
                if k == 0:
                    sp.dma_start(w_raw[:].rearrange("p a k c -> p (a k c)"), wq_v[0]).then_inc(sem["w_in"], 16)
            sp.dma_start(bias[:, :, :], qkvb).then_inc(sem["const_in"], 16)
            for n in range(4):
                sp.dma_start(sc[:, n:n + 1], scales[n].rearrange("(a n) -> a n", a=1).to_broadcast([P, 1])).then_inc(sem["const_in"], 16)
            sp.dma_start(ob_sb[:, :], ob.rearrange("(a n) -> a n", a=1).to_broadcast([P, H])).then_inc(sem["const_in"], 16)

            def pack(s, par, j, which):
                rows = slice(j * HD, (j + 1) * HD)
                if which == "q":
                    parts = ((qp, 0, q_hi), (qp, PACK_HI2, q_lo), (qp, PACK_LO, q_hi))
                else:
                    parts = ((kp, 0, k_hi), (kp, PACK_HI2, k_hi), (kp, PACK_LO, k_lo))
                if not isinstance(s, int) or s >= 2:
                    sp.wait_ge(sem["st_mm"], NS * (s - 2) + QT * (j + 1))
                for dst, row, src in parts:
                    sp.dma_start(dst[row:row + HD, par, j, :].bitcast(f32), src[rows, :].bitcast(f32)).then_inc(packed[j], 16)

            def step(s, par, g):
                proj, maxima, finish = stages(s)
                if proj and par == 0 and (not isinstance(s, int) or s < UNITS - 2):
                    wait_alone(sp, sem["w_split"], 3 * (g + 1))
                    sp.dma_start(w_raw[:].rearrange("p a k c -> p (a k c)"), wq_v[bass.ds(g + 1, 1)].rearrange("a p n -> (a p) n")).then_inc(sem["w_in"], 16)
                if proj:
                    if not isinstance(s, int) or s >= 1:
                        wait_alone(sp, sem["ctxq_ok"], s)
                    sp.dma_start(wst[:, 0, :], ctx_tiles[bass.ds(s, 1)].rearrange("a p n -> (a p) n")).then_inc(sem["ctxq_in"], 16)
                    sp.wait_ge(sem["lo_ok"], 2 * s + 1)
                    pack(s, par, 0, "q")
                    pack(s, par, 1, "q")
                    wait_alone(sp, sem["ctxq_ok"], s + 1)
                    sp.dma_start(c2_d[bass.ds(s, 1)].rearrange("a p n -> (a p) n"), c_q[:, :]).then_inc(sem["c2_out"], 16)
                    sp.wait_ge(sem["lo_ok"], 2 * s + 2)
                    pack(s, par, 0, "k")
                    pack(s, par, 1, "k")
                    pack(s, par, 2, "q")
                    pack(s, par, 2, "k")
                if maxima:
                    sp.wait_ge(sem["m_ok"], s)
                    for half in range(2):
                        sp.dma_start(qp[SHIFT + half:SHIFT + half + 1, 1 - par, :, :].rearrange("a j (t q) -> a (j t) q", q=P).bitcast(f32),
                                     m_row[:, half, :].bitcast(f32)).then_inc(sem["shift_in"], 16)
                if proj:
                    pack(s, par, 3, "q")
                    pack(s, par, 3, "k")
                if finish:
                    wait_alone(sp, sem["ctx_ok"], s - 1)
                    cg = (g - 1) * P
                    sp.dma_start(ctx_d[bass.ds(cg, P), par * S:(par + 1) * S], ctxs[:, :]).then_inc(sem["ctx_out"], 16)

            def weight_load(src, n_in, n_used, first_free, k):
                if k < 2:
                    sp.wait_ge(*first_free)
                else:
                    sp.wait_ge(n_used, k - 1)
                sp.dma_start(wst[:, k % 2, :], src[k * P:(k + 1) * P, :]).then_inc(n_in[k % 2], 16)

            step(0, 0, 0)
            step(1, 1, 0)
            step(2, 0, 1)
            step(3, 1, 1)
            with sp.Fori(2, G - 1) as g:
                step(2 * g, 0, g)
                step(2 * g + 1, 1, g)
            step(UNITS - 2, 0, G - 1)
            step(UNITS - 1, 1, G - 1)
            for k in range(KT):
                weight_load(ow, by_parity["ow_in"], sem["ow_lo"], (sem["ctxq_ok"], UNITS), k)
                if k == 1:
                    sp.wait_ge(sem["proj_done"], 3 * UNITS)
                    sp.wait_ge(sem["c2_out"], 16 * UNITS)
                    for b in range(NB):
                        sp.dma_start(c2[:, b], c2_d[b * KT:(b + 1) * KT].rearrange("k p n -> p k n")).then_inc(sem["c2_in"], 16)
            step(UNITS, 0, G)
            step(UNITS + 1, 1, G)

            sp.wait_ge(sem["ctx_out"], 16 * UNITS)

            def load_tile(n, par, i):
                tok = par * S + i * P
                if not isinstance(n, int) or n >= 2:
                    sp.wait_ge(sem["cx_lo_ok"], n - 1)
                    wait_alone(sp, sem["r1_ok"], n - 1)
                sp.dma_start(cx_raw[:, par], ctx_v[:, :, bass.ds(tok, P)]).then_inc(by_parity["a_in"][par], 16)
                sp.dma_start(xres[:, par, :], x[bass.ds(tok, P), :]).then_inc(by_parity["xr_in"][par], 16)

            def store_x2(m, par, i):
                wait_alone(sp, sem["x2_ok"], m + 1)
                sp.dma_start(x2_d[bass.ds(par * S + i * P, P), :], x1s[:, par, :]).then_inc(by_parity["x2_out"][par], 16)

            load_tile(0, 0, 0)
            load_tile(1, 1, 0)
            with sp.Fori(1, NT // 2) as i:
                load_tile(2 * i, 0, i)
                store_x2(2 * i - 2, 0, i - 1)
                load_tile(2 * i + 1, 1, i)
                store_x2(2 * i - 1, 1, i - 1)
            sp.wait_ge(sem["cx_lo_ok"], NT)
            sp.wait_ge(sem["r1_ok"], NT)
            sp.dma_start(bt_raw[:, :], bt).then_inc(sem["bt_in"], 16)
            sp.dma_start(bb_sb[:, :], bb.rearrange("(a n) -> a n", a=1).to_broadcast([P, H])).then_inc(sem["bt_in"], 16)
            for k in range(KT):
                weight_load(wbT, by_parity["wb_in"], sem["wb_lo"], (sem["ow_lo"], KT), k)
                if k == 1:
                    sp.wait_ge(sem["a_mm"], NT)
                    sp.dma_start(art_sb[:, :, :], art).then_inc(sem["art_in"], 16)
            store_x2(NT - 2, 0, NT // 2 - 1)
            store_x2(NT - 1, 1, NT // 2 - 1)

            for q in range(2):
                sp.wait_ge(by_parity["x2_out"][q], 16 * NT // 2)

            def load_x2(n, par, i):
                if not isinstance(n, int) or n >= 2:
                    sp.wait_ge(sem["xb_ok"], n - 1)
                    wait_alone(sp, sem["xt_mm"], n - 1)
                sp.dma_start(x2s[:, par, :], x2_d[bass.ds(par * S + i * P, P), :]).then_inc(by_parity["x2_in"][par], 16)

            def store(n, par, i):
                wait_alone(sp, sem["o_ok"], n + 1)
                sp.dma_start(out[bass.ds(par * S + i * P, P), :], r3[:, par, :]).then_inc(by_parity["o_out"][par], 16)

            load_x2(0, 0, 0)
            load_x2(1, 1, 0)
            with sp.Fori(1, NT // 2) as i:
                load_x2(2 * i, 0, i)
                store(2 * i - 2, 0, i - 1)
                load_x2(2 * i + 1, 1, i)
                store(2 * i - 1, 1, i - 1)
            store(NT - 2, 0, NT // 2 - 1)
            store(NT - 1, 1, NT // 2 - 1)
            for q in range(2):
                sp.wait_ge(by_parity["o_out"][q], 16 * NT // 2)

        @block.tensor
        def _(pe):
            def split_mm(dst, lhs, rhs, k, last_k, first=None):
                for n, (a, b) in enumerate(((0, 0), (0, 1), (1, 0))):
                    mm = nc.tensor.matmul(dst, lhs[a], rhs[b], start=(k == 0 and n == 0) if first is None else False,
                                          stop=(k == last_k and n == 2))
                return mm

            def step(s, par, g):
                proj, maxima, finish = stages(s)
                first = isinstance(s, int) and s == 0
                cols = slice(par * S, (par + 1) * S)

                def transpose_v():
                    pe.wait_ge(sem["vT_ok"], s)
                    pe.wait_ge(sem["lo_ok"], 2 * s)
                    if isinstance(s, int) and s == 1:
                        pe.wait_ge(sem["const_ok"], 1)
                    for t in range(QT):
                        mm = nc.tensor.transpose(bank(PROJ0, t * P, (t + 1) * P), vT[:, t * P:(t + 1) * P], ident[:, :])
                    mm.then_inc(sem["vt_mm"], 1)

                def project(n):
                    piece, k = n // KT, n % KT
                    dst = bank(PROJ1 if piece != 1 else PROJ0)
                    if k == 0:
                        pe.wait_ge(sem["w_split"], 3 * g + piece + 1)
                        if piece == 0 and not first:
                            pe.wait_ge(sem["vT_ok"], s)
                        if piece == 1 and not first:
                            pe.wait_ge(sem["v_ok"], s)
                        if piece == 2:
                            pe.wait_ge(sem["lo_ok"], 2 * s + 1)
                    if first and piece == 0:
                        pe.wait_ge(sem["x_lo_ok"], k + 1)
                    mm = split_mm(dst, (w_hi[:, piece, k, :], w_lo[:, piece, k, :]),
                                  (big_hi[:, k, cols], big_lo[:, k, cols]), k, KT - 1)
                    if k == KT - 1:
                        mm.then_inc(sem["proj_done"], 1)

                def score(n):
                    j, t = n // QT, n % QT
                    if t == 0:
                        pe.wait_ge(packed[j], PACK_INC * s)
                    if n >= 2:
                        pe.wait_ge(sem["rowmax"], NS * (s - 1) + n - 1)
                    nc.tensor.matmul(bank(MAX0 + n % 2), qp[0:SHIFT, 1 - par, j, t * P:(t + 1) * P],
                                     kp[0:SHIFT, 1 - par, j, :], start=True, stop=True).then_inc(sem["max_mm"], 1)

                def maxima_to_rows():
                    pe.wait_ge(sem["rowmax"], NS * s)
                    if not isinstance(s, int) or s >= 3:
                        pe.wait_ge(sem["recip_ok"], s - 2)
                    nc.tensor.transpose(banks[LSUM][0:NS, 0:P], m_col[:, :], ident[:, :]).then_inc(sem["m_mm"], 1)

                def score_t(n):
                    j, t = n // QT, n % QT
                    if n == 0:
                        pe.wait_ge(sem["shift_in"], 32 * (s - 1))
                        if isinstance(s, int) and s == 2:
                            pe.wait_ge(sem["minus_ok"], 1)
                    if n >= 2:
                        pe.wait_ge(sem["exp_ok"], NS * (s - 2) + n - 1)
                    nc.tensor.matmul(bank(ST0 + n % 2), kp[0:SHIFT + 2, par, j, t * P:(t + 1) * P],
                                     qp[0:SHIFT + 2, par, j, :], start=True, stop=True).then_inc(sem["st_mm"], 1)

                if maxima:
                    transpose_v()
                for i in range(NS):
                    if proj:
                        for n in range(3 * KT * i // NS, 3 * KT * (i + 1) // NS):
                            project(n)
                    if maxima:
                        for n in range(min(NS, 4 * i // 3), min(NS, 4 * (i + 1) // 3)):
                            score(n)
                        if i == NS - 2:
                            maxima_to_rows()
                    if finish:
                        score_t(i)
                if finish:
                    pe.wait_ge(sem["exp_ok"], NS * (s - 1))
                    pe.wait_ge(sem["v_ok"], s - 1)
                    if not isinstance(s, int) or s >= 3:
                        pe.wait_ge(sem["ctx_ok"], s - 2)
                    for t in range(QT):
                        for j in range(HPG):
                            mm = nc.tensor.matmul(banks[CTX][j * HD:(j + 1) * HD, :], v_nat[:, par, t, j * HD:(j + 1) * HD],
                                                  probs[:, j, t, :], start=(t == 0), stop=(t == QT - 1), skip_group_check=True)
                    mm.then_inc(sem["pv_mm"], 1)
                    pe.wait_ge(sem["psum_ok"], HPG * (s - 1))
                    if maxima:
                        pe.wait_ge(sem["m_ok"], s)
                    for j in range(HPG):
                        mm = nc.tensor.matmul(banks[LSUM][j * HD:(j + 1) * HD, :], ones[:, :], psumk[:, j, :],
                                              start=True, stop=True, skip_group_check=True)
                    mm.then_inc(sem["l_mm"], 1)

            steps_of(pe, step)

            pe.wait_ge(sem["c2_in"], 16 * NB)
            pe.wait_ge(sem["recip_ok"], UNITS)
            pe.wait_ge(sem["ctx_ok"], UNITS)
            for b in range(NB):
                if b:
                    pe.wait_ge(sem["corr_ok"], 1)
                for h in range(2):
                    for k in range(KT):
                        mm = nc.tensor.matmul(bank(6 + h), onesb[:, :], c2[:, b, k, h * 512:(h + 1) * 512],
                                              start=(k == 0), stop=(k == KT - 1))
                mm.then_inc(sem["cs_mm"], 1)

            def out_project(n, par, h):
                if h == 0:
                    pe.wait_ge(sem["cx_lo_ok"], n + 1)
                    if not isinstance(n, int) or n >= 1:
                        pe.wait_ge(sem["r1_ok"], n)
                    else:
                        pe.wait_ge(sem["exp_ok"], NS * UNITS)
                for k in range(KT):
                    if isinstance(n, int) and n == 0 and h == 0:
                        pe.wait_ge(sem["ow_lo"], k + 1)
                    mm = split_mm(bank(h), (cx_hi[:, par, k, :], cx_lo[:, par, k, :]),
                                  (big_hi[:, k, h * 512:(h + 1) * 512], big_lo[:, k, h * 512:(h + 1) * 512]), k, KT - 1)
                if h:
                    mm.then_inc(sem["a_mm"], 1)

            def transpose_c1(m):
                pe.wait_ge(sem["c1_ok"], m + 1)
                if not isinstance(m, int) or m >= 1:
                    pe.wait_ge(sem["c1T_ok"], m)
                c1p = banks[4][:, :].bitcast(bf16)
                for k in range(KT):
                    mm = nc.tensor.transpose(c1p[:, k * P:(k + 1) * P], c1[:, k * P:(k + 1) * P], identb[:, :])
                mm.then_inc(sem["tr_mm"], 1)

            def context_product(m, par):
                pe.wait_ge(sem["c1T_ok"], m + 1)
                if not isinstance(m, int) or m >= 1:
                    pe.wait_ge(sem["k1"], m)
                    pe.wait_ge(sem["t_ok"], m)
                for k in range(KT):
                    mm = nc.tensor.matmul(banks[5][:, 0:2], c1T[:, par, k, :], onesb[:, 0:2], start=(k == 0), stop=(k == KT - 1))
                mm.then_inc(sem["rs_mm"], 1)
                for h in range(2):
                    for k in range(KT):
                        mm = nc.tensor.matmul(bank(2 + h), c1T[:, par, k, :], c2[:, par, k, h * 512:(h + 1) * 512],
                                              start=(k == 0), stop=(k == KT - 1))
                mm.then_inc(sem["b_mm"], 1)

            def tail_step(n, par):
                more = not isinstance(n, int) or n < NT
                if more:
                    out_project(n, par, 0)
                if not isinstance(n, int) or n >= 1:
                    transpose_c1(n - 1)
                if more:
                    out_project(n, par, 1)
                if not isinstance(n, int) or n >= 1:
                    context_product(n - 1, 1 - par)

            tail_step(0, 0)
            tail_step(1, 1)
            with pe.Fori(1, NT // 2) as i:
                tail_step(2 * i, 0)
                tail_step(2 * i + 1, 1)
            tail_step(NT, 0)

            def transpose_x2(n, par, i):
                pe.wait_ge(by_parity["x2_in"][par], 16 * (i + 1))
                if not isinstance(n, int) or n >= 1:
                    pe.wait_ge(sem["xt_ok"], n)
                for k in range(KT):
                    mm = nc.tensor.transpose(bank(6 + k // 4, (k % 4) * P, (k % 4 + 1) * P), x2s[:, par, k * P:(k + 1) * P], ident[:, :])
                mm.then_inc(sem["xt_mm"], 1)

            def hidden(n):
                pe.wait_ge(sem["xt_ok"], n + 1)
                if isinstance(n, int) and n == 0:
                    pe.wait_ge(sem["art_in"], 16)
                else:
                    pe.wait_ge(sem["hw_ok"], n)
                for k in range(KT):
                    mm = nc.tensor.matmul(banks[4][:, 0:ER + NE], x2T[:, k, :], art_sb[:, k, :], start=(k == 0), stop=(k == KT - 1))
                mm.then_inc(sem["h_mm"], 1)

            def base(n, par, h):
                if h == 0:
                    pe.wait_ge(sem["xtlo_ok"], n + 1)
                    if not isinstance(n, int) or n >= 2:
                        pe.wait_ge(sem["r3_ok"], n - 1)
                for k in range(KT):
                    if isinstance(n, int) and n == 0 and h == 0:
                        pe.wait_ge(sem["wb_lo"], k + 1)
                    split_mm(bank(2 * par + h), (x2T_hi[:, par, k, :], x2T_lo[:, par, k, :]),
                             (big_hi[:, k, h * 512:(h + 1) * 512], big_lo[:, k, h * 512:(h + 1) * 512]), k, -1)

            def transpose_hw(n):
                pe.wait_ge(sem["hw_ok"], n + 1)
                if not isinstance(n, int) or n >= 1:
                    pe.wait_ge(sem["hwtlo_ok"], n)
                nc.tensor.transpose(banks[5][:, 0:P], hw[:, :], ident[:, :]).then_inc(sem["hwt_mm"], 1)

            def experts(n, par):
                pe.wait_ge(sem["hwtlo_ok"], n + 1)
                if isinstance(n, int) and n == 0:
                    pe.wait_ge(sem["bt_ok"], 1)
                for h in range(2):
                    cols = slice(h * 512, (h + 1) * 512)
                    mm = split_mm(bank(2 * par + h), (hwT_hi[:, :], hwT_lo[:, :]), (bt_hi[:, cols], bt_lo[:, cols]), 0, 0, first=False)
                mm.then_inc(sem["c_mm"], 1)

            def last_step(n, par, i, more):
                hidden(n)
                base(n, par, 0)
                if more:
                    transpose_x2(n + 1, 1 - par, i + par)
                transpose_hw(n)
                base(n, par, 1)
                experts(n, par)

            pe.wait_ge(sem["t_ok"], NT)
            pe.wait_ge(sem["kc_ok"], NT)
            transpose_x2(0, 0, 0)
            last_step(0, 0, 0, True)
            last_step(1, 1, 0, True)
            with pe.Fori(1, NT // 2 - 1) as i:
                last_step(2 * i, 0, i, True)
                last_step(2 * i + 1, 1, i, True)
            last_step(NT - 2, 0, NT // 2 - 1, True)
            last_step(NT - 1, 1, NT // 2 - 1, False)

        @block.scalar
        def _(act):
            for k in range(KT):
                act.wait_ge(x_in[k], 16)
                nc.scalar.activation(big_hi[:, k, :], x_raw[:, k, :], ACT.Identity).then_inc(sem["x_hi_ok"], 1)
            act.wait_ge(sem["const_in"], 16 * 6)

            def step(s, par, g):
                proj, maxima, finish = stages(s)
                prev = not isinstance(s, int) or s >= 1
                for i in range(NS):
                    j, t = i // QT, i % QT
                    if finish:
                        act.wait_ge(sem["st_mm"], NS * (s - 2) + i + 1)
                        if i == 0 and (not isinstance(s, int) or s >= 3):
                            act.wait_ge(sem["pv_mm"], s - 2)
                            act.wait_ge(sem["psum_ok"], HPG * (s - 2))
                        if i == 0 and isinstance(s, int) and s == 2:
                            act.wait_ge(sem["x_lo_ok"], KT)
                        nc.scalar.activation(probs[:, j, t, :], bank(ST0 + i % 2), ACT.Exp, scale=SM_SCALE).then_inc(sem["exp_ok"], 1)
                    if proj and i in (5, 10):
                        piece = 0 if i == 5 else 1
                        wait_alone(act, sem["proj_done"], 3 * s + piece + 1)
                        if prev:
                            for h in range(HPG):
                                wait_alone(act, packed[h], PACK_INC * s)
                        nc.scalar.activation((q_hi, k_hi)[piece][:, :], bank(PROJ1 if piece == 0 else PROJ0), ACT.Identity,
                                             bias=bias[:, bass.ds(g, 1), piece:piece + 1].rearrange("p a b -> p (a b)")).then_inc(sem["hi_ok"], 1)
                if proj:
                    act.wait_ge(sem["proj_done"], 3 * s + 3)
                    if prev:
                        wait_alone(act, sem["vt_mm"], s)
                    nc.scalar.activation(vT[:, :], bank(PROJ1), ACT.Identity,
                                         bias=bias[:, bass.ds(g, 1), 2:3].rearrange("p a b -> p (a b)")).then_inc(sem["vT_ok"], 1)

            step(0, 0, 0)
            step(1, 1, 0)
            step(2, 0, 1)
            step(3, 1, 1)
            with act.Fori(2, G - 1) as g:
                step(2 * g, 0, g)
                step(2 * g + 1, 1, g)
            step(UNITS - 2, 0, G - 1)
            step(UNITS - 1, 1, G - 1)
            for k in range(KT):
                act.wait_ge(by_parity["ow_in"][k % 2], 16 * (k // 2 + 1))
                nc.scalar.activation(big_hi[:, k, :], wst[:, k % 2, :], ACT.Identity).then_inc(sem["ow_hi"], 1)
            step(UNITS, 0, G)
            step(UNITS + 1, 1, G)

            def split_cx(n, par, i):
                act.wait_ge(by_parity["a_in"][par], 16 * (i + 1))
                if not isinstance(n, int) or n >= 2:
                    act.wait_ge(sem["a_mm"], n - 1)
                nc.scalar.activation(cx_hi[:, par].rearrange("p k c -> p (k c)"), cx_raw[:, par].rearrange("p k c -> p (k c)"), ACT.Identity).then_inc(sem["cx_hi_ok"], 1)

            def tail_step(n, par, i):
                more = not isinstance(n, int) or n < NT
                prev = not isinstance(n, int) or n >= 1
                if prev:
                    q = 1 - par
                    act.wait_ge(sem["tr_mm"], n)
                    nc.scalar.activation(c1T[:, q].rearrange("p k c -> p (k c)"), banks[4][:, :].bitcast(bf16), ACT.Copy).then_inc(sem["c1T_ok"], 1)
                if not isinstance(n, int) or n < NT - 1:
                    split_cx(n + 1, 1 - par, i + par)
                if prev:
                    act.wait_ge(sem["b_mm"], n)
                    act.wait_ge(sem["kc_ok"], n)
                    for h in range(2):
                        mm = nc.scalar.activation(qtmp[:, q, h * 512:(h + 1) * 512], bank(2 + h), ACT.Identity,
                                                  scale=sc[:, 5:6], bias=kcol[:, 1:2])
                    mm.then_inc(sem["t_ok"], 1)
                if more:
                    act.wait_ge(sem["nm1"], n + 1)
                    nc.scalar.activation(x1s[:, par, :], x1s[:, par, :], ACT.Identity, scale=mv[:, 0, 2:3], bias=mv[:, 0, 3:4]).then_inc(sem["x1_ok"], 1)
                    act.wait_ge(sem["x1_ok"], n + 1)
                    nc.scalar.activation(qtmp[:, par, :], x1s[:, par, :], ACT.Identity, scale=sc[:, 4:5], bias=sc[:, 1:2]).then_inc(sem["qp1"], 1)
                if prev:
                    act.wait_ge(sem["nm2"], n)
                    nc.scalar.activation(x1s[:, q, :], x1s[:, q, :], ACT.Identity, scale=mv[:, 1, 2:3], bias=mv[:, 1, 3:4]).then_inc(sem["x2_ok"], 1)

            split_cx(0, 0, 0)
            tail_step(0, 0, 0)
            tail_step(1, 1, 0)
            with act.Fori(1, NT // 2 - 1) as i:
                tail_step(2 * i, 0, i)
                tail_step(2 * i + 1, 1, i)
            tail_step(NT - 2, 0, NT // 2 - 1)
            tail_step(NT - 1, 1, NT // 2 - 1)
            act.wait_ge(sem["a_mm"], NT)
            for k in range(KT):
                act.wait_ge(by_parity["wb_in"][k % 2], 16 * (k // 2 + 1))
                nc.scalar.activation(big_hi[:, k, :], wst[:, k % 2, :], ACT.Identity).then_inc(sem["wb_hi"], 1)
            tail_step(NT, 0, NT // 2)

            def copy_x2T(n, par):
                act.wait_ge(sem["xt_mm"], n + 1)
                if not isinstance(n, int) or n >= 1:
                    act.wait_ge(sem["h_mm"], n)
                    act.wait_ge(sem["xtlo_ok"], n)
                for h in range(2):
                    mm = nc.scalar.activation(x2T[:, 4 * h:4 * h + 4, :].rearrange("p k c -> p (k c)"), bank(6 + h), ACT.Copy)
                mm.then_inc(sem["xt_ok"], 1)

            def last_step(n, par, more):
                act.wait_ge(sem["rv3"], n + 1)
                nc.scalar.activation(rt[:, 8:16], rt[:, 0:8], ACT.Exp, bias=rt[:, 16:17]).then_inc(sem["re_ok"], 1)
                if more:
                    copy_x2T(n + 1, 1 - par)
                act.wait_ge(sem["nm3"], n + 1)
                nc.scalar.activation(r3[:, par, :], r3[:, par, :], ACT.Identity, scale=mv[:, 0, 2:3], bias=mv[:, 0, 3:4]).then_inc(sem["o_ok"], 1)

            act.wait_ge(sem["c2_in"], 16 * NB)
            copy_x2T(0, 0)
            with act.Fori(0, NT // 2 - 1) as i:
                last_step(2 * i, 0, True)
                last_step(2 * i + 1, 1, True)
            last_step(NT - 2, 0, True)
            last_step(NT - 1, 1, False)

        @block.gpsimd
        def _(pool):
            def split_w(g_next, piece, done):
                pool.wait_ge(sem["w_in"], 16 * (g_next + 1))
                if done is not None:
                    wait_alone(pool, sem["proj_done"], done)
                nc.gpsimd.tensor_scalar(w_hi[:, piece], w_raw[:, piece], 1.0, 0.0, ALU.mult, ALU.add).then_inc(sem["w_hi_ok"], 1)
                pool.wait_ge(sem["w_hi_ok"], 3 * g_next + piece + 1)
                nc.gpsimd.tensor_tensor(w_lo[:, piece], w_raw[:, piece], w_hi[:, piece].bitcast(f32), ALU.subtract).then_inc(sem["w_split"], 1)

            split_w(0, 0, None)
            nc.gpsimd.memset(ident[:, :], 0.0).then_inc(sem["idb_ok"], 1)
            nc.gpsimd.memset(ones[:, :], 1.0).then_inc(sem["idb_ok"], 1)
            nc.gpsimd.memset(onesb[:, :], 1.0).then_inc(sem["idb_ok"], 1)
            nc.gpsimd.memset(consts[:, 0:1], -0.5).then_inc(sem["idb_ok"], 1)
            nc.gpsimd.iota(iota[:, :], [[1, NE]], channel_multiplier=0, allow_small_or_imprecise_dtypes=True).then_inc(sem["idb_ok"], 1)
            pool.wait_ge(sem["idb_ok"], 5)
            nc.gpsimd.affine_select(out=ident[:, :], in_=ident[:, :], compare_op=ALU.not_equal, fill=1.0,
                                    base=0, pattern=[[-1, P]], channel_multiplier=1).then_inc(sem["idb_ok"], 1)
            pool.wait_ge(sem["idb_ok"], 6)
            nc.gpsimd.tensor_copy(identb[:, :], ident[:, :]).then_inc(sem["const_ok"], 1)
            split_w(0, 1, None)
            split_w(0, 2, None)

            def add_keys(s, j):
                u = s - 2
                pool.wait_ge(sem["exp_ok"], NS * u + QT * (j + 1))
                if j == 0 and (not isinstance(s, int) or s >= 3):
                    pool.wait_ge(sem["l_mm"], s - 2)
                nc.gpsimd.tensor_tensor(psumk[:, j, :], probs[:, j, 0, :], probs[:, j, 1, :], ALU.add).then_inc(sem["pool_sum"], 1)
                pool.wait_ge(sem["pool_sum"], 2 * HPG * u + 2 * j + 1)
                nc.gpsimd.tensor_tensor(psumk[:, j, :], psumk[:, j, :], probs[:, j, 2, :], ALU.add).then_inc(sem["pool_sum"], 1)
                pool.wait_ge(sem["pool_sum"], 2 * HPG * u + 2 * j + 2)
                nc.gpsimd.tensor_tensor(psumk[:, j, :], psumk[:, j, :], probs[:, j, 3, :], ALU.add).then_inc(sem["psum_ok"], 1)

            def step(s, par, g):
                proj, maxima, finish = stages(s)
                split = proj and par == 1 and (not isinstance(s, int) or s < UNITS - 1)
                if proj:
                    wait_alone(pool, sem["ctxq_in"], 16 * (s + 1))
                    if isinstance(s, int) and s == 0:
                        pool.wait_ge(sem["sc_ok"], 3)
                    nc.gpsimd.tensor_scalar(wst[:, 0, :], wst[:, 0, :], sc[:, 6:7], sc[:, 3:4], ALU.mult, ALU.add).then_inc(sem["ctxq_1"], 1)
                if finish:
                    add_keys(s, 0)
                if split:
                    split_w(g + 1, 0, 3 * s + 1)
                if finish:
                    add_keys(s, 1)
                    add_keys(s, 2)
                if split:
                    split_w(g + 1, 1, 3 * s + 2)
                if finish:
                    add_keys(s, 3)
                if split:
                    split_w(g + 1, 2, 3 * s + 3)

            steps_of(pool, step)

            def residual(par, i):
                pool.wait_ge(by_parity["xr_in"][par], 16 * (i + 1))
                nc.gpsimd.tensor_tensor(xres[:, par, :], xres[:, par, :], ob_sb[:, :], ALU.add).then_inc(sem["xr_ok"], 1)

            def rstd(ve, ok, n, row):
                pool.wait_ge(sem[ve], n)
                nc.gpsimd.tensor_tensor(mv[:, row, 2:3], mv[:, row, 1:2], consts[:, 0:1], ALU.pow).then_inc(sem[ok], 1)

            def tail_step(n, par, i):
                more = not isinstance(n, int) or n < NT
                prev = not isinstance(n, int) or n >= 1
                if more:
                    residual(par, i)
                if prev:
                    q = 1 - par
                    if isinstance(n, int) and n == 1:
                        pool.wait_ge(sem["corr_ok"], NB)
                    pool.wait_ge(sem["qp1"], n)
                    nc.gpsimd.tensor_tensor(x1s[:, q, :], x1s[:, q, :], corr[:, q, :], ALU.add).then_inc(sem["x1c_ok"], 1)
                if more:
                    rstd("ve1", "rstd1", n + 1, 0)
                if prev:
                    rstd("ve2", "rstd2", n, 1)

            tail_step(0, 0, 0)
            tail_step(1, 1, 0)
            with pool.Fori(1, NT // 2) as i:
                tail_step(2 * i, 0, i)
                tail_step(2 * i + 1, 1, i)
            tail_step(NT, 0, NT // 2)

            def last_step(n, par, i):
                pool.wait_ge(by_parity["x2_in"][par], 16 * (i + 1))
                if not isinstance(n, int) or n >= 2:
                    pool.wait_ge(sem["r3_ok"], n - 1)
                nc.gpsimd.tensor_tensor(xb[:, par, :], x2s[:, par, :], bb_sb[:, :], ALU.add).then_inc(sem["xb_ok"], 1)
                rstd("ve3", "rstd3", n + 1, 0)

            pool.wait_ge(sem["bt_in"], 32)
            last_step(0, 0, 0)
            last_step(1, 1, 0)
            with pool.Fori(1, NT // 2) as i:
                last_step(2 * i, 0, i)
                last_step(2 * i + 1, 1, i)

        @block.vector
        def _(dve):
            nc.vector.memset(kp[SHIFT:SHIFT + 2, :, :, :].bitcast(f32), -1.0).then_inc(sem["minus_ok"], 1)
            dve.wait_ge(sem["const_in"], 16 * 6)
            nc.vector.reciprocal(sc[:, 4:5], sc[:, 0:1])
            nc.vector.reciprocal(sc[:, 6:7], sc[:, 2:3])
            nc.vector.tensor_scalar(sc[:, 5:6], sc[:, 0:1], sc[:, 2:3], None, ALU.mult)
            nc.vector.tensor_scalar(sc[:, 7:8], sc[:, 1:2], 0.0, QMAX, ALU.max, ALU.min)
            nc.vector.tensor_scalar(sc[:, 8:9], sc[:, 3:4], 0.0, QMAX, ALU.max, ALU.min).then_inc(sem["sc_ok"], 1)
            dve.wait_ge(sem["sc_ok"], 1)
            nc.vector.tensor_scalar(sc[:, 7:9], sc[:, 7:9], MAGIC, -MAGIC, ALU.add, ALU.add).then_inc(sem["sc_ok"], 1)
            dve.wait_ge(sem["sc_ok"], 2)
            nc.vector.tensor_tensor(sc[:, 9:10], sc[:, 7:8], sc[:, 1:2], ALU.subtract)
            nc.vector.tensor_tensor(sc[:, 10:11], sc[:, 8:9], sc[:, 3:4], ALU.subtract).then_inc(sem["sc_ok"], 1)
            dve.wait_ge(sem["sc_ok"], 3)
            for n in range(2):
                last = nc.vector.tensor_scalar(consts[:, 1 + n:2 + n], sc[:, 7 + n:8 + n], MAGIC, None, ALU.add)
            last.then_inc(sem["sc_ok"], 1)
            for k in range(KT):
                dve.wait_ge(sem["x_hi_ok"], k + 1)
                nc.vector.tensor_tensor(big_lo[:, k, :], x_raw[:, k, :], big_hi[:, k, :].bitcast(f32), ALU.subtract).then_inc(sem["x_lo_ok"], 1)
            dve.wait_ge(sem["sc_ok"], 4)

            def step(s, par, g):
                proj, maxima, finish = stages(s)

                def low(piece):
                    dve.wait_ge(sem["hi_ok"], 2 * s + piece + 1)
                    hi, lo = ((q_hi, q_lo), (k_hi, k_lo))[piece]
                    nc.vector.scalar_tensor_tensor(lo[:, :], bank(PROJ1 if piece == 0 else PROJ0),
                                                   bias[:, bass.ds(g, 1), piece:piece + 1].rearrange("p a b -> p (a b)"),
                                                   hi[:, :].bitcast(f32), ALU.add, ALU.subtract).then_inc(sem["lo_ok"], 1)

                def quantise_context():
                    dve.wait_ge(sem["ctxq_1"], s + 1)
                    if not isinstance(s, int) or s >= 1:
                        dve.wait_ge(sem["c2_out"], 16 * s)
                    nc.vector.tensor_scalar(wst[:, 0, :], wst[:, 0, :], 0.0, QMAX, ALU.max, ALU.min).then_inc(sem["ctxq_2"], 1)
                    dve.wait_ge(sem["ctxq_2"], s + 1)
                    nc.vector.tensor_scalar(c_q[:, :], wst[:, 0, :], MAGIC, consts[:, 2:3], ALU.add, ALU.subtract).then_inc(sem["ctxq_ok"], 1)

                if maxima:
                    dve.wait_ge(sem["vt_mm"], s)
                    if not isinstance(s, int) or s >= 3:
                        dve.wait_ge(sem["pv_mm"], s - 2)
                    nc.vector.tensor_copy(v_nat[:, 1 - par].rearrange("p t c -> p (t c)"), bank(PROJ0)).then_inc(sem["v_ok"], 1)
                for n in range(NS):
                    if maxima:
                        dve.wait_ge(sem["max_mm"], NS * (s - 1) + n + 1)
                        if n == 0 and (not isinstance(s, int) or s >= 2):
                            dve.wait_ge(sem["m_mm"], s - 1)
                        nc.vector.reduce_max(m_col[:, n:n + 1], bank(MAX0 + n % 2), AX).then_inc(sem["rowmax"], 1)
                    if proj and n == 3:
                        quantise_context()
                    if proj and n in (7, 14):
                        low(0 if n == 7 else 1)
                if maxima:
                    dve.wait_ge(sem["m_mm"], s)
                    if not isinstance(s, int) or s >= 2:
                        dve.wait_ge(sem["shift_in"], 32 * (s - 1))
                    nc.vector.tensor_copy(m_row[:, 0, :], banks[LSUM][0:NS, 0:P]).then_inc(sem["m_hi_ok"], 1)
                    dve.wait_ge(sem["m_hi_ok"], s)
                    nc.vector.tensor_tensor(m_row[:, 1, :], banks[LSUM][0:NS, 0:P], m_row[:, 0, :].bitcast(f32), ALU.subtract).then_inc(sem["m_ok"], 1)
                if finish:
                    dve.wait_ge(sem["l_mm"], s - 1)
                    nc.vector.reciprocal(recip[:, :], bank(LSUM)).then_inc(sem["recip_ok"], 1)
                    dve.wait_ge(sem["recip_ok"], s - 1)
                    if not isinstance(s, int) or s >= 3:
                        dve.wait_ge(sem["ctx_out"], 16 * (s - 2))
                    nc.vector.tensor_tensor(ctxs[:, :], bank(CTX), recip[:, :], ALU.mult).then_inc(sem["ctx_ok"], 1)

            step(0, 0, 0)
            step(1, 1, 0)
            step(2, 0, 1)
            step(3, 1, 1)
            with dve.Fori(2, G - 1) as g:
                step(2 * g, 0, g)
                step(2 * g + 1, 1, g)
            step(UNITS - 2, 0, G - 1)
            step(UNITS - 1, 1, G - 1)
            for k in range(KT):
                dve.wait_ge(sem["ow_hi"], k + 1)
                nc.vector.tensor_tensor(big_lo[:, k, :], wst[:, k % 2, :], big_hi[:, k, :].bitcast(f32), ALU.subtract).then_inc(sem["ow_lo"], 1)
            step(UNITS, 0, G)
            step(UNITS + 1, 1, G)

            def stats(r, row, n, a, b, c):
                for h in range(2):
                    last = nc.vector.bn_stats(st[:, row, h, :], r[:, h * 512:(h + 1) * 512])
                last.then_inc(sem[a], 1)
                wait_alone(dve, sem[a], n)
                nc.vector.bn_aggr(mv[:, row, 0:2], st[:, row].rearrange("p a b -> p (a b)")).then_inc(sem[b], 1)
                dve.wait_ge(sem[b], n)
                nc.vector.tensor_scalar(mv[:, row, 1:2], mv[:, row, 1:2], EPS, None, ALU.add).then_inc(sem[c], 1)

            def minus_mean(row, n, ok, done):
                dve.wait_ge(sem[ok], n)
                nc.vector.tensor_scalar(mv[:, row, 3:4], mv[:, row, 0:1], mv[:, row, 2:3], -1.0, ALU.mult, ALU.mult).then_inc(sem[done], 1)

            def split_cx(n, par):
                dve.wait_ge(sem["cx_hi_ok"], n + 1)
                nc.vector.tensor_tensor(cx_lo[:, par], cx_raw[:, par], cx_hi[:, par].bitcast(f32), ALU.subtract).then_inc(sem["cx_lo_ok"], 1)

            def tail_step(n, par, i):
                more = not isinstance(n, int) or n < NT
                prev = not isinstance(n, int) or n >= 1
                q = 1 - par
                if not isinstance(n, int) or n < NT - 1:
                    split_cx(n + 1, q)
                if prev:
                    dve.wait_ge(sem["rs_mm"], n)
                    nc.vector.tensor_scalar(kcol[:, 0:1], banks[5][:, 0:1], sc[:, 10:11], sc[:, 11:12], ALU.mult, ALU.add).then_inc(sem["k1"], 1)
                    dve.wait_ge(sem["k1"], n)
                    nc.vector.tensor_scalar(kcol[:, 1:2], kcol[:, 0:1], sc[:, 5:6], None, ALU.mult).then_inc(sem["kc_ok"], 1)
                if more:
                    dve.wait_ge(sem["a_mm"], n + 1)
                    dve.wait_ge(sem["xr_ok"], n + 1)
                    if not isinstance(n, int) or n >= 2:
                        dve.wait_ge(by_parity["x2_out"][par], 16 * i)
                    for h in range(2):
                        cols = slice(h * 512, (h + 1) * 512)
                        last = nc.vector.tensor_tensor(x1s[:, par, cols], bank(h), xres[:, par, cols], ALU.add)
                    last.then_inc(sem["r1_ok"], 1)
                    dve.wait_ge(sem["r1_ok"], n + 1)
                    stats(x1s[:, par, :], 0, n + 1, "st1", "mv1", "ve1")
                if prev:
                    dve.wait_ge(sem["t_ok"], n)
                    dve.wait_ge(sem["x1c_ok"], n)
                    nc.vector.tensor_tensor(x1s[:, q, :], x1s[:, q, :], qtmp[:, q, :], ALU.add).then_inc(sem["r2_ok"], 1)
                if more:
                    minus_mean(0, n + 1, "rstd1", "nm1")
                if prev:
                    dve.wait_ge(sem["r2_ok"], n)
                    stats(x1s[:, q, :], 1, n, "st2", "mv2", "ve2")
                if more:
                    dve.wait_ge(sem["qp1"], n + 1)
                    nc.vector.tensor_scalar(qtmp[:, par, :], qtmp[:, par, :], 0.0, QMAX, ALU.max, ALU.min).then_inc(sem["qp2"], 1)
                    dve.wait_ge(sem["qp2"], n + 1)
                    if prev:
                        dve.wait_ge(sem["tr_mm"], n)
                    nc.vector.tensor_scalar(c1[:, :], qtmp[:, par, :], MAGIC, consts[:, 1:2], ALU.add, ALU.subtract).then_inc(sem["c1_ok"], 1)
                if prev:
                    minus_mean(1, n, "rstd2", "nm2")

            split_cx(0, 0)
            nc.vector.tensor_scalar(sc[:, 11:12], sc[:, 9:10], sc[:, 10:11], float(H), ALU.mult, ALU.mult).then_inc(sem["sc_ok"], 1)
            for b in range(NB):
                dve.wait_ge(sem["cs_mm"], b + 1)
                for h in range(2):
                    last = nc.vector.tensor_scalar(corr[:, b, h * 512:(h + 1) * 512], bank(6 + h), sc[:, 9:10], sc[:, 5:6], ALU.mult, ALU.mult)
                last.then_inc(sem["corr_ok"], 1)
            dve.wait_ge(sem["sc_ok"], 5)
            tail_step(0, 0, 0)
            tail_step(1, 1, 0)
            with dve.Fori(1, NT // 2 - 1) as i:
                tail_step(2 * i, 0, i)
                tail_step(2 * i + 1, 1, i)
            tail_step(NT - 2, 0, NT // 2 - 1)
            tail_step(NT - 1, 1, NT // 2 - 1)
            for k in range(KT):
                dve.wait_ge(sem["wb_hi"], k + 1)
                nc.vector.tensor_tensor(big_lo[:, k, :], wst[:, k % 2, :], big_hi[:, k, :].bitcast(f32), ALU.subtract).then_inc(sem["wb_lo"], 1)
            dve.wait_ge(sem["bt_in"], 32)
            nc.vector.tensor_copy(bt_hi[:, :], bt_raw[:, :]).then_inc(sem["bt_hi_ok"], 1)
            dve.wait_ge(sem["bt_hi_ok"], 1)
            nc.vector.tensor_tensor(bt_lo[:, :], bt_raw[:, :], bt_hi[:, :].bitcast(f32), ALU.subtract).then_inc(sem["bt_ok"], 1)
            tail_step(NT, 0, NT // 2)

            def split_x2T(n, par):
                dve.wait_ge(sem["xt_ok"], n + 1)
                if not isinstance(n, int) or n >= 2:
                    dve.wait_ge(sem["c_mm"], n - 1)
                nc.vector.tensor_copy(x2T_hi[:, par].rearrange("p k c -> p (k c)"), x2T[:].rearrange("p k c -> p (k c)")).then_inc(sem["xthi_ok"], 1)
                dve.wait_ge(sem["xthi_ok"], n + 1)
                nc.vector.tensor_tensor(x2T_lo[:, par], x2T[:, :, :], x2T_hi[:, par].bitcast(f32), ALU.subtract).then_inc(sem["xtlo_ok"], 1)

            def route(n):
                logits = banks[4][:, ER:ER + NE]
                wait_alone(dve, sem["h_mm"], n + 1)
                nc.vector.max(rt[:, 0:8], logits).then_inc(sem["rv1"], 1)
                wait_alone(dve, sem["rv1"], n + 1)
                nc.vector.max_index(ridx[:, :], rt[:, 0:8], logits).then_inc(sem["rv2"], 1)
                nc.vector.tensor_scalar(rt[:, 16:17], rt[:, 0:1], -1.0, None, ALU.mult).then_inc(sem["rv3"], 1)
                dve.wait_ge(sem["rv2"], n + 1)
                nc.vector.tensor_copy(rt[:, 21:23], ridx[:, 0:2]).then_inc(sem["rw1"], 1)
                dve.wait_ge(sem["re_ok"], n + 1)
                nc.vector.tensor_tensor(rt[:, 17:18], rt[:, 8:9], rt[:, 9:10], ALU.add).then_inc(sem["rw2"], 1)
                dve.wait_ge(sem["rw2"], n + 1)
                nc.vector.reciprocal(rt[:, 18:19], rt[:, 17:18]).then_inc(sem["rw3"], 1)
                dve.wait_ge(sem["rw3"], n + 1)
                nc.vector.tensor_scalar(rt[:, 19:21], rt[:, 8:10], rt[:, 18:19], SCALING, ALU.mult, ALU.mult).then_inc(sem["rw4"], 1)
                dve.wait_ge(sem["rw4"], n + 1)
                dve.wait_ge(sem["rw1"], n + 1)
                for e in range(2):
                    last = nc.vector.tensor_scalar(rt[:, 24 + 8 * e:32 + 8 * e], iota[:, :], rt[:, 21 + e:22 + e], rt[:, 19 + e:20 + e],
                                                   ALU.is_equal, ALU.mult)
                last.then_inc(sem["rw5"], 1)
                dve.wait_ge(sem["rw5"], n + 1)
                nc.vector.tensor_tensor(rt[:, 24:32], rt[:, 24:32], rt[:, 32:40], ALU.add).then_inc(sem["comb_ok"], 1)
                dve.wait_ge(sem["comb_ok"], n + 1)
                if not isinstance(n, int) or n >= 1:
                    dve.wait_ge(sem["hwt_mm"], n)
                nc.vector.tensor_tensor(hw[:, :].rearrange("p (e r) -> p e r", r=R), banks[4][:, 0:ER].rearrange("p (e r) -> p e r", r=R),
                                        rt[:, 24:32].unsqueeze(2).to_broadcast([P, NE, R]), ALU.mult).then_inc(sem["hw_ok"], 1)
                dve.wait_ge(sem["hwt_mm"], n + 1)
                if not isinstance(n, int) or n >= 1:
                    dve.wait_ge(sem["c_mm"], n)
                nc.vector.tensor_copy(hwT_hi[:, :], banks[5][:, 0:P]).then_inc(sem["hwthi_ok"], 1)
                dve.wait_ge(sem["hwthi_ok"], n + 1)
                nc.vector.tensor_tensor(hwT_lo[:, :], banks[5][:, 0:P], hwT_hi[:, :].bitcast(f32), ALU.subtract).then_inc(sem["hwtlo_ok"], 1)

            def last_step(n, par, i, more):
                route(n)
                if more:
                    split_x2T(n + 1, 1 - par)
                dve.wait_ge(sem["c_mm"], n + 1)
                dve.wait_ge(sem["xb_ok"], n + 1)
                if not isinstance(n, int) or n >= 2:
                    dve.wait_ge(by_parity["o_out"][par], 16 * i)
                for h in range(2):
                    cols = slice(h * 512, (h + 1) * 512)
                    last = nc.vector.tensor_tensor(r3[:, par, cols], bank(2 * par + h), xb[:, par, cols], ALU.add)
                last.then_inc(sem["r3_ok"], 1)
                dve.wait_ge(sem["r3_ok"], n + 1)
                if not isinstance(n, int) or n >= 1:
                    dve.wait_ge(sem["o_ok"], n)
                stats(r3[:, par, :], 0, n + 1, "st3", "mv3", "ve3")
                minus_mean(0, n + 1, "rstd3", "nm3")

            split_x2T(0, 0)
            last_step(0, 0, 0, True)
            last_step(1, 1, 0, True)
            with dve.Fori(1, NT // 2 - 1) as i:
                last_step(2 * i, 0, i, True)
                last_step(2 * i + 1, 1, i, True)
            last_step(NT - 2, 0, NT // 2 - 1, True)
            last_step(NT - 1, 1, NT // 2 - 1, False)


def kernel(x, ctx_4096, L0_attn_attn_qkvw, L0_attn_attn_qkvb, L0_attn_attn_ow, L0_attn_attn_ob,
           L0_xattn_x1_scale, L0_xattn_x1_zp, L0_xattn_x2_scale, L0_xattn_x2_zp,
           L0_ffn_W_base, L0_ffn_b_base, L0_ffn_W_router, L0_ffn_A, L0_ffn_B):
    import numpy as np
    import concourse.bacc as bacc
    from concourse.bass_utils import run_bass_kernel_spmd

    P = 128
    B, S, H = x.shape
    G = H // P
    c = np.ascontiguousarray
    x2d = np.asarray(x).reshape(B * S, H)
    arrays = {
        "xT": c(x2d.T),
        "x": c(x2d),
        "wqkv": c(np.asarray(L0_attn_attn_qkvw).reshape(G, P, 3, G, P).transpose(3, 1, 2, 0, 4)),
        "qkvb": c(np.asarray(L0_attn_attn_qkvb).reshape(3, G, P).transpose(2, 1, 0)),
        "ow": c(L0_attn_attn_ow),
        "ob": c(L0_attn_attn_ob),
        "ctx": c(ctx_4096),
        "scales": c(np.stack([np.asarray(a).reshape(1) for a in (L0_xattn_x1_scale, L0_xattn_x1_zp, L0_xattn_x2_scale, L0_xattn_x2_zp)])),
        "wbT": c(np.asarray(L0_ffn_W_base).T),
        "bb": c(L0_ffn_b_base),
    }
    E, R, _ = L0_ffn_A.shape
    ar = np.concatenate([np.asarray(L0_ffn_A).reshape(E * R, H), np.asarray(L0_ffn_W_router)], axis=0)
    arrays["art"] = c(ar.T.reshape(G, P, E * R + E).transpose(1, 0, 2))
    arrays["bt"] = c(np.asarray(L0_ffn_B).transpose(0, 2, 1).reshape(E * R, H))

    nc = bacc.Bacc("TRN2", target_bir_lowering=False, num_devices=1)
    aps = [nc.dram_tensor(f"in_{n}", a.shape, mybir.dt.from_np(a.dtype), kind="ExternalInput").ap() for n, a in arrays.items()]
    out = nc.dram_tensor("out", (B * S, H), mybir.dt.float32, kind="ExternalOutput").ap()
    decoder_layer(nc, *aps, out)
    r = run_bass_kernel_spmd(nc, [{f"in_{n}": a for n, a in arrays.items()}], core_ids=[0])
    return r.results[0]["out"].reshape(B, S, H)
```

```python
import concourse.bass as bass
from concourse import mybir
from concourse.alu_op_type import AluOpType as ALU
from contextlib import ExitStack


def decoder_layer(nc, xT, x, wqkv, qkvb, ow, ob, ctx_in, scales, wbT, bb, art, bt, out):
    f32, f32r, bf16, u32 = mybir.dt.float32, mybir.dt.float32r, mybir.dt.bfloat16, mybir.dt.uint32
    ACT = mybir.ActivationFunctionType
    AX = mybir.AxisListType.X

    P = 128
    H = x.shape[1]
    TOK = x.shape[0]
    NB = ctx_in.shape[0]
    S = TOK // NB
    KT = H // P
    HD = 32
    HPG = P // HD
    G = H // P
    QT = S // P
    NS = HPG * QT
    UNITS = G * NB
    SM_SCALE = float(HD) ** -0.5
    NE = 8
    ER = art.shape[2] - NE
    R = ER // NE
    SCALING = 32.0 / R
    EPS = 1e-5
    QMAX = 255.0
    MAGIC = 1.5 * 2.0 ** 23
    PACK_HI2, PACK_LO, SHIFT = HD, 2 * HD, 3 * HD
    NT = TOK // P
    PACK_INC = 6 * 16

    es = ExitStack()
    with es:
        KB = 1024
        base = 16512

        def at(name, off, shape, dt):
            return nc.alloc_sbuf_tensor_at(name, shape, dt, offset=base + int(off * KB))

        big_hi = at("big_hi", 0, [P, KT, H], f32r)
        big_lo = at("big_lo", 32, [P, KT, H], f32r)
        big_raw = at("big_raw", 32, [P, KT, H], f32)
        w_hi = at("w_hi", 64, [P, 3, KT, P], f32r)
        w_lo = at("w_lo", 76, [P, 3, KT, P], f32r)
        w_raw = at("w_raw", 88, [P, 3, KT, P], f32)
        q_hi = at("q_hi", 100, [P, S], f32r)
        q_lo = at("q_lo", 102, [P, S], f32r)
        k_hi = at("k_hi", 104, [P, S], f32r)
        k_lo = at("k_lo", 106, [P, S], f32r)
        qp = at("qp", 108, [P, 2, HPG, S], f32r)
        kp = at("kp", 124, [P, 2, HPG, S], f32r)
        probs = at("probs", 140, [P, HPG, QT, S], f32)
        v_nat = at("v_nat", 172, [P, 2, QT, P], f32)
        vT = at("vT", 176, [P, S], f32)
        psumk = at("psumk", 178, [P, HPG, S], f32)
        recip = at("recip", 186, [P, S], f32)
        ctxs = at("ctxs", 188, [P, S], f32)
        ident = at("ident", 190, [P, P], f32)
        identb = at("identb", 190.5, [P, P], bf16)
        m_row = at("m_row", 190.75, [NS, 2, P], f32r)
        ones = at("ones", 191.75, [P, HD], f32)
        bias = at("bias", 191.875, [P, G, 3], f32)
        c_raw = at("c_raw", 192, [P, H], f32)
        ob_sb = at("ob_sb", 200, [P, H], f32)
        c_q = at("c_q", 204, [P, H], bf16)
        m_col = at("m_col", 206, [P, NS], f32)
        sc = at("sc", 206.0625, [P, 12], f32)
        consts = at("consts", 206.125, [P, 4], f32)
        onesb = at("onesb", 206.15625, [P, P], bf16)
        iota = at("iota", 206.40625, [P, NE], f32)
        st = at("st", 206.4375, [P, 2, 2, 6], f32)
        mv = at("mv", 206.53125, [P, 2, 4], f32)
        kcol = at("kcol", 206.5625, [P, 2], f32)
        rt = at("rt", 206.59375, [P, 40], f32)
        ridx = at("ridx", 206.75, [P, NE], u32)
        c2 = at("c2", 64, [P, NB, KT, H], bf16)
        c1T = at("c1T", 96, [P, 2, KT, P], bf16)
        cx_hi = [at(f"cx_hi{q}", 108 + 8 * q, [P, KT, P], f32r) for q in range(2)]
        cx_lo = [at(f"cx_lo{q}", 112 + 8 * q, [P, KT, P], f32r) for q in range(2)]
        corr = at("corr", 124, [P, NB, H], f32)
        cx_raw = at("cx_raw", 100, [P, 2, KT, P], f32)
        qtmp = at("qtmp", 132, [P, 2, H], f32)
        wb_raw = at("wb_raw", 140, [P, KT, H], f32)
        x1s = at("x1s", 172, [P, 2, H], f32)
        xres = at("xres", 180, [P, 2, H], f32)
        c1 = at("c1", 188, [P, H], bf16)
        x2T = at("x2T", 64, [P, KT, P], f32)
        x2T_hi = [at(f"x2T_hi{q}", 68 + 4 * q, [P, KT, P], f32r) for q in range(2)]
        x2T_lo = [at(f"x2T_lo{q}", off, [P, KT, P], f32r) for q, off in enumerate((76, 104))]
        art_sb = at("art_sb", 108, [P, KT, ER + NE], f32)
        bt_hi = at("bt_hi", 112.25, [P, H], f32r)
        bt_lo = at("bt_lo", 116.25, [P, H], f32r)
        hw = at("hw", 120.5, [P, ER], f32)
        hwT_hi = at("hwT_hi", 121, [P, P], f32r)
        hwT_lo = at("hwT_lo", 121.5, [P, P], f32r)
        r3 = at("r3", 124, [P, 2, H], f32)
        bt_raw = at("bt_raw", 100, [P, H], f32)
        xb = at("xb", 180, [P, 2, H], f32)
        x2s = at("x2s", 192, [P, 2, H], f32)
        bb_sb = at("bb_sb", 200, [P, H], f32)

        banks = [es.enter_context(nc.psum_tensor(f"bank{i}", [P, 512], f32)) for i in range(8)]
        PROJ0, PROJ1, MAX0, ST0, CTX, LSUM = 0, 1, 2, 4, 6, 7

        ctx_d = nc.dram_tensor("ctx_scratch", [H, TOK], f32).ap()
        c2_d = nc.dram_tensor("c2_scratch", [NB * KT, P, H], bf16).ap()
        x2_d = nc.dram_tensor("x2_scratch", [TOK, H], f32).ap()
        ctx_v = ctx_d.rearrange("(k p) t -> p k t", p=P)
        ctx_tiles = ctx_in.rearrange("b (k p) n -> (b k) p n", p=P)

        names = """x_hi_ok x_lo_ok const_in w_in w_hi_ok w_split proj_done hi_ok lo_ok vT_ok vt_mm v_ok
        max_mm rowmax m_mm m_hi_ok m_ok shift_in st_mm exp_ok pool_sum psum_ok pv_mm l_mm recip_ok ctx_ok
        ctx_out const_ok idb_ok ctxq_in ctxq_1 ctxq_2 ctxq_ok c2_out ow_hi ow_lo wb_in const_w
        cs_mm corr_ok sc_ok
        cx_hi_ok cx_lo_ok cx7_in cx7_hi cx7_lo xr_ok a_half a_mm r1_ok st1 mv1 ve1 rstd1 nm1 x1_ok qp1 qp2 c1_ok tr_mm c1T_ok
        rs_mm b_mm k1 kc_ok x1c_ok t_ok r2_ok st2 mv2 ve2 rstd2 nm2 x2_ok
        bt_in bt_hi_ok bt_ok art_in wb_hi wb_lo_even wb_lo_odd xt_mm xt_ok xthi_ok xtlo_ok h_mm rv1 rv2 rv3 re_ok
        rw1 rw2 rw3 rw4 rw5 comb_ok hw_ok hwt_mm hwthi_ok hwtlo_ok c_mm xb_ok r3_ok st3 mv3 ve3 rstd3 nm3
        o_ok passed minus_ok""".split()
        sem = {n: es.enter_context(nc.semaphore(n)) for n in names}
        big_in = [[es.enter_context(nc.semaphore(f"big_in{b}_{k}")) for k in range(KT)] for b in range(NB)]
        c2_in = [es.enter_context(nc.semaphore(f"c2_in{b}")) for b in range(NB)]
        w_first = [es.enter_context(nc.semaphore(f"w_first{n}")) for n in range(3)]
        by_parity = {n: [es.enter_context(nc.semaphore(f"{n}_{q}")) for q in range(2)]
                     for n in ("a_in", "xr_in", "x2_in", "x2_out", "o_out")}
        packed = [es.enter_context(nc.semaphore(f"packed{j}")) for j in range(HPG)]
        block = es.enter_context(nc.Block())

        def steps_of(eng, step):
            step(0, 0, 0)
            step(1, 1, 0)
            step(2, 0, 1)
            step(3, 1, 1)
            with eng.Fori(2, G - 1) as g:
                step(2 * g, 0, g)
                step(2 * g + 1, 1, g)
            for s in range(UNITS - 2, UNITS + 2):
                step(s, s % 2, s // 2)

        def stages(s):
            if not isinstance(s, int):
                return True, True, True
            return s < UNITS, 1 <= s <= UNITS, s >= 2

        def divides(s):
            return not isinstance(s, int) or s >= 3

        def wait_alone(eng, semaphore, value):
            eng.wait_ge(semaphore, value)
            eng.sem_inc(sem["passed"], 1)

        def bank(i, lo=0, hi=512):
            return banks[i][:, lo:hi]

        @block.sync
        def _(sp):
            wq_v = wqkv.rearrange("g p a k c -> g p (a k c)")
            sp.dma_start(w_raw[:, 0], wqkv[0, :, 0]).then_inc(w_first[0], 16)
            for b in range(NB):
                for k in range(KT):
                    sp.dma_start(big_raw[:, k, b * S:(b + 1) * S], xT[k * P:(k + 1) * P, b * S:(b + 1) * S]).then_inc(big_in[b][k], 16)
                    if b == 0 and k == 1:
                        sp.dma_start(bias[:, :, :], qkvb).then_inc(sem["const_in"], 16)
                        for n in range(4):
                            sp.dma_start(sc[:, n:n + 1], scales[n].rearrange("(a n) -> a n", a=1).to_broadcast([P, 1])).then_inc(sem["const_in"], 16)
                for n in (1, 2) if b == 0 else ():
                    sp.dma_start(w_raw[:, n], wqkv[0, :, n]).then_inc(w_first[n], 16)
            sp.dma_start(ob_sb[:, :], ob.rearrange("(a n) -> a n", a=1).to_broadcast([P, H])).then_inc(sem["const_w"], 16)

            def pack(s, par, j, which):
                rows = slice(j * HD, (j + 1) * HD)
                if which == "q":
                    parts = ((qp, 0, q_hi), (qp, PACK_HI2, q_lo), (qp, PACK_LO, q_hi))
                else:
                    parts = ((kp, 0, k_hi), (kp, PACK_HI2, k_hi), (kp, PACK_LO, k_lo))
                if not isinstance(s, int) or s >= 2:
                    sp.wait_ge(sem["st_mm"], NS * (s - 2) + QT * (j + 1))
                for dst, row, src in parts:
                    sp.dma_start(dst[row:row + HD, par, j, :].bitcast(f32), src[rows, :].bitcast(f32)).then_inc(packed[j], 16)

            def store_context(u, q, gu):
                wait_alone(sp, sem["ctx_ok"], u + 1)
                sp.dma_start(ctx_d[bass.ds(gu * P, P), q * S:(q + 1) * S], ctxs[:, :]).then_inc(sem["ctx_out"], 16)

            def step(s, par, g):
                proj, maxima, finish = stages(s)
                if proj and par == 0 and (not isinstance(s, int) or s < UNITS - 2):
                    wait_alone(sp, sem["w_split"], 3 * (g + 1))
                    sp.dma_start(w_raw[:].rearrange("p a k c -> p (a k c)"), wq_v[bass.ds(g + 1, 1)].rearrange("a p n -> (a p) n")).then_inc(sem["w_in"], 16)
                if proj:
                    if not isinstance(s, int) or s >= 1:
                        wait_alone(sp, sem["ctxq_ok"], s)
                    sp.dma_start(c_raw[:, :], ctx_tiles[bass.ds(s, 1)].rearrange("a p n -> (a p) n")).then_inc(sem["ctxq_in"], 16)
                if divides(s) and (not isinstance(s, int) or s <= UNITS):
                    store_context(s - 3, 1 - par, g - 2 + par)
                if proj:
                    sp.wait_ge(sem["lo_ok"], 2 * s + 1)
                    pack(s, par, 0, "q")
                    pack(s, par, 1, "q")
                    sp.wait_ge(sem["lo_ok"], 2 * s + 2)
                    pack(s, par, 0, "k")
                    pack(s, par, 1, "k")
                    pack(s, par, 2, "q")
                    pack(s, par, 2, "k")
                if maxima:
                    sp.wait_ge(sem["m_ok"], s)
                    for half in range(2):
                        sp.dma_start(qp[SHIFT + half:SHIFT + half + 1, 1 - par, :, :].rearrange("a j (t q) -> a (j t) q", q=P).bitcast(f32),
                                     m_row[:, half, :].bitcast(f32)).then_inc(sem["shift_in"], 16)
                if proj:
                    pack(s, par, 3, "q")
                    pack(s, par, 3, "k")
                if proj:
                    wait_alone(sp, sem["ctxq_ok"], s + 1)
                    sp.dma_start(c2_d[bass.ds(s, 1)].rearrange("a p n -> (a p) n"), c_q[:, :]).then_inc(sem["c2_out"], 16)

            step(0, 0, 0)
            step(1, 1, 0)
            step(2, 0, 1)
            step(3, 1, 1)
            with sp.Fori(2, G - 1) as g:
                step(2 * g, 0, g)
                step(2 * g + 1, 1, g)
            step(UNITS - 2, 0, G - 1)
            step(UNITS - 1, 1, G - 1)
            sp.wait_ge(sem["proj_done"], 3 * UNITS)
            for k in range(KT // 2):
                sp.dma_start(big_raw[:, k, :], ow[k * P:(k + 1) * P, :]).then_inc(big_in[0][k], 16)
            sp.wait_ge(sem["c2_out"], 16 * UNITS)
            sp.dma_start(c2[:, 0], c2_d[0:KT].rearrange("k p n -> p k n")).then_inc(c2_in[0], 16)
            for k in range(KT // 2, KT):
                sp.dma_start(big_raw[:, k, :], ow[k * P:(k + 1) * P, :]).then_inc(big_in[0][k], 16)
            step(UNITS, 0, G)

            def load_tile(n, par, i):
                if not isinstance(n, int) or n >= 2:
                    wait_alone(sp, sem["cx_lo_ok"], n - 1)
                sp.dma_start(cx_raw[:, par], ctx_v[:, :, bass.ds(par * S + i * P, P)]).then_inc(by_parity["a_in"][par], 16)

            def load_residual(n, par, i):
                if not isinstance(n, int) or n >= 2:
                    wait_alone(sp, sem["r1_ok"], n - 1)
                sp.dma_start(xres[:, par, :], x[bass.ds(par * S + i * P, P), :]).then_inc(by_parity["xr_in"][par], 16)

            def store_x2(m, par, i):
                wait_alone(sp, sem["x2_ok"], m + 1)
                sp.dma_start(x2_d[bass.ds(par * S + i * P, P), :], x1s[:, par, :]).then_inc(by_parity["x2_out"][par], 16)

            def load_first_tile(q):
                sp.dma_start(cx_raw[:, q, 0:KT - 1], ctx_v[:, 0:KT - 1, q * S:q * S + P]).then_inc(by_parity["a_in"][q], 16)

            def load_last_group(q):
                sp.wait_ge(sem["ctx_ok"], UNITS - 1 + q)
                sp.dma_start(cx_raw[:, q, KT - 1, :], ctxs[:, 0:P]).then_inc(sem["cx7_in"], 16)

            for j in range(HPG):
                sp.wait_ge(packed[j], PACK_INC * UNITS)
            sp.wait_ge(sem["ctx_out"], 16 * (UNITS - 2))
            load_first_tile(0)
            sp.dma_start(c2[:, 1], c2_d[KT:2 * KT].rearrange("k p n -> p k n")).then_inc(c2_in[1], 16)
            load_first_tile(1)
            load_last_group(0)
            store_context(UNITS - 2, 0, G - 1)
            sp.wait_ge(sem["l_mm"], UNITS)
            load_residual(0, 0, 0)
            load_last_group(1)
            store_context(UNITS - 1, 1, G - 1)
            load_residual(1, 1, 0)
            sp.wait_ge(sem["ctx_out"], 16 * UNITS)
            sp.wait_ge(sem["cx7_lo"], 1)
            load_tile(2, 0, 1)

            def load_wb(k):
                sp.dma_start(wb_raw[:, bass.ds(k, 1), :].rearrange("p a n -> p (a n)"), wbT[bass.ds(k * P, P), :]).then_inc(sem["wb_in"], 16)

            load_wb(0)
            load_wb(1)
            load_residual(2, 0, 1)
            with sp.Fori(1, NT // 2 - 1) as i:
                load_tile(2 * i + 1, 1, i)
                load_wb(3 * i - 1)
                load_wb(3 * i)
                load_residual(2 * i + 1, 1, i)
                store_x2(2 * i - 2, 0, i - 1)
                load_tile(2 * i + 2, 0, i + 1)
                load_wb(3 * i + 1)
                load_residual(2 * i + 2, 0, i + 1)
                store_x2(2 * i - 1, 1, i - 1)
            load_tile(NT - 1, 1, NT // 2 - 1)
            load_residual(NT - 1, 1, NT // 2 - 1)

            def load_x2(n, par, i):
                if not isinstance(n, int) or n >= 2:
                    sp.wait_ge(sem["xb_ok"], n - 1)
                    wait_alone(sp, sem["xt_mm"], n - 1)
                sp.dma_start(x2s[:, par, :], x2_d[bass.ds(par * S + i * P, P), :]).then_inc(by_parity["x2_in"][par], 16)

            for q in range(2):
                sp.wait_ge(by_parity["x2_out"][q], 16)
                load_x2(q, q, 0)
            store_x2(NT - 4, 0, NT // 2 - 2)
            sp.wait_ge(sem["cx_lo_ok"], NT)
            sp.dma_start(bt_raw[:, :], bt).then_inc(sem["bt_in"], 16)
            sp.wait_ge(sem["xr_ok"], NT)
            sp.dma_start(bb_sb[:, :], bb.rearrange("(a n) -> a n", a=1).to_broadcast([P, H])).then_inc(sem["bt_in"], 16)
            store_x2(NT - 3, 1, NT // 2 - 2)
            sp.wait_ge(sem["a_mm"], NT)
            sp.dma_start(art_sb[:, :, :], art).then_inc(sem["art_in"], 16)
            store_x2(NT - 2, 0, NT // 2 - 1)

            def store(n, par, i):
                wait_alone(sp, sem["o_ok"], n + 1)
                sp.dma_start(out[bass.ds(par * S + i * P, P), :], r3[:, par, :]).then_inc(by_parity["o_out"][par], 16)

            sp.wait_ge(by_parity["x2_out"][0], 32)
            load_x2(2, 0, 1)
            store_x2(NT - 1, 1, NT // 2 - 1)
            sp.wait_ge(by_parity["x2_out"][1], 32)
            store(0, 0, 0)
            load_x2(3, 1, 1)
            store(1, 1, 0)
            for q in range(2):
                sp.wait_ge(by_parity["x2_out"][q], 16 * NT // 2)
            with sp.Fori(2, NT // 2) as i:
                load_x2(2 * i, 0, i)
                store(2 * i - 2, 0, i - 1)
                load_x2(2 * i + 1, 1, i)
                store(2 * i - 1, 1, i - 1)
            store(NT - 2, 0, NT // 2 - 1)
            store(NT - 1, 1, NT // 2 - 1)
            for q in range(2):
                sp.wait_ge(by_parity["o_out"][q], 16 * NT // 2)

        @block.tensor
        def _(pe):
            def split_mm(dst, lhs, rhs, k, last_k, first=None):
                for n, (a, b) in enumerate(((0, 0), (0, 1), (1, 0))):
                    mm = nc.tensor.matmul(dst, lhs[a], rhs[b], start=(k == 0 and n == 0) if first is None else False,
                                          stop=(k == last_k and n == 2))
                return mm

            def row_sums(u):
                pe.wait_ge(sem["psum_ok"], HPG * (u + 1))
                if not isinstance(u, int) or u + 2 <= UNITS:
                    pe.wait_ge(sem["m_ok"], u + 2)
                else:
                    pe.wait_ge(sem["recip_ok"], u)
                for j in range(HPG):
                    mm = nc.tensor.matmul(banks[LSUM][j * HD:(j + 1) * HD, :], ones[:, :], psumk[:, j, :],
                                          start=True, stop=True, skip_group_check=True)
                mm.then_inc(sem["l_mm"], 1)

            def step(s, par, g):
                proj, maxima, finish = stages(s)
                first = isinstance(s, int) and s == 0
                cols = slice(par * S, (par + 1) * S)

                def transpose_v():
                    pe.wait_ge(sem["vT_ok"], s)
                    pe.wait_ge(sem["lo_ok"], 2 * s)
                    if isinstance(s, int) and s == 1:
                        pe.wait_ge(sem["const_ok"], 1)
                    for t in range(QT):
                        mm = nc.tensor.transpose(bank(PROJ0, t * P, (t + 1) * P), vT[:, t * P:(t + 1) * P], ident[:, :])
                    mm.then_inc(sem["vt_mm"], 1)

                def project(n):
                    piece, k = n // KT, n % KT
                    dst = bank(PROJ1 if piece != 1 else PROJ0)
                    if k == 0:
                        pe.wait_ge(sem["w_split"], 3 * g + piece + 1)
                        if piece == 0 and not first:
                            pe.wait_ge(sem["vT_ok"], s)
                        if piece == 1 and not first:
                            pe.wait_ge(sem["v_ok"], s)
                        if piece == 2:
                            pe.wait_ge(sem["lo_ok"], 2 * s + 1)
                    if isinstance(s, int) and s < NB and piece == 0:
                        pe.wait_ge(sem["x_lo_ok"], s * KT + k + 1)
                    mm = split_mm(dst, (w_hi[:, piece, k, :], w_lo[:, piece, k, :]),
                                  (big_hi[:, k, cols], big_lo[:, k, cols]), k, KT - 1)
                    if k == KT - 1:
                        mm.then_inc(sem["proj_done"], 1)

                def score(n):
                    j, t = n // QT, n % QT
                    if t == 0:
                        pe.wait_ge(packed[j], PACK_INC * s)
                    if n >= 2:
                        pe.wait_ge(sem["rowmax"], NS * (s - 1) + n - 1)
                    nc.tensor.matmul(bank(MAX0 + n % 2), qp[0:SHIFT, 1 - par, j, t * P:(t + 1) * P],
                                     kp[0:SHIFT, 1 - par, j, :], start=True, stop=True).then_inc(sem["max_mm"], 1)

                def maxima_to_rows():
                    pe.wait_ge(sem["rowmax"], NS * s)
                    if not isinstance(s, int) or s >= 3:
                        pe.wait_ge(sem["recip_ok"], s - 2)
                    nc.tensor.transpose(banks[LSUM][0:NS, 0:P], m_col[:, :], ident[:, :]).then_inc(sem["m_mm"], 1)

                def score_t(n):
                    j, t = n // QT, n % QT
                    if n == 0:
                        pe.wait_ge(sem["shift_in"], 32 * (s - 1))
                        if isinstance(s, int) and s == 2:
                            pe.wait_ge(sem["minus_ok"], 1)
                    if n >= 2:
                        pe.wait_ge(sem["exp_ok"], NS * (s - 2) + n - 1)
                    nc.tensor.matmul(bank(ST0 + n % 2), kp[0:SHIFT + 2, par, j, t * P:(t + 1) * P],
                                     qp[0:SHIFT + 2, par, j, :], start=True, stop=True).then_inc(sem["st_mm"], 1)

                def context():
                    pe.wait_ge(sem["v_ok"], s - 1)
                    if divides(s):
                        pe.wait_ge(sem["ctx_ok"], s - 2)
                    for t in range(QT):
                        pe.wait_ge(sem["exp_ok"], NS * (s - 1) - QT + t + 1)
                        for j in range(HPG):
                            mm = nc.tensor.matmul(banks[CTX][j * HD:(j + 1) * HD, :], v_nat[:, par, t, j * HD:(j + 1) * HD],
                                                  probs[:, j, t, :], start=(t == 0), stop=(t == QT - 1), skip_group_check=True)
                    mm.then_inc(sem["pv_mm"], 1)

                def last_steps():
                    for n in range(NS):
                        if maxima:
                            score(n)
                            if n == 1:
                                row_sums(s - 3)
                        score_t(n)
                        if not maxima:
                            if n == 0:
                                pe.wait_ge(sem["v_ok"], UNITS)
                                pe.wait_ge(c2_in[1], 16)
                            column_sums(1, n)
                    if maxima:
                        maxima_to_rows()
                    context()
                    if maxima:
                        pe.wait_ge(c2_in[0], 16)
                        for n in range(2 * KT):
                            column_sums(0, n)
                        row_sums(s - 2)

                if maxima:
                    transpose_v()
                if not proj:
                    last_steps()
                    return
                done = 0
                for q in range(3 * NS):
                    if proj and q % 2 == 0:
                        project(q // 2)
                    if maxima and q >= FIRST_SCORE and done < NS and 5 * (q - FIRST_SCORE) >= 11 * done:
                        score(done)
                        done += 1
                    if maxima and q == 3 * NS - 3:
                        maxima_to_rows()
                    if finish and q % 3 == 2:
                        score_t(q // 3)
                    if divides(s) and q == 4:
                        row_sums(s - 3)
                if finish:
                    context()

            def column_sums(b, n):
                h, k = n // KT, n % KT
                mm = nc.tensor.matmul(bank(2 - 2 * b + h), onesb[:, :], c2[:, b, k, h * 512:(h + 1) * 512],
                                      start=(k == 0), stop=(k == KT - 1))
                if n == 2 * KT - 1:
                    mm.then_inc(sem["cs_mm"], 1)

            FIRST_SCORE = 10
            steps_of(pe, step)

            def out_project(n, par, h):
                if h == 0:
                    pe.wait_ge(sem["cx_lo_ok"], n + 1)
                    if not isinstance(n, int) or n >= 1:
                        pe.wait_ge(sem["r1_ok"], n)
                    else:
                        pe.wait_ge(sem["corr_ok"], NB)
                for k in range(KT):
                    if isinstance(n, int) and n < 2 and h == 0 and k == KT - 1:
                        pe.wait_ge(sem["cx7_lo"], n + 1)
                    if isinstance(n, int) and n == 0 and h == 0:
                        pe.wait_ge(sem["ow_lo"], k + 1)
                    if isinstance(n, int) and n == 0 and h == 1 and k == 0:
                        row_sums(UNITS - 1)
                    if h and k == KT // 2 and (not isinstance(n, int) or n >= 1):
                        transpose_c1(n - 1)
                    mm = split_mm(bank(h), (cx_hi[par][:, k, :], cx_lo[par][:, k, :]),
                                  (big_hi[:, k, h * 512:(h + 1) * 512], big_lo[:, k, h * 512:(h + 1) * 512]), k, KT - 1)
                mm.then_inc(sem["a_mm" if h else "a_half"], 1)

            def transpose_c1(m):
                pe.wait_ge(sem["c1_ok"], m + 1)
                if not isinstance(m, int) or m >= 1:
                    pe.wait_ge(sem["c1T_ok"], m)
                c1p = banks[4][:, :].bitcast(bf16)
                for k in range(KT):
                    mm = nc.tensor.transpose(c1p[:, k * P:(k + 1) * P], c1[:, k * P:(k + 1) * P], identb[:, :])
                mm.then_inc(sem["tr_mm"], 1)

            def context_product(m, par):
                pe.wait_ge(sem["c1T_ok"], m + 1)
                if not isinstance(m, int) or m >= 1:
                    pe.wait_ge(sem["k1"], m)
                    pe.wait_ge(sem["t_ok"], m)
                for k in range(KT):
                    mm = nc.tensor.matmul(banks[5][:, 0:2], c1T[:, par, k, :], onesb[:, 0:2], start=(k == 0), stop=(k == KT - 1))
                mm.then_inc(sem["rs_mm"], 1)
                for h in range(2):
                    for k in range(KT):
                        mm = nc.tensor.matmul(bank(2 + h), c1T[:, par, k, :], c2[:, par, k, h * 512:(h + 1) * 512],
                                              start=(k == 0), stop=(k == KT - 1))
                mm.then_inc(sem["b_mm"], 1)

            def tail_step(n, par):
                out_project(n, par, 0)
                out_project(n, par, 1)
                if not isinstance(n, int) or n >= 1:
                    context_product(n - 1, 1 - par)

            tail_step(0, 0)
            tail_step(1, 1)
            with pe.Fori(1, NT // 2) as i:
                tail_step(2 * i, 0)
                tail_step(2 * i + 1, 1)

            def transpose_x2(n, par, i):
                pe.wait_ge(by_parity["x2_in"][par], 16 * (i + 1))
                if not isinstance(n, int) or n >= 1:
                    pe.wait_ge(sem["xt_ok"], n)
                for k in range(KT):
                    mm = nc.tensor.transpose(bank(6 + k // 4, (k % 4) * P, (k % 4 + 1) * P), x2s[:, par, k * P:(k + 1) * P], ident[:, :])
                mm.then_inc(sem["xt_mm"], 1)

            def hidden(n):
                pe.wait_ge(sem["xt_ok"], n + 1)
                if isinstance(n, int) and n == 0:
                    pe.wait_ge(sem["art_in"], 16)
                    pe.wait_ge(sem["c1T_ok"], NT - 1)
                else:
                    pe.wait_ge(sem["hw_ok"], n)
                for k in range(KT):
                    mm = nc.tensor.matmul(banks[4][:, 0:ER + NE], x2T[:, k, :], art_sb[:, k, :], start=(k == 0), stop=(k == KT - 1))
                mm.then_inc(sem["h_mm"], 1)

            def base(n, par, h):
                if h == 0:
                    pe.wait_ge(sem["xtlo_ok"], n + 1)
                    if not isinstance(n, int) or n >= 2:
                        pe.wait_ge(sem["r3_ok"], n - 1)
                    elif n == 0:
                        pe.wait_ge(sem["r1_ok"], NT)
                    else:
                        pe.wait_ge(sem["t_ok"], NT)
                for k in range(KT):
                    if isinstance(n, int) and n == 0:
                        pe.wait_ge(sem["wb_lo_odd" if k % 2 else "wb_lo_even"], h * KT // 2 + k // 2 + 1)
                    split_mm(bank(2 * par + h), (x2T_hi[par][:, k, :], x2T_lo[par][:, k, :]),
                             (big_hi[:, k, h * 512:(h + 1) * 512], big_lo[:, k, h * 512:(h + 1) * 512]), k, -1)

            def transpose_hw(n):
                pe.wait_ge(sem["hw_ok"], n + 1)
                if not isinstance(n, int) or n >= 1:
                    pe.wait_ge(sem["hwtlo_ok"], n)
                    if isinstance(n, int) and n == 1:
                        pe.wait_ge(sem["kc_ok"], NT)
                else:
                    pe.wait_ge(sem["kc_ok"], NT - 1)
                nc.tensor.transpose(banks[5][:, 0:P], hw[:, :], ident[:, :]).then_inc(sem["hwt_mm"], 1)

            def experts(n, par):
                pe.wait_ge(sem["hwtlo_ok"], n + 1)
                if isinstance(n, int) and n == 0:
                    pe.wait_ge(sem["bt_ok"], 1)
                for h in range(2):
                    cols = slice(h * 512, (h + 1) * 512)
                    mm = split_mm(bank(2 * par + h), (hwT_hi[:, :], hwT_lo[:, :]), (bt_hi[:, cols], bt_lo[:, cols]), 0, 0, first=False)
                mm.then_inc(sem["c_mm"], 1)

            def last_step(n, par, i, more):
                hidden(n)
                base(n, par, 0)
                if more:
                    transpose_x2(n + 1, 1 - par, i + par)
                transpose_hw(n)
                if isinstance(n, int) and n == 0:
                    transpose_c1(NT - 1)
                base(n, par, 1)
                experts(n, par)
                if isinstance(n, int) and n == 0:
                    context_product(NT - 1, 1)

            transpose_x2(0, 0, 0)
            last_step(0, 0, 0, True)
            last_step(1, 1, 0, True)
            with pe.Fori(1, NT // 2 - 1) as i:
                last_step(2 * i, 0, i, True)
                last_step(2 * i + 1, 1, i, True)
            last_step(NT - 2, 0, NT // 2 - 1, True)
            last_step(NT - 1, 1, NT // 2 - 1, False)

        @block.scalar
        def _(act):
            def split_x(b):
                cols = slice(b * S, (b + 1) * S)
                for k in range(KT):
                    act.wait_ge(big_in[b][k], 16)
                    nc.scalar.activation(big_hi[:, k, cols], big_raw[:, k, cols], ACT.Identity).then_inc(sem["x_hi_ok"], 1)

            split_x(0)
            act.wait_ge(sem["const_in"], 16 * 5)

            def round_ow(k):
                act.wait_ge(big_in[0][k], 32)
                nc.scalar.activation(big_hi[:, k, :], big_raw[:, k, :], ACT.Identity).then_inc(sem["ow_hi"], 1)

            def step(s, par, g):
                proj, maxima, finish = stages(s)
                prev = not isinstance(s, int) or s >= 1
                for i in range(NS):
                    j, t = i // QT, i % QT
                    if finish:
                        act.wait_ge(sem["st_mm"], NS * (s - 2) + i + 1)
                        if t == 0 and (not isinstance(s, int) or s >= 3):
                            if j == 0:
                                act.wait_ge(sem["pv_mm"], s - 2)
                            act.wait_ge(sem["psum_ok"], HPG * (s - 3) + j + 1)
                        nc.scalar.activation(probs[:, j, t, :], bank(ST0 + i % 2), ACT.Exp, scale=SM_SCALE).then_inc(sem["exp_ok"], 1)
                    if proj and i in (4, 10):
                        piece = 0 if i == 4 else 1
                        wait_alone(act, sem["proj_done"], 3 * s + piece + 1)
                        if prev:
                            for h in range(HPG):
                                wait_alone(act, packed[h], PACK_INC * s)
                        nc.scalar.activation((q_hi, k_hi)[piece][:, :], bank(PROJ1 if piece == 0 else PROJ0), ACT.Identity,
                                             bias=bias[:, bass.ds(g, 1), piece:piece + 1].rearrange("p a b -> p (a b)")).then_inc(sem["hi_ok"], 1)
                    if isinstance(s, int) and s == UNITS and i % 2 and i >= 3:
                        round_ow((i - 3) // 2)
                    if isinstance(s, int) and s == UNITS + 1 and i == 8:
                        split_last_group(0)
                if isinstance(s, int) and s == UNITS:
                    round_ow(KT - 1)
                if isinstance(s, int) and s == 0:
                    split_x(1)
                if proj:
                    act.wait_ge(sem["proj_done"], 3 * s + 3)
                    if prev:
                        wait_alone(act, sem["vt_mm"], s)
                    nc.scalar.activation(vT[:, :], bank(PROJ1), ACT.Identity,
                                         bias=bias[:, bass.ds(g, 1), 2:3].rearrange("p a b -> p (a b)")).then_inc(sem["vT_ok"], 1)

            step(0, 0, 0)
            step(1, 1, 0)
            step(2, 0, 1)
            step(3, 1, 1)
            with act.Fori(2, G - 1) as g:
                step(2 * g, 0, g)
                step(2 * g + 1, 1, g)
            step(UNITS - 2, 0, G - 1)
            step(UNITS - 1, 1, G - 1)
            step(UNITS, 0, G)

            def split_first_tile(q):
                act.wait_ge(by_parity["a_in"][q], 16)
                nc.scalar.activation(cx_hi[q][:, 0:KT - 1].rearrange("p k c -> p (k c)"),
                                     cx_raw[:, q, 0:KT - 1].rearrange("p k c -> p (k c)"), ACT.Identity).then_inc(sem["cx_hi_ok"], 1)

            def split_last_group(q):
                act.wait_ge(sem["cx7_in"], 16 * (q + 1))
                nc.scalar.activation(cx_hi[q][:, KT - 1, :], cx_raw[:, q, KT - 1, :], ACT.Identity).then_inc(sem["cx7_hi"], 1)

            act.wait_ge(sem["st_mm"], NS * (UNITS - 1))
            split_first_tile(0)
            step(UNITS + 1, 1, G)

            def split_cx(n, par, i):
                act.wait_ge(by_parity["a_in"][par], 16 * (i + 1))
                if not isinstance(n, int) or n >= 2:
                    act.wait_ge(sem["a_mm"], n - 1)
                nc.scalar.activation(cx_hi[par][:].rearrange("p k c -> p (k c)"), cx_raw[:, par].rearrange("p k c -> p (k c)"), ACT.Identity).then_inc(sem["cx_hi_ok"], 1)

            def copy_c1T(m, q):
                act.wait_ge(sem["tr_mm"], m + 1)
                nc.scalar.activation(c1T[:, q].rearrange("p k c -> p (k c)"), banks[4][:, :].bitcast(bf16), ACT.Copy).then_inc(sem["c1T_ok"], 1)

            def scale_product(m, q):
                act.wait_ge(sem["b_mm"], m + 1)
                act.wait_ge(sem["kc_ok"], m + 1)
                for h in range(2):
                    last = nc.scalar.activation(qtmp[:, q, h * 512:(h + 1) * 512], bank(2 + h), ACT.Identity,
                                                scale=sc[:, 5:6], bias=kcol[:, 1:2])
                last.then_inc(sem["t_ok"], 1)

            def normalise(row, r, wait, done, n):
                act.wait_ge(sem[wait], n + 1)
                nc.scalar.activation(r, r, ACT.Identity, scale=mv[:, row, 2:3], bias=mv[:, row, 3:4]).then_inc(sem[done], 1)

            def round_wb(h, k):
                cols = slice(h * 512, (h + 1) * 512)
                nc.scalar.activation(big_hi[:, k, cols], wb_raw[:, k, cols], ACT.Identity).then_inc(sem["wb_hi"], 1)

            def copy_x2T(n, par):
                act.wait_ge(sem["xt_mm"], n + 1)
                if not isinstance(n, int) or n >= 1:
                    act.wait_ge(sem["h_mm"], n)
                    act.wait_ge(sem["xtlo_ok"], n)
                for h in range(2):
                    mm = nc.scalar.activation(x2T[:, 4 * h:4 * h + 4, :].rearrange("p k c -> p (k c)"), bank(6 + h), ACT.Copy)
                mm.then_inc(sem["xt_ok"], 1)

            def tail_step(n, par, i):
                prev = not isinstance(n, int) or n >= 1
                last = isinstance(n, int) and n == NT - 1
                if isinstance(n, int) and n == 0:
                    split_last_group(1)
                elif not last:
                    split_cx(n + 1, 1 - par, i + par)
                if prev:
                    copy_c1T(n - 1, 1 - par)
                if last:
                    act.wait_ge(sem["wb_in"], 16 * KT)
                    act.wait_ge(sem["a_half"], NT)
                    for k in range(KT):
                        round_wb(0, k)
                    act.wait_ge(sem["a_mm"], NT)
                    round_wb(1, 0)
                    round_wb(1, 1)
                if prev:
                    scale_product(n - 1, 1 - par)
                if last:
                    copy_x2T(0, 0)
                normalise(0, x1s[:, par, :], "nm1", "x1_ok", n)
                act.wait_ge(sem["x1_ok"], n + 1)
                nc.scalar.activation(qtmp[:, par, :], x1s[:, par, :], ACT.Identity, scale=sc[:, 4:5], bias=sc[:, 1:2]).then_inc(sem["qp1"], 1)
                if last:
                    for k in range(2, KT):
                        round_wb(1, k)
                if prev:
                    normalise(1, x1s[:, 1 - par, :], "nm2", "x2_ok", n - 1)

            act.wait_ge(sem["st_mm"], NS * UNITS)
            split_first_tile(1)
            tail_step(0, 0, 0)
            tail_step(1, 1, 0)
            with act.Fori(1, NT // 2 - 1) as i:
                tail_step(2 * i, 0, i)
                tail_step(2 * i + 1, 1, i)
            tail_step(NT - 2, 0, NT // 2 - 1)
            tail_step(NT - 1, 1, NT // 2 - 1)

            def last_step(n, par, more):
                act.wait_ge(sem["rv3"], n + 1)
                nc.scalar.activation(rt[:, 8:16], rt[:, 0:8], ACT.Exp, bias=rt[:, 16:17]).then_inc(sem["re_ok"], 1)
                if more:
                    copy_x2T(n + 1, 1 - par)
                if isinstance(n, int) and n == 0:
                    copy_c1T(NT - 1, 1)
                    scale_product(NT - 1, 1)
                    normalise(1, x1s[:, 1, :], "nm2", "x2_ok", NT - 1)
                act.wait_ge(sem["nm3"], n + 1)
                nc.scalar.activation(r3[:, par, :], r3[:, par, :], ACT.Identity, scale=mv[:, 0, 2:3], bias=mv[:, 0, 3:4]).then_inc(sem["o_ok"], 1)

            last_step(0, 0, True)
            last_step(1, 1, True)
            with act.Fori(1, NT // 2 - 1) as i:
                last_step(2 * i, 0, True)
                last_step(2 * i + 1, 1, True)
            last_step(NT - 2, 0, True)
            last_step(NT - 1, 1, False)

        @block.gpsimd
        def _(pool):
            def split_w(g_next, piece, done):
                if done is None:
                    pool.wait_ge(w_first[piece], 16)
                else:
                    pool.wait_ge(sem["w_in"], 16 * g_next)
                if done is not None:
                    wait_alone(pool, sem["proj_done"], done)
                nc.gpsimd.tensor_scalar(w_hi[:, piece], w_raw[:, piece], 1.0, 0.0, ALU.mult, ALU.add).then_inc(sem["w_hi_ok"], 1)
                pool.wait_ge(sem["w_hi_ok"], 3 * g_next + piece + 1)
                nc.gpsimd.tensor_tensor(w_lo[:, piece], w_raw[:, piece], w_hi[:, piece].bitcast(f32), ALU.subtract).then_inc(sem["w_split"], 1)

            split_w(0, 0, None)
            nc.gpsimd.memset(ident[:, :], 0.0).then_inc(sem["idb_ok"], 1)
            nc.gpsimd.memset(ones[:, :], 1.0).then_inc(sem["idb_ok"], 1)
            nc.gpsimd.memset(onesb[:, :], 1.0).then_inc(sem["idb_ok"], 1)
            nc.gpsimd.memset(consts[:, 0:1], -0.5).then_inc(sem["idb_ok"], 1)
            nc.gpsimd.iota(iota[:, :], [[1, NE]], channel_multiplier=0, allow_small_or_imprecise_dtypes=True).then_inc(sem["idb_ok"], 1)
            pool.wait_ge(sem["idb_ok"], 5)
            nc.gpsimd.affine_select(out=ident[:, :], in_=ident[:, :], compare_op=ALU.not_equal, fill=1.0,
                                    base=0, pattern=[[-1, P]], channel_multiplier=1).then_inc(sem["idb_ok"], 1)
            pool.wait_ge(sem["idb_ok"], 6)
            nc.gpsimd.tensor_copy(identb[:, :], ident[:, :]).then_inc(sem["const_ok"], 1)
            split_w(0, 1, None)
            split_w(0, 2, None)

            def add_keys(s, j):
                u = s - 2
                pool.wait_ge(sem["exp_ok"], NS * u + QT * (j + 1))
                if j == 0 and (not isinstance(s, int) or s >= 3):
                    pool.wait_ge(sem["l_mm"], s - 2)
                nc.gpsimd.tensor_tensor(psumk[:, j, :], probs[:, j, 0, :], probs[:, j, 1, :], ALU.add).then_inc(sem["pool_sum"], 1)
                pool.wait_ge(sem["pool_sum"], 2 * HPG * u + 2 * j + 1)
                nc.gpsimd.tensor_tensor(psumk[:, j, :], psumk[:, j, :], probs[:, j, 2, :], ALU.add).then_inc(sem["pool_sum"], 1)
                pool.wait_ge(sem["pool_sum"], 2 * HPG * u + 2 * j + 2)
                nc.gpsimd.tensor_tensor(psumk[:, j, :], psumk[:, j, :], probs[:, j, 3, :], ALU.add).then_inc(sem["psum_ok"], 1)

            def step(s, par, g):
                proj, maxima, finish = stages(s)
                split = proj and par == 1 and (not isinstance(s, int) or s < UNITS - 1)
                if proj:
                    wait_alone(pool, sem["ctxq_in"], 16 * (s + 1))
                    if isinstance(s, int) and s == 0:
                        pool.wait_ge(sem["sc_ok"], 3)
                    nc.gpsimd.tensor_scalar(c_raw[:, :], c_raw[:, :], sc[:, 6:7], sc[:, 3:4], ALU.mult, ALU.add).then_inc(sem["ctxq_1"], 1)
                if finish:
                    add_keys(s, 0)
                if split:
                    split_w(g + 1, 0, 3 * s + 1)
                if finish:
                    add_keys(s, 1)
                    add_keys(s, 2)
                    add_keys(s, 3)
                if split:
                    split_w(g + 1, 1, 3 * s + 2)
                    split_w(g + 1, 2, 3 * s + 3)

            steps_of(pool, step)

            def residual(par, i):
                pool.wait_ge(by_parity["xr_in"][par], 16 * (i + 1))
                nc.gpsimd.tensor_tensor(xres[:, par, :], xres[:, par, :], ob_sb[:, :], ALU.add).then_inc(sem["xr_ok"], 1)

            def rstd(ve, ok, n, row):
                pool.wait_ge(sem[ve], n)
                nc.gpsimd.tensor_tensor(mv[:, row, 2:3], mv[:, row, 1:2], consts[:, 0:1], ALU.pow).then_inc(sem[ok], 1)

            def split_wb(h, k):
                cols = slice(h * 512, (h + 1) * 512)
                pool.wait_ge(sem["wb_hi"], h * KT + k + 1)
                nc.gpsimd.tensor_tensor(big_lo[:, k, cols], wb_raw[:, k, cols], big_hi[:, k, cols].bitcast(f32), ALU.subtract).then_inc(sem["wb_lo_odd"], 1)

            def tail_step(n, par, i):
                more = not isinstance(n, int) or n < NT
                prev = not isinstance(n, int) or n >= 1
                if more:
                    if isinstance(n, int) and n == 0:
                        pool.wait_ge(sem["const_w"], 16)
                    residual(par, i)
                last = isinstance(n, int) and n == NT - 1
                if prev:
                    q = 1 - par
                    if isinstance(n, int) and n == 1:
                        pool.wait_ge(sem["corr_ok"], NB)
                    pool.wait_ge(sem["qp1"], n)
                    nc.gpsimd.tensor_tensor(x1s[:, q, :], x1s[:, q, :], corr[:, q, :], ALU.add).then_inc(sem["x1c_ok"], 1)
                if last:
                    split_wb(0, 1)
                    split_wb(0, 3)
                if more:
                    rstd("ve1", "rstd1", n + 1, 0)
                if last:
                    split_wb(0, 5)
                    split_wb(0, 7)
                    split_wb(1, 1)
                if prev:
                    rstd("ve2", "rstd2", n, 1)
                if last:
                    for k in range(3, KT, 2):
                        split_wb(1, k)

            tail_step(0, 0, 0)
            tail_step(1, 1, 0)
            with pool.Fori(1, NT // 2 - 1) as i:
                tail_step(2 * i, 0, i)
                tail_step(2 * i + 1, 1, i)
            tail_step(NT - 2, 0, NT // 2 - 1)
            tail_step(NT - 1, 1, NT // 2 - 1)

            def last_step(n, par, i):
                pool.wait_ge(by_parity["x2_in"][par], 16 * (i + 1))
                if not isinstance(n, int) or n >= 2:
                    pool.wait_ge(sem["r3_ok"], n - 1)
                nc.gpsimd.tensor_tensor(xb[:, par, :], x2s[:, par, :], bb_sb[:, :], ALU.add).then_inc(sem["xb_ok"], 1)
                if isinstance(n, int) and n == 0:
                    tail_step(NT, 0, NT // 2)
                rstd("ve3", "rstd3", n + 1, 0)

            pool.wait_ge(sem["bt_in"], 32)
            last_step(0, 0, 0)
            last_step(1, 1, 0)
            with pool.Fori(1, NT // 2) as i:
                last_step(2 * i, 0, i)
                last_step(2 * i + 1, 1, i)

        @block.vector
        def _(dve):
            nc.vector.memset(kp[SHIFT:SHIFT + 2, :, :, :].bitcast(f32), -1.0).then_inc(sem["minus_ok"], 1)
            dve.wait_ge(sem["const_in"], 16 * 5)
            nc.vector.reciprocal(sc[:, 4:5], sc[:, 0:1])
            nc.vector.reciprocal(sc[:, 6:7], sc[:, 2:3])
            nc.vector.tensor_scalar(sc[:, 5:6], sc[:, 0:1], sc[:, 2:3], None, ALU.mult)
            nc.vector.tensor_scalar(sc[:, 7:8], sc[:, 1:2], 0.0, QMAX, ALU.max, ALU.min)
            nc.vector.tensor_scalar(sc[:, 8:9], sc[:, 3:4], 0.0, QMAX, ALU.max, ALU.min).then_inc(sem["sc_ok"], 1)
            dve.wait_ge(sem["sc_ok"], 1)
            nc.vector.tensor_scalar(sc[:, 7:9], sc[:, 7:9], MAGIC, -MAGIC, ALU.add, ALU.add).then_inc(sem["sc_ok"], 1)
            dve.wait_ge(sem["sc_ok"], 2)
            nc.vector.tensor_tensor(sc[:, 9:10], sc[:, 7:8], sc[:, 1:2], ALU.subtract)
            nc.vector.tensor_tensor(sc[:, 10:11], sc[:, 8:9], sc[:, 3:4], ALU.subtract).then_inc(sem["sc_ok"], 1)
            dve.wait_ge(sem["sc_ok"], 3)
            for n in range(2):
                last = nc.vector.tensor_scalar(consts[:, 1 + n:2 + n], sc[:, 7 + n:8 + n], MAGIC, None, ALU.add)
            last.then_inc(sem["sc_ok"], 1)
            dve.wait_ge(sem["sc_ok"], 4)

            def split_x(b):
                cols = slice(b * S, (b + 1) * S)
                for k in range(KT):
                    dve.wait_ge(sem["x_hi_ok"], b * KT + k + 1)
                    nc.vector.tensor_tensor(big_lo[:, k, cols], big_raw[:, k, cols], big_hi[:, k, cols].bitcast(f32), ALU.subtract).then_inc(sem["x_lo_ok"], 1)

            split_x(0)

            def divide(u):
                dve.wait_ge(sem["l_mm"], u + 1)
                nc.vector.reciprocal(recip[:, :], bank(LSUM)).then_inc(sem["recip_ok"], 1)
                dve.wait_ge(sem["recip_ok"], u + 1)
                if not isinstance(u, int) or u >= 1:
                    dve.wait_ge(sem["ctx_out"], 16 * u)
                nc.vector.tensor_tensor(ctxs[:, :], bank(CTX), recip[:, :], ALU.mult).then_inc(sem["ctx_ok"], 1)

            def step(s, par, g):
                proj, maxima, finish = stages(s)

                def low(piece):
                    dve.wait_ge(sem["hi_ok"], 2 * s + piece + 1)
                    hi, lo = ((q_hi, q_lo), (k_hi, k_lo))[piece]
                    nc.vector.scalar_tensor_tensor(lo[:, :], bank(PROJ1 if piece == 0 else PROJ0),
                                                   bias[:, bass.ds(g, 1), piece:piece + 1].rearrange("p a b -> p (a b)"),
                                                   hi[:, :].bitcast(f32), ALU.add, ALU.subtract).then_inc(sem["lo_ok"], 1)

                def clip_context():
                    dve.wait_ge(sem["ctxq_1"], s + 1)
                    if not isinstance(s, int) or s >= 1:
                        dve.wait_ge(sem["c2_out"], 16 * s)
                    nc.vector.tensor_scalar(c_raw[:, :], c_raw[:, :], 0.0, QMAX, ALU.max, ALU.min).then_inc(sem["ctxq_2"], 1)

                def round_context():
                    dve.wait_ge(sem["ctxq_2"], s + 1)
                    nc.vector.tensor_scalar(c_q[:, :], c_raw[:, :], MAGIC, consts[:, 2:3], ALU.add, ALU.subtract).then_inc(sem["ctxq_ok"], 1)

                if maxima:
                    dve.wait_ge(sem["vt_mm"], s)
                    if not isinstance(s, int) or s >= 3:
                        dve.wait_ge(sem["pv_mm"], s - 2)
                    nc.vector.tensor_copy(v_nat[:, 1 - par].rearrange("p t c -> p (t c)"), bank(PROJ0)).then_inc(sem["v_ok"], 1)
                if divides(s) and proj:
                    divide(s - 3)
                for n in range(NS):
                    if not proj and n == 2:
                        divide(s - 3)
                    if maxima:
                        dve.wait_ge(sem["max_mm"], NS * (s - 1) + n + 1)
                        if n == 0 and (not isinstance(s, int) or s >= 2):
                            dve.wait_ge(sem["m_mm"], s - 1)
                        nc.vector.reduce_max(m_col[:, n:n + 1], bank(MAX0 + n % 2), AX).then_inc(sem["rowmax"], 1)
                    if proj and n in (3, 10):
                        low(0 if n == 3 else 1)
                    if proj and n == 6:
                        clip_context()
                    if proj and n == 12:
                        round_context()
                if isinstance(s, int) and s == 0:
                    split_x(1)
                if maxima:
                    dve.wait_ge(sem["m_mm"], s)
                    if not isinstance(s, int) or s >= 2:
                        dve.wait_ge(sem["shift_in"], 32 * (s - 1))
                    nc.vector.tensor_copy(m_row[:, 0, :], banks[LSUM][0:NS, 0:P]).then_inc(sem["m_hi_ok"], 1)
                    dve.wait_ge(sem["m_hi_ok"], s)
                    nc.vector.tensor_tensor(m_row[:, 1, :], banks[LSUM][0:NS, 0:P], m_row[:, 0, :].bitcast(f32), ALU.subtract).then_inc(sem["m_ok"], 1)

            step(0, 0, 0)
            step(1, 1, 0)
            step(2, 0, 1)
            step(3, 1, 1)
            with dve.Fori(2, G - 1) as g:
                step(2 * g, 0, g)
                step(2 * g + 1, 1, g)
            step(UNITS - 2, 0, G - 1)
            step(UNITS - 1, 1, G - 1)
            step(UNITS, 0, G)

            def column_correction(b):
                dve.wait_ge(sem["cs_mm"], b + 1)
                for h in range(2):
                    last = nc.vector.tensor_scalar(corr[:, b, h * 512:(h + 1) * 512], bank(2 - 2 * b + h), sc[:, 9:10], sc[:, 5:6], ALU.mult, ALU.mult)
                last.then_inc(sem["corr_ok"], 1)

            def split_ow(k):
                dve.wait_ge(sem["ow_hi"], k + 1)
                nc.vector.tensor_tensor(big_lo[:, k, :], big_raw[:, k, :], big_hi[:, k, :].bitcast(f32), ALU.subtract).then_inc(sem["ow_lo"], 1)

            def split_first_tile(q):
                dve.wait_ge(sem["cx_hi_ok"], q + 1)
                nc.vector.tensor_tensor(cx_lo[q][:, 0:KT - 1], cx_raw[:, q, 0:KT - 1], cx_hi[q][:, 0:KT - 1].bitcast(f32), ALU.subtract).then_inc(sem["cx_lo_ok"], 1)

            def split_last_group(q):
                dve.wait_ge(sem["cx7_hi"], q + 1)
                nc.vector.tensor_tensor(cx_lo[q][:, KT - 1, :], cx_raw[:, q, KT - 1, :], cx_hi[q][:, KT - 1, :].bitcast(f32), ALU.subtract).then_inc(sem["cx7_lo"], 1)

            column_correction(0)
            divide(UNITS - 2)
            for k in range(KT // 2):
                split_ow(k)
            split_first_tile(0)
            split_last_group(0)
            column_correction(1)
            for k in range(KT // 2, KT):
                split_ow(k)
            split_first_tile(1)
            divide(UNITS - 1)
            split_last_group(1)

            def split_cx(n, par):
                dve.wait_ge(sem["cx_hi_ok"], n + 1)
                nc.vector.tensor_tensor(cx_lo[par][:, :], cx_raw[:, par], cx_hi[par][:, :].bitcast(f32), ALU.subtract).then_inc(sem["cx_lo_ok"], 1)

            def stats(r, row, n, a, b, c):
                for h in range(2):
                    last = nc.vector.bn_stats(st[:, row, h, :], r[:, h * 512:(h + 1) * 512])
                last.then_inc(sem[a], 1)
                wait_alone(dve, sem[a], n)
                nc.vector.bn_aggr(mv[:, row, 0:2], st[:, row].rearrange("p a b -> p (a b)")).then_inc(sem[b], 1)
                dve.wait_ge(sem[b], n)
                nc.vector.tensor_scalar(mv[:, row, 1:2], mv[:, row, 1:2], EPS, None, ALU.add).then_inc(sem[c], 1)

            def minus_mean(row, n, ok, done):
                dve.wait_ge(sem[ok], n)
                nc.vector.tensor_scalar(mv[:, row, 3:4], mv[:, row, 0:1], mv[:, row, 2:3], -1.0, ALU.mult, ALU.mult).then_inc(sem[done], 1)

            def row_correction(m):
                dve.wait_ge(sem["rs_mm"], m + 1)
                nc.vector.tensor_scalar(kcol[:, 0:1], banks[5][:, 0:1], sc[:, 10:11], sc[:, 11:12], ALU.mult, ALU.add).then_inc(sem["k1"], 1)
                dve.wait_ge(sem["k1"], m + 1)
                nc.vector.tensor_scalar(kcol[:, 1:2], kcol[:, 0:1], sc[:, 5:6], None, ALU.mult).then_inc(sem["kc_ok"], 1)

            def add_product(m, q):
                dve.wait_ge(sem["t_ok"], m + 1)
                dve.wait_ge(sem["x1c_ok"], m + 1)
                nc.vector.tensor_tensor(x1s[:, q, :], x1s[:, q, :], qtmp[:, q, :], ALU.add).then_inc(sem["r2_ok"], 1)

            def product_stats(m, q):
                dve.wait_ge(sem["r2_ok"], m + 1)
                stats(x1s[:, q, :], 1, m + 1, "st2", "mv2", "ve2")

            def split_wb(h, k):
                cols = slice(h * 512, (h + 1) * 512)
                dve.wait_ge(sem["wb_hi"], h * KT + k + 1)
                nc.vector.tensor_tensor(big_lo[:, k, cols], wb_raw[:, k, cols], big_hi[:, k, cols].bitcast(f32), ALU.subtract).then_inc(sem["wb_lo_even"], 1)

            def split_x2T(n, par):
                dve.wait_ge(sem["xt_ok"], n + 1)
                if not isinstance(n, int) or n >= 2:
                    dve.wait_ge(sem["c_mm"], n - 1)
                nc.vector.tensor_copy(x2T_hi[par][:].rearrange("p k c -> p (k c)"), x2T[:].rearrange("p k c -> p (k c)")).then_inc(sem["xthi_ok"], 1)
                dve.wait_ge(sem["xthi_ok"], n + 1)
                nc.vector.tensor_tensor(x2T_lo[par][:, :, :], x2T[:, :, :], x2T_hi[par][:, :, :].bitcast(f32), ALU.subtract).then_inc(sem["xtlo_ok"], 1)

            def tail_step(n, par, i):
                prev = not isinstance(n, int) or n >= 1
                last = isinstance(n, int) and n == NT - 1
                q = 1 - par
                if not last and (not isinstance(n, int) or n >= 1):
                    split_cx(n + 1, q)
                dve.wait_ge(sem["a_mm"], n + 1)
                dve.wait_ge(sem["xr_ok"], n + 1)
                if not isinstance(n, int) or n >= 2:
                    dve.wait_ge(by_parity["x2_out"][par], 16 * i)
                for h in range(2):
                    cols = slice(h * 512, (h + 1) * 512)
                    add = nc.vector.tensor_tensor(x1s[:, par, cols], bank(h), xres[:, par, cols], ALU.add)
                add.then_inc(sem["r1_ok"], 1)
                dve.wait_ge(sem["r1_ok"], n + 1)
                stats(x1s[:, par, :], 0, n + 1, "st1", "mv1", "ve1")
                if prev and last:
                    row_correction(n - 1)
                    split_wb(0, 0)
                minus_mean(0, n + 1, "rstd1", "nm1")
                if last:
                    for k in range(2, KT, 2):
                        split_wb(0, k)
                    split_x2T(0, 0)
                elif prev:
                    row_correction(n - 1)
                if prev:
                    add_product(n - 1, q)
                    product_stats(n - 1, q)
                dve.wait_ge(sem["qp1"], n + 1)
                nc.vector.tensor_scalar(qtmp[:, par, :], qtmp[:, par, :], 0.0, QMAX, ALU.max, ALU.min).then_inc(sem["qp2"], 1)
                dve.wait_ge(sem["qp2"], n + 1)
                if prev:
                    dve.wait_ge(sem["tr_mm"], n)
                else:
                    dve.wait_ge(sem["ctx_out"], 16 * UNITS)
                nc.vector.tensor_scalar(c1[:, :], qtmp[:, par, :], MAGIC, consts[:, 1:2], ALU.add, ALU.subtract).then_inc(sem["c1_ok"], 1)
                if prev:
                    minus_mean(1, n, "rstd2", "nm2")

            nc.vector.tensor_scalar(sc[:, 11:12], sc[:, 9:10], sc[:, 10:11], float(H), ALU.mult, ALU.mult).then_inc(sem["sc_ok"], 1)
            dve.wait_ge(sem["sc_ok"], 5)

            tail_step(0, 0, 0)
            tail_step(1, 1, 0)
            with dve.Fori(1, NT // 2 - 1) as i:
                tail_step(2 * i, 0, i)
                tail_step(2 * i + 1, 1, i)
            tail_step(NT - 2, 0, NT // 2 - 1)
            tail_step(NT - 1, 1, NT // 2 - 1)
            for k in range(0, KT, 2):
                split_wb(1, k)

            def route(n):
                logits = banks[4][:, ER:ER + NE]
                wait_alone(dve, sem["h_mm"], n + 1)
                nc.vector.max(rt[:, 0:8], logits).then_inc(sem["rv1"], 1)
                wait_alone(dve, sem["rv1"], n + 1)
                nc.vector.max_index(ridx[:, :], rt[:, 0:8], logits).then_inc(sem["rv2"], 1)
                nc.vector.tensor_scalar(rt[:, 16:17], rt[:, 0:1], -1.0, None, ALU.mult).then_inc(sem["rv3"], 1)
                dve.wait_ge(sem["rv2"], n + 1)
                nc.vector.tensor_copy(rt[:, 21:23], ridx[:, 0:2]).then_inc(sem["rw1"], 1)
                dve.wait_ge(sem["re_ok"], n + 1)
                nc.vector.tensor_tensor(rt[:, 17:18], rt[:, 8:9], rt[:, 9:10], ALU.add).then_inc(sem["rw2"], 1)
                dve.wait_ge(sem["rw2"], n + 1)
                nc.vector.reciprocal(rt[:, 18:19], rt[:, 17:18]).then_inc(sem["rw3"], 1)
                dve.wait_ge(sem["rw3"], n + 1)
                nc.vector.tensor_scalar(rt[:, 19:21], rt[:, 8:10], rt[:, 18:19], SCALING, ALU.mult, ALU.mult).then_inc(sem["rw4"], 1)
                dve.wait_ge(sem["rw4"], n + 1)
                dve.wait_ge(sem["rw1"], n + 1)
                for e in range(2):
                    last = nc.vector.tensor_scalar(rt[:, 24 + 8 * e:32 + 8 * e], iota[:, :], rt[:, 21 + e:22 + e], rt[:, 19 + e:20 + e],
                                                   ALU.is_equal, ALU.mult)
                last.then_inc(sem["rw5"], 1)
                dve.wait_ge(sem["rw5"], n + 1)
                nc.vector.tensor_tensor(rt[:, 24:32], rt[:, 24:32], rt[:, 32:40], ALU.add).then_inc(sem["comb_ok"], 1)
                dve.wait_ge(sem["comb_ok"], n + 1)
                if not isinstance(n, int) or n >= 1:
                    dve.wait_ge(sem["hwt_mm"], n)
                nc.vector.tensor_tensor(hw[:, :].rearrange("p (e r) -> p e r", r=R), banks[4][:, 0:ER].rearrange("p (e r) -> p e r", r=R),
                                        rt[:, 24:32].unsqueeze(2).to_broadcast([P, NE, R]), ALU.mult).then_inc(sem["hw_ok"], 1)
                dve.wait_ge(sem["hwt_mm"], n + 1)
                if not isinstance(n, int) or n >= 1:
                    dve.wait_ge(sem["c_mm"], n)
                nc.vector.tensor_copy(hwT_hi[:, :], banks[5][:, 0:P]).then_inc(sem["hwthi_ok"], 1)
                dve.wait_ge(sem["hwthi_ok"], n + 1)
                nc.vector.tensor_tensor(hwT_lo[:, :], banks[5][:, 0:P], hwT_hi[:, :].bitcast(f32), ALU.subtract).then_inc(sem["hwtlo_ok"], 1)

            def last_step(n, par, i, more):
                route(n)
                if more:
                    split_x2T(n + 1, 1 - par)
                if isinstance(n, int) and n == 0:
                    row_correction(NT - 1)
                    add_product(NT - 1, 1)
                    product_stats(NT - 1, 1)
                    minus_mean(1, NT, "rstd2", "nm2")
                dve.wait_ge(sem["c_mm"], n + 1)
                dve.wait_ge(sem["xb_ok"], n + 1)
                if not isinstance(n, int) or n >= 2:
                    dve.wait_ge(by_parity["o_out"][par], 16 * i)
                for h in range(2):
                    cols = slice(h * 512, (h + 1) * 512)
                    last = nc.vector.tensor_tensor(r3[:, par, cols], bank(2 * par + h), xb[:, par, cols], ALU.add)
                last.then_inc(sem["r3_ok"], 1)
                dve.wait_ge(sem["r3_ok"], n + 1)
                if not isinstance(n, int) or n >= 1:
                    dve.wait_ge(sem["o_ok"], n)
                stats(r3[:, par, :], 0, n + 1, "st3", "mv3", "ve3")
                minus_mean(0, n + 1, "rstd3", "nm3")

            dve.wait_ge(sem["bt_in"], 32)
            nc.vector.tensor_copy(bt_hi[:, :], bt_raw[:, :]).then_inc(sem["bt_hi_ok"], 1)
            dve.wait_ge(sem["bt_hi_ok"], 1)
            nc.vector.tensor_tensor(bt_lo[:, :], bt_raw[:, :], bt_hi[:, :].bitcast(f32), ALU.subtract).then_inc(sem["bt_ok"], 1)
            last_step(0, 0, 0, True)
            last_step(1, 1, 0, True)
            with dve.Fori(1, NT // 2 - 1) as i:
                last_step(2 * i, 0, i, True)
                last_step(2 * i + 1, 1, i, True)
            last_step(NT - 2, 0, NT // 2 - 1, True)
            last_step(NT - 1, 1, NT // 2 - 1, False)


def kernel(x, ctx_4096, L0_attn_attn_qkvw, L0_attn_attn_qkvb, L0_attn_attn_ow, L0_attn_attn_ob,
           L0_xattn_x1_scale, L0_xattn_x1_zp, L0_xattn_x2_scale, L0_xattn_x2_zp,
           L0_ffn_W_base, L0_ffn_b_base, L0_ffn_W_router, L0_ffn_A, L0_ffn_B):
    import numpy as np
    import concourse.bacc as bacc
    from concourse.bass_utils import run_bass_kernel_spmd

    P = 128
    B, S, H = x.shape
    G = H // P
    c = np.ascontiguousarray
    x2d = np.asarray(x).reshape(B * S, H)
    arrays = {
        "xT": c(x2d.T),
        "x": c(x2d),
        "wqkv": c(np.asarray(L0_attn_attn_qkvw).reshape(G, P, 3, G, P).transpose(3, 1, 2, 0, 4)),
        "qkvb": c(np.asarray(L0_attn_attn_qkvb).reshape(3, G, P).transpose(2, 1, 0)),
        "ow": c(L0_attn_attn_ow),
        "ob": c(L0_attn_attn_ob),
        "ctx": c(ctx_4096),
        "scales": c(np.stack([np.asarray(a).reshape(1) for a in (L0_xattn_x1_scale, L0_xattn_x1_zp, L0_xattn_x2_scale, L0_xattn_x2_zp)])),
        "wbT": c(np.asarray(L0_ffn_W_base).T),
        "bb": c(L0_ffn_b_base),
    }
    E, R, _ = L0_ffn_A.shape
    ar = np.concatenate([np.asarray(L0_ffn_A).reshape(E * R, H), np.asarray(L0_ffn_W_router)], axis=0)
    arrays["art"] = c(ar.T.reshape(G, P, E * R + E).transpose(1, 0, 2))
    arrays["bt"] = c(np.asarray(L0_ffn_B).transpose(0, 2, 1).reshape(E * R, H))

    nc = bacc.Bacc("TRN2", target_bir_lowering=False, num_devices=1)
    aps = [nc.dram_tensor(f"in_{n}", a.shape, mybir.dt.from_np(a.dtype), kind="ExternalInput").ap() for n, a in arrays.items()]
    out = nc.dram_tensor("out", (B * S, H), mybir.dt.float32, kind="ExternalOutput").ap()
    decoder_layer(nc, *aps, out)
    r = run_bass_kernel_spmd(nc, [{f"in_{n}": a for n, a in arrays.items()}], core_ids=[0])
    return r.results[0]["out"].reshape(B, S, H)
```

```python
import concourse.bass as bass
from concourse import mybir
from concourse.alu_op_type import AluOpType as ALU
from contextlib import ExitStack


def decoder_layer(nc, xT, x, wqkv, qkvb, ow, ob, ctx_in, scales, wbT, bb, art, bt, out):
    f32, f32r, bf16, u32 = mybir.dt.float32, mybir.dt.float32r, mybir.dt.bfloat16, mybir.dt.uint32
    ACT = mybir.ActivationFunctionType
    AX = mybir.AxisListType.X

    P = 128
    H = x.shape[1]
    TOK = x.shape[0]
    NB = ctx_in.shape[0]
    S = TOK // NB
    KT = H // P
    HD = 32
    HPG = P // HD
    G = H // P
    QT = S // P
    NS = HPG * QT
    UNITS = G * NB
    SM_SCALE = float(HD) ** -0.5
    NE = 8
    ER = art.shape[2] - NE
    R = ER // NE
    SCALING = 32.0 / R
    EPS = 1e-5
    QMAX = 255.0
    MAGIC = 1.5 * 2.0 ** 23
    PACK_HI2, PACK_LO, SHIFT = HD, 2 * HD, 3 * HD
    NT = TOK // P
    PACK_INC = 6 * 16

    es = ExitStack()
    with es:
        KB = 1024
        base = 16512

        def at(name, off, shape, dt):
            return nc.alloc_sbuf_tensor_at(name, shape, dt, offset=base + int(off * KB))

        big_hi = at("big_hi", 0, [P, KT, H], f32r)
        big_lo = at("big_lo", 32, [P, KT, H], f32r)
        big_raw = at("big_raw", 32, [P, KT, H], f32)
        w_hi = at("w_hi", 64, [P, 3, KT, P], f32r)
        w_lo = at("w_lo", 76, [P, 3, KT, P], f32r)
        w_raw = at("w_raw", 88, [P, 3, KT, P], f32)
        q_hi = at("q_hi", 100, [P, S], f32r)
        q_lo = at("q_lo", 102, [P, S], f32r)
        k_hi = at("k_hi", 104, [P, S], f32r)
        k_lo = at("k_lo", 106, [P, S], f32r)
        qp = at("qp", 108, [P, 2, HPG, S], f32r)
        kp = at("kp", 124, [P, 2, HPG, S], f32r)
        probs = at("probs", 140, [P, HPG, QT, S], f32)
        v_nat = at("v_nat", 172, [P, 2, QT, P], f32)
        vT = at("vT", 176, [P, S], f32)
        psumk = at("psumk", 178, [P, HPG, S], f32)
        recip = at("recip", 186, [P, S], f32)
        ctxs = at("ctxs", 188, [P, S], f32)
        ident = at("ident", 190, [P, P], f32)
        identb = at("identb", 190.5, [P, P], bf16)
        m_row = at("m_row", 190.75, [NS, 2, P], f32r)
        ones = at("ones", 191.75, [P, HD], f32)
        bias = at("bias", 191.875, [P, G, 3], f32)
        c_raw = at("c_raw", 192, [P, H], f32)
        ob_sb = at("ob_sb", 200, [P, H], f32)
        c_q = at("c_q", 204, [P, H], bf16)
        m_col = at("m_col", 206, [P, NS], f32)
        sc = at("sc", 206.0625, [P, 12], f32)
        consts = at("consts", 206.125, [P, 4], f32)
        onesb = at("onesb", 206.15625, [P, P], bf16)
        iota = at("iota", 206.40625, [P, NE], f32)
        st = at("st", 206.4375, [P, 2, 2, 6], f32)
        mv = at("mv", 206.53125, [P, 2, 4], f32)
        kcol = at("kcol", 206.5625, [P, 2], f32)
        rt = at("rt", 206.59375, [P, 40], f32)
        ridx = at("ridx", 206.75, [P, NE], u32)
        c2 = at("c2", 64, [P, NB, KT, H], bf16)
        c1T = at("c1T", 96, [P, 2, KT, P], bf16)
        cx_hi = [at(f"cx_hi{q}", 108 + 8 * q, [P, KT, P], f32r) for q in range(2)]
        cx_lo = [at(f"cx_lo{q}", 112 + 8 * q, [P, KT, P], f32r) for q in range(2)]
        corr = at("corr", 124, [P, NB, H], f32)
        cx_raw = at("cx_raw", 100, [P, 2, KT, P], f32)
        qtmp = at("qtmp", 132, [P, 2, H], f32)
        wb_raw = at("wb_raw", 140, [P, KT, H], f32)
        x1s = at("x1s", 172, [P, 2, H], f32)
        xres = at("xres", 180, [P, 2, H], f32)
        c1 = at("c1", 188, [P, H], bf16)
        x2T = at("x2T", 64, [P, KT, P], f32)
        x2T_hi = [at(f"x2T_hi{q}", 68 + 4 * q, [P, KT, P], f32r) for q in range(2)]
        x2T_lo = [at(f"x2T_lo{q}", off, [P, KT, P], f32r) for q, off in enumerate((76, 104))]
        art_sb = at("art_sb", 108, [P, KT, ER + NE], f32)
        bt_hi = at("bt_hi", 112.25, [P, H], f32r)
        bt_lo = at("bt_lo", 116.25, [P, H], f32r)
        hw = at("hw", 120.5, [P, ER], f32)
        hwT_hi = at("hwT_hi", 121, [P, P], f32r)
        hwT_lo = at("hwT_lo", 121.5, [P, P], f32r)
        r3 = at("r3", 124, [P, 2, H], f32)
        bt_raw = at("bt_raw", 100, [P, H], f32)
        xb = at("xb", 180, [P, 2, H], f32)
        x2s = at("x2s", 192, [P, 2, H], f32)
        bb_sb = at("bb_sb", 200, [P, H], f32)

        banks = [es.enter_context(nc.psum_tensor(f"bank{i}", [P, 512], f32)) for i in range(8)]
        PROJ0, PROJ1, MAX0, ST0, CTX, LSUM = 0, 1, 2, 4, 6, 7

        def rows_bank(s):
            return PROJ1 if isinstance(s, int) and s == UNITS else LSUM

        def context_bank(u):
            return PROJ0 if isinstance(u, int) and u == UNITS - 2 else CTX

        ctx_d = nc.dram_tensor("ctx_scratch", [H, TOK], f32).ap()
        c2_d = nc.dram_tensor("c2_scratch", [NB * KT, P, H], bf16).ap()
        x2_d = nc.dram_tensor("x2_scratch", [TOK, H], f32).ap()
        ctx_v = ctx_d.rearrange("(k p) t -> p k t", p=P)
        ctx_tiles = ctx_in.rearrange("b (k p) n -> (b k) p n", p=P)

        names = """x_hi_ok x_lo_ok wq_hi wq_lo const_in w_in w_hi_ok w_split proj_done hi_ok lo_ok vT_ok vt_mm v_ok
        max_mm rowmax m_mm m_hi_ok m_ok shift_in st_mm exp_ok pool_sum psum_ok pv_mm l_mm recip_ok ctx_ok
        ctx_out const_ok idb_ok ctxq_in ctxq_1 ctxq_2 ctxq_ok c2_out ow_hi ow_lo wb_in const_w
        cs_mm corr_ok sc_ok
        cx_hi_ok cx_lo_ok cx7_in cx7_hi cx7_lo xr_ok a_half a_mm r1_half r1_ok st1 mv1 ve1 rstd1 nm1 x1_ok qp1 qp2 c1_ok tr_mm c1T_ok
        rs_mm b_mm k1 kc_ok x1c_ok t_ok r2_ok st2 mv2 ve2 rstd2 nm2 x2_ok
        bt_in bt_hi_ok bt_ok art_in wb_hi wb_lo_even wb_lo_odd xt_mm xt_ok xthi_ok xtlo_ok h_mm rv1 rv2 rv3 re_ok
        rw1 rw2 rw3 rw4 rw5 comb_ok hw_ok hwt_mm hwthi_ok hwtlo_ok c_mm c_half xb_ok r3_ok st3 mv3 ve3 rstd3 nm3
        o_ok o_first o_second r3_half passed minus_ok""".split()
        sem = {n: es.enter_context(nc.semaphore(n)) for n in names}
        big_in = [[es.enter_context(nc.semaphore(f"big_in{b}_{k}")) for k in range(KT)] for b in range(NB)]
        c2_in = [es.enter_context(nc.semaphore(f"c2_in{b}")) for b in range(NB)]
        wq_in = [es.enter_context(nc.semaphore(f"wq_in{half}")) for half in range(2)]
        w_first = [es.enter_context(nc.semaphore(f"w_first{n}")) for n in (1, 2)]
        by_parity = {n: [es.enter_context(nc.semaphore(f"{n}_{q}")) for q in range(2)]
                     for n in ("a_in", "xr_in", "x2_in", "x2_out", "o_out")}
        packed = [es.enter_context(nc.semaphore(f"packed{j}")) for j in range(HPG)]
        block = es.enter_context(nc.Block())

        def steps_of(eng, step):
            step(0, 0, 0)
            step(1, 1, 0)
            step(2, 0, 1)
            step(3, 1, 1)
            with eng.Fori(2, G - 1) as g:
                step(2 * g, 0, g)
                step(2 * g + 1, 1, g)
            for s in range(UNITS - 2, UNITS + 2):
                step(s, s % 2, s // 2)

        def stages(s):
            if not isinstance(s, int):
                return True, True, True
            return s < UNITS, 1 <= s <= UNITS, s >= 2

        def divides(s):
            return not isinstance(s, int) or s >= 3

        def wait_alone(eng, semaphore, value):
            eng.wait_ge(semaphore, value)
            eng.sem_inc(sem["passed"], 1)

        def bank(i, lo=0, hi=512):
            return banks[i][:, lo:hi]

        @block.sync
        def _(sp):
            def load_x(b, k):
                sp.dma_start(big_raw[:, k, b * S:(b + 1) * S], xT[k * P:(k + 1) * P, b * S:(b + 1) * S]).then_inc(big_in[b][k], 16)

            wq_v = wqkv.rearrange("g p a k c -> g p (a k c)")
            for half in range(2):
                ks = slice(half * KT // 2, (half + 1) * KT // 2)
                sp.dma_start(w_raw[:, 0, ks], wqkv[0, :, 0, ks]).then_inc(wq_in[half], 16)
                if half == 0:
                    load_x(0, 0)
            for k in range(1, KT):
                load_x(0, k)
            sp.dma_start(bias[:, :, :], qkvb).then_inc(sem["const_in"], 16)
            for n in (1, 2):
                sp.dma_start(w_raw[:, n], wqkv[0, :, n]).then_inc(w_first[n - 1], 16)
            for n in range(4):
                sp.dma_start(sc[:, n:n + 1], scales[n].rearrange("(a n) -> a n", a=1).to_broadcast([P, 1])).then_inc(sem["const_in"], 16)
            for k in range(KT):
                load_x(1, k)
            sp.dma_start(ob_sb[:, :], ob.rearrange("(a n) -> a n", a=1).to_broadcast([P, H])).then_inc(sem["const_w"], 16)

            def pack(s, par, j, which):
                rows = slice(j * HD, (j + 1) * HD)
                if which == "q":
                    parts = ((qp, 0, q_hi), (qp, PACK_HI2, q_lo), (qp, PACK_LO, q_hi))
                else:
                    parts = ((kp, 0, k_hi), (kp, PACK_HI2, k_hi), (kp, PACK_LO, k_lo))
                if not isinstance(s, int) or s >= 2:
                    sp.wait_ge(sem["st_mm"], NS * (s - 2) + QT * (j + 1))
                for dst, row, src in parts:
                    sp.dma_start(dst[row:row + HD, par, j, :].bitcast(f32), src[rows, :].bitcast(f32)).then_inc(packed[j], 16)

            def load_ow(h, projected):
                sp.wait_ge(sem["proj_done"], projected)
                for k in range(KT):
                    sp.dma_start(big_raw[:, k, h * S:(h + 1) * S], ow[k * P:(k + 1) * P, h * S:(h + 1) * S]).then_inc(big_in[h][k], 16)

            def load_c2(b):
                sp.wait_ge(sem["c2_out"], 16 * KT * (b + 1))
                sp.dma_start(c2[:, b], c2_d[b * KT:(b + 1) * KT].rearrange("k p n -> p k n")).then_inc(c2_in[b], 16)

            def store_context(u, q, gu):
                wait_alone(sp, sem["ctx_ok"], u + 1)
                sp.dma_start(ctx_d[bass.ds(gu * P, P), q * S:(q + 1) * S], ctxs[:, :]).then_inc(sem["ctx_out"], 16)

            def step(s, par, g):
                proj, maxima, finish = stages(s)
                if proj:
                    if not isinstance(s, int) or s >= 1:
                        wait_alone(sp, sem["ctxq_ok"], s)
                    sp.dma_start(c_raw[:, :], ctx_tiles[bass.ds(s, 1)].rearrange("a p n -> (a p) n")).then_inc(sem["ctxq_in"], 16)
                if proj and par == 0 and (not isinstance(s, int) or s < UNITS - 2):
                    if isinstance(s, int) and s == 0:
                        sp.wait_ge(sem["wq_lo"], 2)
                    wait_alone(sp, sem["w_split"], 3 * (g + 1) - 1)
                    sp.dma_start(w_raw[:].rearrange("p a k c -> p (a k c)"), wq_v[bass.ds(g + 1, 1)].rearrange("a p n -> (a p) n")).then_inc(sem["w_in"], 16)
                if isinstance(s, int) and s == UNITS - 1:
                    load_ow(0, 3 * s)
                if divides(s) and (not isinstance(s, int) or s < UNITS):
                    store_context(s - 3, 1 - par, g - 2 + par)
                if proj:
                    sp.wait_ge(sem["lo_ok"], 2 * s + 1)
                    early = range(HPG if isinstance(s, int) and s < 2 else 2)
                    for j in early:
                        pack(s, par, j, "q")
                    sp.wait_ge(sem["lo_ok"], 2 * s + 2)
                    pack(s, par, 0, "k")
                    pack(s, par, 1, "k")
                    if 2 not in early:
                        pack(s, par, 2, "q")
                if maxima:
                    sp.wait_ge(sem["m_ok"], s)
                    for half in range(2):
                        sp.dma_start(qp[SHIFT + half:SHIFT + half + 1, 1 - par, :, :].rearrange("a j (t q) -> a (j t) q", q=P).bitcast(f32),
                                     m_row[:, half, :].bitcast(f32)).then_inc(sem["shift_in"], 16)
                if isinstance(s, int) and s == UNITS - 1:
                    sp.wait_ge(sem["proj_done"], 3 * UNITS)
                    load_c2(0)
                if proj:
                    pack(s, par, 2, "k")
                    if 3 not in early:
                        pack(s, par, 3, "q")
                    pack(s, par, 3, "k")
                if proj:
                    wait_alone(sp, sem["ctxq_ok"], s + 1)
                    sp.dma_start(c2_d[bass.ds(s, 1)].rearrange("a p n -> (a p) n"), c_q[:, :]).then_inc(sem["c2_out"], 16)

            step(0, 0, 0)
            step(1, 1, 0)
            step(2, 0, 1)
            step(3, 1, 1)
            with sp.Fori(2, G - 1) as g:
                step(2 * g, 0, g)
                step(2 * g + 1, 1, g)
            step(UNITS - 2, 0, G - 1)
            step(UNITS - 1, 1, G - 1)
            step(UNITS, 0, G)

            def load_tile(n, par, i):
                if not isinstance(n, int) or n >= 2:
                    wait_alone(sp, sem["cx_lo_ok"], n - 1)
                sp.dma_start(cx_raw[:, par], ctx_v[:, :, bass.ds(par * S + i * P, P)]).then_inc(by_parity["a_in"][par], 16)

            def load_residual(n, par, i):
                if not isinstance(n, int) or n >= 2:
                    wait_alone(sp, sem["r1_ok"], n - 1)
                sp.dma_start(xres[:, par, :], x[bass.ds(par * S + i * P, P), :]).then_inc(by_parity["xr_in"][par], 16)

            def store_x2(m, par, i):
                wait_alone(sp, sem["x2_ok"], m + 1)
                sp.dma_start(x2_d[bass.ds(par * S + i * P, P), :], qtmp[:, par, :]).then_inc(by_parity["x2_out"][par], 16)

            def load_first_tile(q):
                sp.dma_start(cx_raw[:, q, 0:KT - 1], ctx_v[:, 0:KT - 1, q * S:q * S + P]).then_inc(by_parity["a_in"][q], 16)

            def load_last_group(q):
                sp.wait_ge(sem["ctx_ok"], UNITS - 1 + q)
                sp.dma_start(cx_raw[:, q, KT - 1, :], ctxs[:, 0:P]).then_inc(sem["cx7_in"], 16)

            for j in range(HPG):
                sp.wait_ge(packed[j], PACK_INC * UNITS)
            sp.wait_ge(sem["ctx_out"], 16 * (UNITS - 3))
            load_first_tile(0)
            load_c2(1)
            store_context(UNITS - 3, 1, G - 2)
            load_last_group(0)
            store_context(UNITS - 2, 0, G - 1)
            load_ow(1, 3 * UNITS)
            sp.wait_ge(sem["ctx_out"], 16 * (UNITS - 2))
            load_first_tile(1)
            sp.wait_ge(sem["l_mm"], UNITS)
            load_residual(0, 0, 0)
            load_last_group(1)
            store_context(UNITS - 1, 1, G - 1)
            load_residual(1, 1, 0)
            sp.wait_ge(sem["ctx_out"], 16 * UNITS)
            sp.wait_ge(sem["cx7_lo"], 1)
            load_tile(2, 0, 1)

            def load_wb(k):
                sp.dma_start(wb_raw[:, bass.ds(k, 1), :].rearrange("p a n -> p (a n)"), wbT[bass.ds(k * P, P), :]).then_inc(sem["wb_in"], 16)

            load_wb(0)
            load_wb(1)
            load_residual(2, 0, 1)
            sp.wait_ge(sem["cx7_lo"], 2)
            with sp.Fori(1, NT // 2 - 1) as i:
                load_tile(2 * i + 1, 1, i)
                load_wb(3 * i - 1)
                load_wb(3 * i)
                load_residual(2 * i + 1, 1, i)
                store_x2(2 * i - 2, 0, i - 1)
                load_tile(2 * i + 2, 0, i + 1)
                load_wb(3 * i + 1)
                load_residual(2 * i + 2, 0, i + 1)
                store_x2(2 * i - 1, 1, i - 1)
            load_tile(NT - 1, 1, NT // 2 - 1)
            load_residual(NT - 1, 1, NT // 2 - 1)

            def load_x2(n, par, i):
                if not isinstance(n, int) or n >= 2:
                    sp.wait_ge(sem["xb_ok"], n - 1)
                    wait_alone(sp, sem["xt_mm"], n - 1)
                sp.dma_start(x2s[:, par, :], x2_d[bass.ds(par * S + i * P, P), :]).then_inc(by_parity["x2_in"][par], 16)

            for q in range(2):
                sp.wait_ge(by_parity["x2_out"][q], 16)
                load_x2(q, q, 0)
            store_x2(NT - 4, 0, NT // 2 - 2)
            sp.wait_ge(sem["cx_lo_ok"], NT)
            sp.dma_start(bt_raw[:, :], bt).then_inc(sem["bt_in"], 16)
            sp.wait_ge(sem["xr_ok"], NT)
            sp.dma_start(bb_sb[:, :], bb.rearrange("(a n) -> a n", a=1).to_broadcast([P, H])).then_inc(sem["bt_in"], 16)
            store_x2(NT - 3, 1, NT // 2 - 2)
            sp.wait_ge(sem["a_mm"], NT)
            sp.dma_start(art_sb[:, :, :], art).then_inc(sem["art_in"], 16)
            store_x2(NT - 2, 0, NT // 2 - 1)

            def store(n, par, i):
                wait_alone(sp, sem["o_ok"], n + 1)
                sp.dma_start(out[bass.ds(par * S + i * P, P), :], r3[:, par, :]).then_inc(by_parity["o_out"][par], 16)

            sp.wait_ge(by_parity["x2_out"][0], 32)
            load_x2(2, 0, 1)
            store_x2(NT - 1, 1, NT // 2 - 1)
            sp.wait_ge(by_parity["x2_out"][1], 32)
            store(0, 0, 0)
            load_x2(3, 1, 1)
            store(1, 1, 0)
            for q in range(2):
                sp.wait_ge(by_parity["x2_out"][q], 16 * NT // 2)
            with sp.Fori(2, NT // 2) as i:
                load_x2(2 * i, 0, i)
                store(2 * i - 2, 0, i - 1)
                load_x2(2 * i + 1, 1, i)
                store(2 * i - 1, 1, i - 1)
            store(NT - 2, 0, NT // 2 - 1)
            for half, done in ((1, "o_second"), (0, "o_first")):
                cols = slice(half * 512, (half + 1) * 512)
                sp.wait_ge(sem[done], 1)
                sp.dma_start(out[(NB * S - P):NB * S, cols], r3[:, 1, cols]).then_inc(by_parity["o_out"][1], 16)
            for q in range(2):
                sp.wait_ge(by_parity["o_out"][q], 16 * NT // 2 + 16 * q)

        @block.tensor
        def _(pe):
            def split_mm(dst, lhs, rhs, k, last_k, first=None):
                for n, (a, b) in enumerate(((0, 0), (0, 1), (1, 0))):
                    mm = nc.tensor.matmul(dst, lhs[a], rhs[b], start=(k == 0 and n == 0) if first is None else False,
                                          stop=(k == last_k and n == 2))
                return mm

            def row_sums(u):
                pe.wait_ge(sem["psum_ok"], HPG * (u + 1))
                if not isinstance(u, int) or u + 2 <= UNITS:
                    pe.wait_ge(sem["m_ok"], u + 2)
                if isinstance(u, int) and u >= UNITS - 2:
                    pe.wait_ge(sem["recip_ok"], u)
                for j in range(HPG):
                    mm = nc.tensor.matmul(banks[LSUM][j * HD:(j + 1) * HD, :], ones[:, :], psumk[:, j, :],
                                          start=True, stop=True, skip_group_check=True)
                mm.then_inc(sem["l_mm"], 1)

            def step(s, par, g):
                proj, maxima, finish = stages(s)
                first = isinstance(s, int) and s == 0
                cols = slice(par * S, (par + 1) * S)

                def transpose_v():
                    pe.wait_ge(sem["vT_ok"], s)
                    pe.wait_ge(sem["lo_ok"], 2 * s)
                    if isinstance(s, int) and s == 1:
                        pe.wait_ge(sem["const_ok"], 1)
                    for t in range(QT):
                        mm = nc.tensor.transpose(bank(PROJ0, t * P, (t + 1) * P), vT[:, t * P:(t + 1) * P], ident[:, :])
                    mm.then_inc(sem["vt_mm"], 1)

                def project(n):
                    piece, k = n // KT, n % KT
                    dst = bank(PROJ1 if piece != 1 else PROJ0)
                    if first and piece == 0 and k in (0, KT // 2):
                        pe.wait_ge(sem["wq_lo"], 1 + 2 * k // KT)
                    elif k == 0:
                        pe.wait_ge(sem["w_split"], 3 * g + piece)
                        if piece == 0 and not first:
                            pe.wait_ge(sem["vT_ok"], s)
                        if piece == 1 and not first:
                            pe.wait_ge(sem["v_ok"], s)
                        if piece == 2:
                            pe.wait_ge(sem["lo_ok"], 2 * s + 1)
                    if isinstance(s, int) and s < NB and piece == 0:
                        pe.wait_ge(sem["x_lo_ok"], s * KT + k + 1)
                    mm = split_mm(dst, (w_hi[:, piece, k, :], w_lo[:, piece, k, :]),
                                  (big_hi[:, k, cols], big_lo[:, k, cols]), k, KT - 1)
                    if k == KT - 1:
                        mm.then_inc(sem["proj_done"], 1)

                def score(n):
                    j, t = n // QT, n % QT
                    if t == 0:
                        pe.wait_ge(packed[j], PACK_INC * s)
                    if n >= 2:
                        pe.wait_ge(sem["rowmax"], NS * (s - 1) + n - 1)
                    nc.tensor.matmul(bank(MAX0 + n % 2), qp[0:SHIFT, 1 - par, j, t * P:(t + 1) * P],
                                     kp[0:SHIFT, 1 - par, j, :], start=True, stop=True).then_inc(sem["max_mm"], 1)

                def maxima_to_rows():
                    pe.wait_ge(sem["rowmax"], NS * s)
                    if not isinstance(s, int) or 3 <= s < UNITS:
                        pe.wait_ge(sem["recip_ok"], s - 2)
                    nc.tensor.transpose(banks[rows_bank(s)][0:NS, 0:P], m_col[:, :], ident[:, :]).then_inc(sem["m_mm"], 1)

                def score_t(n):
                    j, t = n // QT, n % QT
                    if n == 0:
                        pe.wait_ge(sem["shift_in"], 32 * (s - 1))
                        if isinstance(s, int) and s == 2:
                            pe.wait_ge(sem["minus_ok"], 1)
                    if n >= 2:
                        pe.wait_ge(sem["exp_ok"], NS * (s - 2) + n - 1)
                    nc.tensor.matmul(bank(ST0 + n % 2), kp[0:SHIFT + 2, par, j, t * P:(t + 1) * P],
                                     qp[0:SHIFT + 2, par, j, :], start=True, stop=True).then_inc(sem["st_mm"], 1)

                def context():
                    pe.wait_ge(sem["v_ok"], s - 1)
                    if isinstance(s, int) and s == UNITS:
                        pe.wait_ge(sem["v_ok"], s)
                    elif divides(s):
                        pe.wait_ge(sem["ctx_ok"], s - 2)
                    for t in range(QT):
                        pe.wait_ge(sem["exp_ok"], NS * (s - 1) - QT + t + 1)
                        for j in range(HPG):
                            mm = nc.tensor.matmul(banks[context_bank(s - 2)][j * HD:(j + 1) * HD, :], v_nat[:, par, t, j * HD:(j + 1) * HD],
                                                  probs[:, j, t, :], start=(t == 0), stop=(t == QT - 1), skip_group_check=True)
                    mm.then_inc(sem["pv_mm"], 1)

                def last_steps():
                    sums = 0
                    for n in range(NS):
                        if maxima:
                            score(n)
                            if n == 1:
                                row_sums(s - 3)
                        score_t(n)
                        if not maxima:
                            if n == 4:
                                row_sums(s - 3)
                            until = (n + 1) * 8 // 5 if n < 10 else 2 * KT + (n - 9) * 2 * KT // 6
                            while sums < until:
                                if sums % (2 * KT) == 0:
                                    pe.wait_ge(c2_in[sums // (2 * KT)], 16)
                                if sums == 2 * KT:
                                    pe.wait_ge(sem["ctx_ok"], UNITS - 1)
                                column_sums(sums // (2 * KT), sums % (2 * KT))
                                sums += 1
                    if maxima:
                        maxima_to_rows()
                    context()

                if maxima:
                    transpose_v()
                if not proj:
                    last_steps()
                    return
                done = 0
                for q in range(3 * NS):
                    if proj and q % 2 == 0:
                        project(q // 2)
                    if maxima and done < NS and 15 * (q - FIRST_SCORE) >= 32 * done:
                        score(done)
                        done += 1
                    if maxima and q == 3 * NS - 3:
                        maxima_to_rows()
                    if finish and q % 3 == 2:
                        score_t(q // 3)
                    if divides(s) and q == 4:
                        row_sums(s - 3)
                if finish:
                    context()

            def column_sums(b, n):
                h, k = n // KT, n % KT
                mm = nc.tensor.matmul(bank(2 - 2 * b + h), onesb[:, :], c2[:, b, k, h * 512:(h + 1) * 512],
                                      start=(k == 0), stop=(k == KT - 1))
                if n == 2 * KT - 1:
                    mm.then_inc(sem["cs_mm"], 1)

            FIRST_SCORE = 11
            steps_of(pe, step)

            def out_project(n, par, h):
                if h == 0:
                    pe.wait_ge(sem["cx_lo_ok"], n + 1)
                    if not isinstance(n, int) or n >= 1:
                        pe.wait_ge(sem["r1_half"], n)
                    else:
                        pe.wait_ge(sem["corr_ok"], NB)
                elif not isinstance(n, int) or n >= 1:
                    pe.wait_ge(sem["r1_ok"], n)
                for k in range(KT):
                    if isinstance(n, int) and n < 2 and h == 0 and k == KT - 1:
                        pe.wait_ge(sem["cx7_lo"], n + 1)
                    if isinstance(n, int) and n == 0:
                        pe.wait_ge(sem["ow_lo"], h * KT + k + 1)
                    if isinstance(n, int) and n == 0 and h == 0 and k == 5:
                        row_sums(UNITS - 1)
                    if h and k == KT // 2 and (not isinstance(n, int) or n >= 1):
                        transpose_c1(n - 1)
                    mm = split_mm(bank(h), (cx_hi[par][:, k, :], cx_lo[par][:, k, :]),
                                  (big_hi[:, k, h * 512:(h + 1) * 512], big_lo[:, k, h * 512:(h + 1) * 512]), k, KT - 1)
                mm.then_inc(sem["a_mm" if h else "a_half"], 1)

            def transpose_c1(m):
                pe.wait_ge(sem["c1_ok"], m + 1)
                if not isinstance(m, int) or m >= 1:
                    pe.wait_ge(sem["c1T_ok"], m)
                c1p = banks[4][:, :].bitcast(bf16)
                for k in range(KT):
                    mm = nc.tensor.transpose(c1p[:, k * P:(k + 1) * P], c1[:, k * P:(k + 1) * P], identb[:, :])
                mm.then_inc(sem["tr_mm"], 1)

            def context_product(m, par):
                pe.wait_ge(sem["c1T_ok"], m + 1)
                if not isinstance(m, int) or m >= 1:
                    pe.wait_ge(sem["k1"], m)
                    pe.wait_ge(sem["t_ok"], m)
                for k in range(KT):
                    mm = nc.tensor.matmul(banks[5][:, 0:2], c1T[:, par, k, :], onesb[:, 0:2], start=(k == 0), stop=(k == KT - 1))
                mm.then_inc(sem["rs_mm"], 1)
                for h in range(2):
                    for k in range(KT):
                        mm = nc.tensor.matmul(bank(2 + h), c1T[:, par, k, :], c2[:, par, k, h * 512:(h + 1) * 512],
                                              start=(k == 0), stop=(k == KT - 1))
                mm.then_inc(sem["b_mm"], 1)

            def tail_step(n, par):
                out_project(n, par, 0)
                out_project(n, par, 1)
                if not isinstance(n, int) or n >= 1:
                    context_product(n - 1, 1 - par)

            tail_step(0, 0)
            tail_step(1, 1)
            with pe.Fori(1, NT // 2) as i:
                tail_step(2 * i, 0)
                tail_step(2 * i + 1, 1)

            def transpose_x2(n, par, i):
                pe.wait_ge(by_parity["x2_in"][par], 16 * (i + 1))
                if not isinstance(n, int) or n >= 1:
                    pe.wait_ge(sem["xt_ok"], n)
                for k in range(KT):
                    mm = nc.tensor.transpose(bank(6 + k // 4, (k % 4) * P, (k % 4 + 1) * P), x2s[:, par, k * P:(k + 1) * P], ident[:, :])
                mm.then_inc(sem["xt_mm"], 1)

            def hidden(n):
                pe.wait_ge(sem["xt_ok"], n + 1)
                if isinstance(n, int) and n == 0:
                    pe.wait_ge(sem["art_in"], 16)
                    pe.wait_ge(sem["c1T_ok"], NT - 1)
                else:
                    pe.wait_ge(sem["hw_ok"], n)
                for k in range(KT):
                    mm = nc.tensor.matmul(banks[4][:, 0:ER + NE], x2T[:, k, :], art_sb[:, k, :], start=(k == 0), stop=(k == KT - 1))
                mm.then_inc(sem["h_mm"], 1)

            def base(n, par, h, more=True):
                if h == 0:
                    pe.wait_ge(sem["xtlo_ok"], n + 1)
                    if not isinstance(n, int) or n >= 2:
                        pe.wait_ge(sem["r3_ok"], n - 1)
                    elif n == 0:
                        pe.wait_ge(sem["r1_ok"], NT)
                    else:
                        pe.wait_ge(sem["t_ok"], NT)
                for k in range(KT):
                    if not more and k == 2:
                        experts(n, par, (0,))
                    if isinstance(n, int) and n == 0:
                        pe.wait_ge(sem["wb_lo_odd" if k % 2 else "wb_lo_even"], h * KT // 2 + k // 2 + 1)
                    split_mm(bank(2 * par + h), (x2T_hi[par][:, k, :], x2T_lo[par][:, k, :]),
                             (big_hi[:, k, h * 512:(h + 1) * 512], big_lo[:, k, h * 512:(h + 1) * 512]), k, -1)

            def transpose_hw(n):
                pe.wait_ge(sem["hw_ok"], n + 1)
                if not isinstance(n, int) or n >= 1:
                    pe.wait_ge(sem["hwtlo_ok"], n)
                    if isinstance(n, int) and n == 1:
                        pe.wait_ge(sem["kc_ok"], NT)
                else:
                    pe.wait_ge(sem["kc_ok"], NT - 1)
                nc.tensor.transpose(banks[5][:, 0:P], hw[:, :], ident[:, :]).then_inc(sem["hwt_mm"], 1)

            def experts(n, par, halves=(0, 1)):
                pe.wait_ge(sem["hwtlo_ok"], n + 1)
                if isinstance(n, int) and n == 0:
                    pe.wait_ge(sem["bt_ok"], 1)
                for h in halves:
                    cols = slice(h * 512, (h + 1) * 512)
                    mm = split_mm(bank(2 * par + h), (hwT_hi[:, :], hwT_lo[:, :]), (bt_hi[:, cols], bt_lo[:, cols]), 0, 0, first=False)
                mm.then_inc(sem["c_mm" if h else "c_half"], 1)

            def last_step(n, par, i, more):
                hidden(n)
                base(n, par, 0)
                if more:
                    transpose_x2(n + 1, 1 - par, i + par)
                transpose_hw(n)
                if isinstance(n, int) and n == 0:
                    transpose_c1(NT - 1)
                base(n, par, 1, more)
                experts(n, par, (0, 1) if more else (1,))
                if isinstance(n, int) and n == 0:
                    context_product(NT - 1, 1)

            transpose_x2(0, 0, 0)
            last_step(0, 0, 0, True)
            last_step(1, 1, 0, True)
            with pe.Fori(1, NT // 2 - 1) as i:
                last_step(2 * i, 0, i, True)
                last_step(2 * i + 1, 1, i, True)
            last_step(NT - 2, 0, NT // 2 - 1, True)
            last_step(NT - 1, 1, NT // 2 - 1, False)

        @block.scalar
        def _(act):
            def split_x(b, ks):
                cols = slice(b * S, (b + 1) * S)
                for k in ks:
                    act.wait_ge(big_in[b][k], 16)
                    nc.scalar.activation(big_hi[:, k, cols], big_raw[:, k, cols], ACT.Identity).then_inc(sem["x_hi_ok"], 1)

            split_x(0, range(KT))
            act.wait_ge(sem["const_in"], 16 * 5)

            def round_ow(h, k):
                cols = slice(h * S, (h + 1) * S)
                act.wait_ge(big_in[h][k], 32)
                nc.scalar.activation(big_hi[:, k, cols], big_raw[:, k, cols], ACT.Identity).then_inc(sem["ow_hi"], 1)

            def step(s, par, g):
                proj, maxima, finish = stages(s)
                prev = not isinstance(s, int) or s >= 1
                for i in range(NS):
                    j, t = i // QT, i % QT
                    if finish:
                        act.wait_ge(sem["st_mm"], NS * (s - 2) + i + 1)
                        if t == 0 and (not isinstance(s, int) or s >= 3):
                            if j == 0:
                                act.wait_ge(sem["pv_mm"], s - 2)
                            act.wait_ge(sem["psum_ok"], HPG * (s - 3) + j + 1)
                        nc.scalar.activation(probs[:, j, t, :], bank(ST0 + i % 2), ACT.Exp, scale=SM_SCALE).then_inc(sem["exp_ok"], 1)
                    if proj and i in (4, 10):
                        piece = 0 if i == 4 else 1
                        wait_alone(act, sem["proj_done"], 3 * s + piece + 1)
                        if prev:
                            for h in range(HPG):
                                wait_alone(act, packed[h], PACK_INC * s)
                        nc.scalar.activation((q_hi, k_hi)[piece][:, :], bank(PROJ1 if piece == 0 else PROJ0), ACT.Identity,
                                             bias=bias[:, bass.ds(g, 1), piece:piece + 1].rearrange("p a b -> p (a b)")).then_inc(sem["hi_ok"], 1)
                    if isinstance(s, int) and s == 0 and i in (4, 10):
                        split_x(1, range(5) if i == 4 else range(5, KT))
                    if isinstance(s, int) and s == UNITS - 1 and i >= NS - KT:
                        round_ow(0, i - (NS - KT))
                    if isinstance(s, int) and s == UNITS + 1 and i == 6:
                        split_first_tile(0)
                    if isinstance(s, int) and s == UNITS + 1 and i == 12:
                        split_last_group(0)
                if proj:
                    act.wait_ge(sem["proj_done"], 3 * s + 3)
                    if prev:
                        wait_alone(act, sem["vt_mm"], s)
                    nc.scalar.activation(vT[:, :], bank(PROJ1), ACT.Identity,
                                         bias=bias[:, bass.ds(g, 1), 2:3].rearrange("p a b -> p (a b)")).then_inc(sem["vT_ok"], 1)

            step(0, 0, 0)
            step(1, 1, 0)
            step(2, 0, 1)
            step(3, 1, 1)
            with act.Fori(2, G - 1) as g:
                step(2 * g, 0, g)
                step(2 * g + 1, 1, g)
            step(UNITS - 2, 0, G - 1)
            step(UNITS - 1, 1, G - 1)
            step(UNITS, 0, G)

            def split_first_tile(q):
                act.wait_ge(sem["st_mm"], NS * (UNITS - 1 + q))
                act.wait_ge(by_parity["a_in"][q], 16)
                nc.scalar.activation(cx_hi[q][:, 0:KT - 1].rearrange("p k c -> p (k c)"),
                                     cx_raw[:, q, 0:KT - 1].rearrange("p k c -> p (k c)"), ACT.Identity).then_inc(sem["cx_hi_ok"], 1)

            def split_last_group(q):
                act.wait_ge(sem["cx7_in"], 16 * (q + 1))
                nc.scalar.activation(cx_hi[q][:, KT - 1, :], cx_raw[:, q, KT - 1, :], ACT.Identity).then_inc(sem["cx7_hi"], 1)

            step(UNITS + 1, 1, G)

            def split_cx(n, par, i):
                act.wait_ge(by_parity["a_in"][par], 16 * (i + 1))
                if not isinstance(n, int) or n >= 2:
                    act.wait_ge(sem["a_mm"], n - 1)
                nc.scalar.activation(cx_hi[par][:].rearrange("p k c -> p (k c)"), cx_raw[:, par].rearrange("p k c -> p (k c)"), ACT.Identity).then_inc(sem["cx_hi_ok"], 1)

            def copy_c1T(m, q):
                act.wait_ge(sem["tr_mm"], m + 1)
                nc.scalar.activation(c1T[:, q].rearrange("p k c -> p (k c)"), banks[4][:, :].bitcast(bf16), ACT.Copy).then_inc(sem["c1T_ok"], 1)

            def scale_product(m, q):
                act.wait_ge(sem["b_mm"], m + 1)
                act.wait_ge(sem["kc_ok"], m + 1)
                for h in range(2):
                    last = nc.scalar.activation(qtmp[:, q, h * 512:(h + 1) * 512], bank(2 + h), ACT.Identity,
                                                scale=sc[:, 5:6], bias=kcol[:, 1:2])
                last.then_inc(sem["t_ok"], 1)

            def normalise(row, dst, r, wait, done, n):
                act.wait_ge(sem[wait], n + 1)
                nc.scalar.activation(dst, r, ACT.Identity, scale=mv[:, row, 2:3], bias=mv[:, row, 3:4]).then_inc(sem[done], 1)

            def round_wb(h, k):
                cols = slice(h * 512, (h + 1) * 512)
                nc.scalar.activation(big_hi[:, k, cols], wb_raw[:, k, cols], ACT.Identity).then_inc(sem["wb_hi"], 1)

            def copy_x2T(n, par):
                act.wait_ge(sem["xt_mm"], n + 1)
                if not isinstance(n, int) or n >= 1:
                    act.wait_ge(sem["h_mm"], n)
                    act.wait_ge(sem["xtlo_ok"], n)
                for h in range(2):
                    mm = nc.scalar.activation(x2T[:, 4 * h:4 * h + 4, :].rearrange("p k c -> p (k c)"), bank(6 + h), ACT.Copy)
                mm.then_inc(sem["xt_ok"], 1)

            def exp_logits(n):
                act.wait_ge(sem["rv3"], n + 1)
                nc.scalar.activation(rt[:, 8:16], rt[:, 0:8], ACT.Exp, bias=rt[:, 16:17]).then_inc(sem["re_ok"], 1)

            def tail_step(n, par, i):
                prev = not isinstance(n, int) or n >= 1
                last = isinstance(n, int) and n == NT - 1
                if isinstance(n, int) and n == 0:
                    split_last_group(1)
                elif not last:
                    split_cx(n + 1, 1 - par, i + par)
                if prev:
                    copy_c1T(n - 1, 1 - par)
                if last:
                    act.wait_ge(sem["wb_in"], 16 * KT)
                    act.wait_ge(sem["a_half"], NT)
                    for k in range(KT):
                        round_wb(0, k)
                    act.wait_ge(sem["a_mm"], NT)
                    round_wb(1, 0)
                    round_wb(1, 1)
                if last:
                    copy_x2T(0, 0)
                if prev:
                    scale_product(n - 1, 1 - par)
                normalise(0, x1s[:, par, :], x1s[:, par, :], "nm1", "x1_ok", n)
                act.wait_ge(sem["x1_ok"], n + 1)
                if not isinstance(n, int) or n >= 2:
                    act.wait_ge(by_parity["x2_out"][par], 16 * i)
                nc.scalar.activation(qtmp[:, par, :], x1s[:, par, :], ACT.Identity, scale=sc[:, 4:5], bias=sc[:, 1:2]).then_inc(sem["qp1"], 1)
                if last:
                    for k in range(2, KT):
                        round_wb(1, k)
                if last:
                    exp_logits(0)
                if prev:
                    normalise(1, qtmp[:, 1 - par, :], x1s[:, 1 - par, :], "nm2", "x2_ok", n - 1)

            for k in range(KT):
                round_ow(1, k)
            split_first_tile(1)
            tail_step(0, 0, 0)
            tail_step(1, 1, 0)
            with act.Fori(1, NT // 2 - 1) as i:
                tail_step(2 * i, 0, i)
                tail_step(2 * i + 1, 1, i)
            tail_step(NT - 2, 0, NT // 2 - 1)
            tail_step(NT - 1, 1, NT // 2 - 1)

            def last_step(n, par, more):
                if not isinstance(n, int) or n >= 2:
                    exp_logits(n)
                if more:
                    copy_x2T(n + 1, 1 - par)
                if isinstance(n, int) and n == 0:
                    copy_c1T(NT - 1, 1)
                    scale_product(NT - 1, 1)
                    exp_logits(1)
                    normalise(1, qtmp[:, 1, :], x1s[:, 1, :], "nm2", "x2_ok", NT - 1)
                act.wait_ge(sem["nm3"], n + 1)
                if not more:
                    nc.scalar.activation(r3[:, par, 0:512], r3[:, par, 0:512], ACT.Identity, scale=mv[:, 0, 2:3], bias=mv[:, 0, 3:4]).then_inc(sem["o_first"], 1)
                    return
                nc.scalar.activation(r3[:, par, :], r3[:, par, :], ACT.Identity, scale=mv[:, 0, 2:3], bias=mv[:, 0, 3:4]).then_inc(sem["o_ok"], 1)

            last_step(0, 0, True)
            last_step(1, 1, True)
            with act.Fori(1, NT // 2 - 1) as i:
                last_step(2 * i, 0, True)
                last_step(2 * i + 1, 1, True)
            last_step(NT - 2, 0, True)
            last_step(NT - 1, 1, False)

        @block.gpsimd
        def _(pool):
            def split_w(g_next, piece, done):
                if done is None:
                    pool.wait_ge(w_first[piece - 1], 16)
                else:
                    pool.wait_ge(sem["w_in"], 16 * g_next)
                if done is not None:
                    wait_alone(pool, sem["proj_done"], done)
                nc.gpsimd.tensor_scalar(w_hi[:, piece], w_raw[:, piece], 1.0, 0.0, ALU.mult, ALU.add).then_inc(sem["w_hi_ok"], 1)
                pool.wait_ge(sem["w_hi_ok"], 3 * g_next + piece)
                nc.gpsimd.tensor_tensor(w_lo[:, piece], w_raw[:, piece], w_hi[:, piece].bitcast(f32), ALU.subtract).then_inc(sem["w_split"], 1)

            for half in range(2):
                ks = slice(half * KT // 2, (half + 1) * KT // 2)
                pool.wait_ge(wq_in[half], 16)
                nc.gpsimd.tensor_scalar(w_hi[:, 0, ks], w_raw[:, 0, ks], 1.0, 0.0, ALU.mult, ALU.add).then_inc(sem["wq_hi"], 1)
            nc.gpsimd.memset(ident[:, :], 0.0).then_inc(sem["idb_ok"], 1)
            nc.gpsimd.memset(ones[:, :], 1.0).then_inc(sem["idb_ok"], 1)
            nc.gpsimd.memset(onesb[:, :], 1.0).then_inc(sem["idb_ok"], 1)
            nc.gpsimd.memset(consts[:, 0:1], -0.5).then_inc(sem["idb_ok"], 1)
            nc.gpsimd.iota(iota[:, :], [[1, NE]], channel_multiplier=0, allow_small_or_imprecise_dtypes=True).then_inc(sem["idb_ok"], 1)
            pool.wait_ge(sem["idb_ok"], 5)
            nc.gpsimd.affine_select(out=ident[:, :], in_=ident[:, :], compare_op=ALU.not_equal, fill=1.0,
                                    base=0, pattern=[[-1, P]], channel_multiplier=1).then_inc(sem["idb_ok"], 1)
            pool.wait_ge(sem["idb_ok"], 6)
            nc.gpsimd.tensor_copy(identb[:, :], ident[:, :]).then_inc(sem["const_ok"], 1)
            split_w(0, 1, None)
            split_w(0, 2, None)

            def add_keys(s, j):
                u = s - 2
                pool.wait_ge(sem["exp_ok"], NS * u + QT * (j + 1))
                if j == 0 and (not isinstance(s, int) or s >= 3):
                    pool.wait_ge(sem["l_mm"], s - 2)
                nc.gpsimd.tensor_tensor(psumk[:, j, :], probs[:, j, 0, :], probs[:, j, 1, :], ALU.add).then_inc(sem["pool_sum"], 1)
                pool.wait_ge(sem["pool_sum"], 2 * HPG * u + 2 * j + 1)
                nc.gpsimd.tensor_tensor(psumk[:, j, :], psumk[:, j, :], probs[:, j, 2, :], ALU.add).then_inc(sem["pool_sum"], 1)
                pool.wait_ge(sem["pool_sum"], 2 * HPG * u + 2 * j + 2)
                nc.gpsimd.tensor_tensor(psumk[:, j, :], psumk[:, j, :], probs[:, j, 3, :], ALU.add).then_inc(sem["psum_ok"], 1)

            def step(s, par, g):
                proj, maxima, finish = stages(s)
                split = proj and par == 1 and (not isinstance(s, int) or s < UNITS - 1)
                if proj:
                    wait_alone(pool, sem["ctxq_in"], 16 * (s + 1))
                    if isinstance(s, int) and s == 0:
                        pool.wait_ge(sem["sc_ok"], 3)
                    nc.gpsimd.tensor_scalar(c_raw[:, :], c_raw[:, :], sc[:, 6:7], sc[:, 3:4], ALU.mult, ALU.add).then_inc(sem["ctxq_1"], 1)
                if finish:
                    add_keys(s, 0)
                if split:
                    split_w(g + 1, 0, 3 * s + 1)
                if finish:
                    add_keys(s, 1)
                    add_keys(s, 2)
                    add_keys(s, 3)
                if split:
                    split_w(g + 1, 1, 3 * s + 2)
                    split_w(g + 1, 2, 3 * s + 3)

            steps_of(pool, step)

            def residual(par, i):
                pool.wait_ge(by_parity["xr_in"][par], 16 * (i + 1))
                nc.gpsimd.tensor_tensor(xres[:, par, :], xres[:, par, :], ob_sb[:, :], ALU.add).then_inc(sem["xr_ok"], 1)

            def rstd(ve, ok, n, row):
                pool.wait_ge(sem[ve], n)
                nc.gpsimd.tensor_tensor(mv[:, row, 2:3], mv[:, row, 1:2], consts[:, 0:1], ALU.pow).then_inc(sem[ok], 1)

            def split_wb(h, k):
                cols = slice(h * 512, (h + 1) * 512)
                pool.wait_ge(sem["wb_hi"], h * KT + k + 1)
                nc.gpsimd.tensor_tensor(big_lo[:, k, cols], wb_raw[:, k, cols], big_hi[:, k, cols].bitcast(f32), ALU.subtract).then_inc(sem["wb_lo_odd"], 1)

            def tail_step(n, par, i):
                more = not isinstance(n, int) or n < NT
                prev = not isinstance(n, int) or n >= 1
                if more:
                    if isinstance(n, int) and n == 0:
                        pool.wait_ge(sem["const_w"], 16)
                    residual(par, i)
                last = isinstance(n, int) and n == NT - 1
                if prev:
                    q = 1 - par
                    if isinstance(n, int) and n == 1:
                        pool.wait_ge(sem["corr_ok"], NB)
                    pool.wait_ge(sem["qp1"], n)
                    nc.gpsimd.tensor_tensor(x1s[:, q, :], x1s[:, q, :], corr[:, q, :], ALU.add).then_inc(sem["x1c_ok"], 1)
                if last:
                    split_wb(0, 1)
                    split_wb(0, 3)
                if more:
                    rstd("ve1", "rstd1", n + 1, 0)
                if last:
                    split_wb(0, 5)
                    split_wb(0, 7)
                    split_wb(1, 1)
                if prev:
                    rstd("ve2", "rstd2", n, 1)
                if last:
                    for k in range(3, KT, 2):
                        split_wb(1, k)

            tail_step(0, 0, 0)
            tail_step(1, 1, 0)
            with pool.Fori(1, NT // 2 - 1) as i:
                tail_step(2 * i, 0, i)
                tail_step(2 * i + 1, 1, i)
            tail_step(NT - 2, 0, NT // 2 - 1)
            tail_step(NT - 1, 1, NT // 2 - 1)

            def last_step(n, par, i):
                pool.wait_ge(by_parity["x2_in"][par], 16 * (i + 1))
                if not isinstance(n, int) or n >= 2:
                    pool.wait_ge(sem["r3_ok"], n - 1)
                nc.gpsimd.tensor_tensor(xb[:, par, :], x2s[:, par, :], bb_sb[:, :], ALU.add).then_inc(sem["xb_ok"], 1)
                if isinstance(n, int) and n == 0:
                    tail_step(NT, 0, NT // 2)
                rstd("ve3", "rstd3", n + 1, 0)

            pool.wait_ge(sem["bt_in"], 32)
            last_step(0, 0, 0)
            last_step(1, 1, 0)
            with pool.Fori(1, NT // 2) as i:
                last_step(2 * i, 0, i)
                last_step(2 * i + 1, 1, i)

        @block.vector
        def _(dve):
            def split_wq(half):
                ks = slice(half * KT // 2, (half + 1) * KT // 2)
                dve.wait_ge(sem["wq_hi"], half + 1)
                nc.vector.tensor_tensor(w_lo[:, 0, ks], w_raw[:, 0, ks], w_hi[:, 0, ks].bitcast(f32), ALU.subtract).then_inc(sem["wq_lo"], 1)

            def split_x(b, ks):
                cols = slice(b * S, (b + 1) * S)
                for k in ks:
                    if b == 0 and k in (0, 2):
                        split_wq(k // 2)
                    dve.wait_ge(sem["x_hi_ok"], b * KT + k + 1)
                    nc.vector.tensor_tensor(big_lo[:, k, cols], big_raw[:, k, cols], big_hi[:, k, cols].bitcast(f32), ALU.subtract).then_inc(sem["x_lo_ok"], 1)

            split_x(0, range(KT))
            dve.wait_ge(sem["const_in"], 16 * 5)
            nc.vector.reciprocal(sc[:, 4:5], sc[:, 0:1])
            nc.vector.reciprocal(sc[:, 6:7], sc[:, 2:3])
            nc.vector.tensor_scalar(sc[:, 5:6], sc[:, 0:1], sc[:, 2:3], None, ALU.mult)
            nc.vector.tensor_scalar(sc[:, 7:8], sc[:, 1:2], 0.0, QMAX, ALU.max, ALU.min)
            nc.vector.tensor_scalar(sc[:, 8:9], sc[:, 3:4], 0.0, QMAX, ALU.max, ALU.min).then_inc(sem["sc_ok"], 1)
            dve.wait_ge(sem["sc_ok"], 1)
            nc.vector.tensor_scalar(sc[:, 7:9], sc[:, 7:9], MAGIC, -MAGIC, ALU.add, ALU.add).then_inc(sem["sc_ok"], 1)
            dve.wait_ge(sem["sc_ok"], 2)
            nc.vector.tensor_tensor(sc[:, 9:10], sc[:, 7:8], sc[:, 1:2], ALU.subtract)
            nc.vector.tensor_tensor(sc[:, 10:11], sc[:, 8:9], sc[:, 3:4], ALU.subtract).then_inc(sem["sc_ok"], 1)
            dve.wait_ge(sem["sc_ok"], 3)
            for n in range(2):
                last = nc.vector.tensor_scalar(consts[:, 1 + n:2 + n], sc[:, 7 + n:8 + n], MAGIC, None, ALU.add)
            last.then_inc(sem["sc_ok"], 1)
            dve.wait_ge(sem["sc_ok"], 4)

            def split_ow(h, k):
                cols = slice(h * S, (h + 1) * S)
                dve.wait_ge(sem["ow_hi"], h * KT + k + 1)
                nc.vector.tensor_tensor(big_lo[:, k, cols], big_raw[:, k, cols], big_hi[:, k, cols].bitcast(f32), ALU.subtract).then_inc(sem["ow_lo"], 1)

            def divide(u):
                if not isinstance(u, int) or u >= 1:
                    dve.wait_ge(sem["ctx_ok"], u)
                dve.wait_ge(sem["l_mm"], u + 1)
                nc.vector.reciprocal(recip[:, :], bank(LSUM)).then_inc(sem["recip_ok"], 1)
                dve.wait_ge(sem["recip_ok"], u + 1)
                if not isinstance(u, int) or u >= 1:
                    dve.wait_ge(sem["ctx_out"], 16 * u)
                nc.vector.tensor_tensor(ctxs[:, :], bank(context_bank(u)), recip[:, :], ALU.mult).then_inc(sem["ctx_ok"], 1)

            def step(s, par, g):
                proj, maxima, finish = stages(s)
                begin = isinstance(s, int) and s == 0

                def low(piece):
                    dve.wait_ge(sem["hi_ok"], 2 * s + piece + 1)
                    hi, lo = ((q_hi, q_lo), (k_hi, k_lo))[piece]
                    nc.vector.scalar_tensor_tensor(lo[:, :], bank(PROJ1 if piece == 0 else PROJ0),
                                                   bias[:, bass.ds(g, 1), piece:piece + 1].rearrange("p a b -> p (a b)"),
                                                   hi[:, :].bitcast(f32), ALU.add, ALU.subtract).then_inc(sem["lo_ok"], 1)

                def clip_context():
                    dve.wait_ge(sem["ctxq_1"], s + 1)
                    if not isinstance(s, int) or s >= 1:
                        dve.wait_ge(sem["c2_out"], 16 * s)
                    nc.vector.tensor_scalar(c_raw[:, :], c_raw[:, :], 0.0, QMAX, ALU.max, ALU.min).then_inc(sem["ctxq_2"], 1)

                def round_context():
                    dve.wait_ge(sem["ctxq_2"], s + 1)
                    nc.vector.tensor_scalar(c_q[:, :], c_raw[:, :], MAGIC, consts[:, 2:3], ALU.add, ALU.subtract).then_inc(sem["ctxq_ok"], 1)

                if maxima:
                    dve.wait_ge(sem["vt_mm"], s)
                    if not isinstance(s, int) or s >= 3:
                        dve.wait_ge(sem["pv_mm"], s - 2)
                    nc.vector.tensor_copy(v_nat[:, 1 - par].rearrange("p t c -> p (t c)"), bank(PROJ0)).then_inc(sem["v_ok"], 1)
                if divides(s) and proj:
                    divide(s - 3)
                for n in range(NS):
                    if maxima:
                        dve.wait_ge(sem["max_mm"], NS * (s - 1) + n + 1)
                        if n == 0 and (not isinstance(s, int) or s >= 2):
                            dve.wait_ge(sem["m_mm"], s - 1)
                        nc.vector.reduce_max(m_col[:, n:n + 1], bank(MAX0 + n % 2), AX).then_inc(sem["rowmax"], 1)
                    if proj and n in (3, 10):
                        low(0 if n == 3 else 1)
                    if proj and n == 8 and not begin:
                        clip_context()
                    if begin and n in (3, 10):
                        split_x(1, range(4) if n == 3 else range(4, KT))
                    if proj and n == 12 and not begin:
                        round_context()
                if begin:
                    clip_context()
                    round_context()
                    nc.vector.memset(kp[SHIFT:SHIFT + 2, :, :, :].bitcast(f32), -1.0).then_inc(sem["minus_ok"], 1)
                if maxima:
                    dve.wait_ge(sem["m_mm"], s)
                    if not isinstance(s, int) or s >= 2:
                        dve.wait_ge(sem["shift_in"], 32 * (s - 1))
                    nc.vector.tensor_copy(m_row[:, 0, :], banks[rows_bank(s)][0:NS, 0:P]).then_inc(sem["m_hi_ok"], 1)
                    dve.wait_ge(sem["m_hi_ok"], s)
                    nc.vector.tensor_tensor(m_row[:, 1, :], banks[rows_bank(s)][0:NS, 0:P], m_row[:, 0, :].bitcast(f32), ALU.subtract).then_inc(sem["m_ok"], 1)
                if not proj:
                    divide(s - 3)

            step(0, 0, 0)
            step(1, 1, 0)
            step(2, 0, 1)
            step(3, 1, 1)
            with dve.Fori(2, G - 1) as g:
                step(2 * g, 0, g)
                step(2 * g + 1, 1, g)
            step(UNITS - 2, 0, G - 1)
            step(UNITS - 1, 1, G - 1)
            step(UNITS, 0, G)

            def column_correction(b):
                dve.wait_ge(sem["cs_mm"], b + 1)
                for h in range(2):
                    last = nc.vector.tensor_scalar(corr[:, b, h * 512:(h + 1) * 512], bank(2 - 2 * b + h), sc[:, 9:10], sc[:, 5:6], ALU.mult, ALU.mult)
                last.then_inc(sem["corr_ok"], 1)

            def split_first_tile(q):
                dve.wait_ge(sem["cx_hi_ok"], q + 1)
                nc.vector.tensor_tensor(cx_lo[q][:, 0:KT - 1], cx_raw[:, q, 0:KT - 1], cx_hi[q][:, 0:KT - 1].bitcast(f32), ALU.subtract).then_inc(sem["cx_lo_ok"], 1)

            def split_last_group(q):
                dve.wait_ge(sem["cx7_hi"], q + 1)
                nc.vector.tensor_tensor(cx_lo[q][:, KT - 1, :], cx_raw[:, q, KT - 1, :], cx_hi[q][:, KT - 1, :].bitcast(f32), ALU.subtract).then_inc(sem["cx7_lo"], 1)

            for k in range(2):
                split_ow(0, k)
            divide(UNITS - 2)
            column_correction(0)
            for k in range(2, KT):
                split_ow(0, k)
            split_first_tile(0)
            split_last_group(0)
            column_correction(1)
            for k in range(KT):
                split_ow(1, k)
            split_first_tile(1)
            divide(UNITS - 1)

            def split_cx(n, par):
                dve.wait_ge(sem["cx_hi_ok"], n + 1)
                nc.vector.tensor_tensor(cx_lo[par][:, :], cx_raw[:, par], cx_hi[par][:, :].bitcast(f32), ALU.subtract).then_inc(sem["cx_lo_ok"], 1)

            def stats(r, row, n, a, b, c):
                for h in range(2):
                    last = nc.vector.bn_stats(st[:, row, h, :], r[:, h * 512:(h + 1) * 512])
                last.then_inc(sem[a], 1)
                aggregate(row, n, a, b, c)

            def aggregate(row, n, a, b, c):
                wait_alone(dve, sem[a], n)
                nc.vector.bn_aggr(mv[:, row, 0:2], st[:, row].rearrange("p a b -> p (a b)")).then_inc(sem[b], 1)
                dve.wait_ge(sem[b], n)
                nc.vector.tensor_scalar(mv[:, row, 1:2], mv[:, row, 1:2], EPS, None, ALU.add).then_inc(sem[c], 1)

            def minus_mean(row, n, ok, done):
                dve.wait_ge(sem[ok], n)
                nc.vector.tensor_scalar(mv[:, row, 3:4], mv[:, row, 0:1], mv[:, row, 2:3], -1.0, ALU.mult, ALU.mult).then_inc(sem[done], 1)

            def row_correction(m):
                dve.wait_ge(sem["rs_mm"], m + 1)
                nc.vector.tensor_scalar(kcol[:, 0:1], banks[5][:, 0:1], sc[:, 10:11], sc[:, 11:12], ALU.mult, ALU.add).then_inc(sem["k1"], 1)
                dve.wait_ge(sem["k1"], m + 1)
                nc.vector.tensor_scalar(kcol[:, 1:2], kcol[:, 0:1], sc[:, 5:6], None, ALU.mult).then_inc(sem["kc_ok"], 1)

            def add_product(m, q):
                dve.wait_ge(sem["t_ok"], m + 1)
                dve.wait_ge(sem["x1c_ok"], m + 1)
                nc.vector.tensor_tensor(x1s[:, q, :], x1s[:, q, :], qtmp[:, q, :], ALU.add).then_inc(sem["r2_ok"], 1)

            def product_stats(m, q):
                dve.wait_ge(sem["r2_ok"], m + 1)
                stats(x1s[:, q, :], 1, m + 1, "st2", "mv2", "ve2")

            def split_wb(h, k):
                cols = slice(h * 512, (h + 1) * 512)
                dve.wait_ge(sem["wb_hi"], h * KT + k + 1)
                nc.vector.tensor_tensor(big_lo[:, k, cols], wb_raw[:, k, cols], big_hi[:, k, cols].bitcast(f32), ALU.subtract).then_inc(sem["wb_lo_even"], 1)

            def split_x2T(n, par):
                dve.wait_ge(sem["xt_ok"], n + 1)
                if not isinstance(n, int) or n >= 2:
                    dve.wait_ge(sem["c_mm"], n - 1)
                nc.vector.tensor_copy(x2T_hi[par][:].rearrange("p k c -> p (k c)"), x2T[:].rearrange("p k c -> p (k c)")).then_inc(sem["xthi_ok"], 1)
                dve.wait_ge(sem["xthi_ok"], n + 1)
                nc.vector.tensor_tensor(x2T_lo[par][:, :, :], x2T[:, :, :], x2T_hi[par][:, :, :].bitcast(f32), ALU.subtract).then_inc(sem["xtlo_ok"], 1)

            def route(n):
                logits = banks[4][:, ER:ER + NE]
                wait_alone(dve, sem["h_mm"], n + 1)
                nc.vector.max(rt[:, 0:8], logits).then_inc(sem["rv1"], 1)
                wait_alone(dve, sem["rv1"], n + 1)
                nc.vector.max_index(ridx[:, :], rt[:, 0:8], logits).then_inc(sem["rv2"], 1)
                nc.vector.tensor_scalar(rt[:, 16:17], rt[:, 0:1], -1.0, None, ALU.mult).then_inc(sem["rv3"], 1)
                dve.wait_ge(sem["rv2"], n + 1)
                nc.vector.tensor_copy(rt[:, 21:23], ridx[:, 0:2]).then_inc(sem["rw1"], 1)
                dve.wait_ge(sem["re_ok"], n + 1)
                nc.vector.tensor_tensor(rt[:, 17:18], rt[:, 8:9], rt[:, 9:10], ALU.add).then_inc(sem["rw2"], 1)
                dve.wait_ge(sem["rw2"], n + 1)
                nc.vector.reciprocal(rt[:, 18:19], rt[:, 17:18]).then_inc(sem["rw3"], 1)
                dve.wait_ge(sem["rw3"], n + 1)
                nc.vector.tensor_scalar(rt[:, 19:21], rt[:, 8:10], rt[:, 18:19], SCALING, ALU.mult, ALU.mult).then_inc(sem["rw4"], 1)
                dve.wait_ge(sem["rw4"], n + 1)
                dve.wait_ge(sem["rw1"], n + 1)
                for e in range(2):
                    last = nc.vector.tensor_scalar(rt[:, 24 + 8 * e:32 + 8 * e], iota[:, :], rt[:, 21 + e:22 + e], rt[:, 19 + e:20 + e],
                                                   ALU.is_equal, ALU.mult)
                last.then_inc(sem["rw5"], 1)
                dve.wait_ge(sem["rw5"], n + 1)
                nc.vector.tensor_tensor(rt[:, 24:32], rt[:, 24:32], rt[:, 32:40], ALU.add).then_inc(sem["comb_ok"], 1)
                dve.wait_ge(sem["comb_ok"], n + 1)
                if not isinstance(n, int) or n >= 1:
                    dve.wait_ge(sem["hwt_mm"], n)
                nc.vector.tensor_tensor(hw[:, :].rearrange("p (e r) -> p e r", r=R), banks[4][:, 0:ER].rearrange("p (e r) -> p e r", r=R),
                                        rt[:, 24:32].unsqueeze(2).to_broadcast([P, NE, R]), ALU.mult).then_inc(sem["hw_ok"], 1)

            def split_hw(n):
                dve.wait_ge(sem["hwt_mm"], n + 1)
                if not isinstance(n, int) or n >= 1:
                    dve.wait_ge(sem["c_mm"], n)
                nc.vector.tensor_copy(hwT_hi[:, :], banks[5][:, 0:P]).then_inc(sem["hwthi_ok"], 1)
                dve.wait_ge(sem["hwthi_ok"], n + 1)
                nc.vector.tensor_tensor(hwT_lo[:, :], banks[5][:, 0:P], hwT_hi[:, :].bitcast(f32), ALU.subtract).then_inc(sem["hwtlo_ok"], 1)

            def tail_step(n, par, i):
                prev = not isinstance(n, int) or n >= 1
                last = isinstance(n, int) and n == NT - 1
                q = 1 - par
                if not last and (not isinstance(n, int) or n >= 1):
                    split_cx(n + 1, q)
                dve.wait_ge(sem["a_mm"], n + 1)
                dve.wait_ge(sem["xr_ok"], n + 1)
                if not isinstance(n, int) or n >= 2:
                    dve.wait_ge(sem["x2_ok"], n - 1)
                for h in range(2):
                    cols = slice(h * 512, (h + 1) * 512)
                    nc.vector.tensor_tensor(x1s[:, par, cols], bank(h), xres[:, par, cols], ALU.add).then_inc(sem["r1_ok" if h else "r1_half"], 1)
                if isinstance(n, int) and n == 0:
                    split_last_group(1)
                if last:
                    row_correction(n - 1)
                dve.wait_ge(sem["r1_ok"], n + 1)
                stats(x1s[:, par, :], 0, n + 1, "st1", "mv1", "ve1")
                if last:
                    split_wb(0, 0)
                minus_mean(0, n + 1, "rstd1", "nm1")
                if last:
                    for k in range(2, KT, 2):
                        split_wb(0, k)
                    split_x2T(0, 0)
                elif prev:
                    row_correction(n - 1)
                if prev:
                    add_product(n - 1, q)
                    product_stats(n - 1, q)
                dve.wait_ge(sem["qp1"], n + 1)
                nc.vector.tensor_scalar(qtmp[:, par, :], qtmp[:, par, :], 0.0, QMAX, ALU.max, ALU.min).then_inc(sem["qp2"], 1)
                dve.wait_ge(sem["qp2"], n + 1)
                if prev:
                    dve.wait_ge(sem["tr_mm"], n)
                else:
                    dve.wait_ge(sem["ctx_out"], 16 * UNITS)
                nc.vector.tensor_scalar(c1[:, :], qtmp[:, par, :], MAGIC, consts[:, 1:2], ALU.add, ALU.subtract).then_inc(sem["c1_ok"], 1)
                if last:
                    route(0)
                if prev:
                    minus_mean(1, n, "rstd2", "nm2")

            nc.vector.tensor_scalar(sc[:, 11:12], sc[:, 9:10], sc[:, 10:11], float(H), ALU.mult, ALU.mult).then_inc(sem["sc_ok"], 1)
            dve.wait_ge(sem["sc_ok"], 5)

            tail_step(0, 0, 0)
            tail_step(1, 1, 0)
            with dve.Fori(1, NT // 2 - 1) as i:
                tail_step(2 * i, 0, i)
                tail_step(2 * i + 1, 1, i)
            tail_step(NT - 2, 0, NT // 2 - 1)
            tail_step(NT - 1, 1, NT // 2 - 1)
            for k in range(0, KT, 2):
                split_wb(1, k)

            def last_step(n, par, i, more):
                if not isinstance(n, int) or n >= 2:
                    route(n)
                split_hw(n)
                if more:
                    split_x2T(n + 1, 1 - par)
                if isinstance(n, int) and n == 0:
                    row_correction(NT - 1)
                    add_product(NT - 1, 1)
                    route(1)
                    product_stats(NT - 1, 1)
                    minus_mean(1, NT, "rstd2", "nm2")
                if more:
                    dve.wait_ge(sem["c_mm"], n + 1)
                dve.wait_ge(sem["xb_ok"], n + 1)
                if not isinstance(n, int) or n >= 2:
                    dve.wait_ge(by_parity["o_out"][par], 16 * i)
                if more:
                    for h in range(2):
                        cols = slice(h * 512, (h + 1) * 512)
                        last = nc.vector.tensor_tensor(r3[:, par, cols], bank(2 * par + h), xb[:, par, cols], ALU.add)
                    last.then_inc(sem["r3_ok"], 1)
                    dve.wait_ge(sem["r3_ok"], n + 1)
                if not isinstance(n, int) or n >= 1:
                    dve.wait_ge(sem["o_ok"], n)
                if more:
                    stats(r3[:, par, :], 0, n + 1, "st3", "mv3", "ve3")
                    minus_mean(0, n + 1, "rstd3", "nm3")
                    return
                for h in range(2):
                    cols = slice(h * 512, (h + 1) * 512)
                    dve.wait_ge(sem["c_mm" if h else "c_half"], n + 1 if h else 1)
                    nc.vector.tensor_tensor(r3[:, par, cols], bank(2 * par + h), xb[:, par, cols], ALU.add).then_inc(sem["r3_ok" if h else "r3_half"], 1)
                    dve.wait_ge(sem["r3_ok" if h else "r3_half"], n + 1 if h else 1)
                    last = nc.vector.bn_stats(st[:, 0, h, :], r3[:, par, cols])
                last.then_inc(sem["st3"], 1)
                aggregate(0, n + 1, "st3", "mv3", "ve3")
                minus_mean(0, n + 1, "rstd3", "nm3")
                dve.wait_ge(sem["nm3"], n + 1)
                nc.vector.tensor_scalar(r3[:, par, 512:1024], r3[:, par, 512:1024], mv[:, 0, 2:3], mv[:, 0, 3:4], ALU.mult, ALU.add).then_inc(sem["o_second"], 1)

            dve.wait_ge(sem["bt_in"], 32)
            nc.vector.tensor_copy(bt_hi[:, :], bt_raw[:, :]).then_inc(sem["bt_hi_ok"], 1)
            dve.wait_ge(sem["bt_hi_ok"], 1)
            nc.vector.tensor_tensor(bt_lo[:, :], bt_raw[:, :], bt_hi[:, :].bitcast(f32), ALU.subtract).then_inc(sem["bt_ok"], 1)
            last_step(0, 0, 0, True)
            last_step(1, 1, 0, True)
            with dve.Fori(1, NT // 2 - 1) as i:
                last_step(2 * i, 0, i, True)
                last_step(2 * i + 1, 1, i, True)
            last_step(NT - 2, 0, NT // 2 - 1, True)
            last_step(NT - 1, 1, NT // 2 - 1, False)


def kernel(x, ctx_4096, L0_attn_attn_qkvw, L0_attn_attn_qkvb, L0_attn_attn_ow, L0_attn_attn_ob,
           L0_xattn_x1_scale, L0_xattn_x1_zp, L0_xattn_x2_scale, L0_xattn_x2_zp,
           L0_ffn_W_base, L0_ffn_b_base, L0_ffn_W_router, L0_ffn_A, L0_ffn_B):
    import numpy as np
    import concourse.bacc as bacc
    from concourse.bass_utils import run_bass_kernel_spmd

    P = 128
    B, S, H = x.shape
    G = H // P
    c = np.ascontiguousarray
    x2d = np.asarray(x).reshape(B * S, H)
    arrays = {
        "xT": c(x2d.T),
        "x": c(x2d),
        "wqkv": c(np.asarray(L0_attn_attn_qkvw).reshape(G, P, 3, G, P).transpose(3, 1, 2, 0, 4)),
        "qkvb": c(np.asarray(L0_attn_attn_qkvb).reshape(3, G, P).transpose(2, 1, 0)),
        "ow": c(L0_attn_attn_ow),
        "ob": c(L0_attn_attn_ob),
        "ctx": c(ctx_4096),
        "scales": c(np.stack([np.asarray(a).reshape(1) for a in (L0_xattn_x1_scale, L0_xattn_x1_zp, L0_xattn_x2_scale, L0_xattn_x2_zp)])),
        "wbT": c(np.asarray(L0_ffn_W_base).T),
        "bb": c(L0_ffn_b_base),
    }
    E, R, _ = L0_ffn_A.shape
    ar = np.concatenate([np.asarray(L0_ffn_A).reshape(E * R, H), np.asarray(L0_ffn_W_router)], axis=0)
    arrays["art"] = c(ar.T.reshape(G, P, E * R + E).transpose(1, 0, 2))
    arrays["bt"] = c(np.asarray(L0_ffn_B).transpose(0, 2, 1).reshape(E * R, H))

    nc = bacc.Bacc("TRN2", target_bir_lowering=False, num_devices=1)
    aps = [nc.dram_tensor(f"in_{n}", a.shape, mybir.dt.from_np(a.dtype), kind="ExternalInput").ap() for n, a in arrays.items()]
    out = nc.dram_tensor("out", (B * S, H), mybir.dt.float32, kind="ExternalOutput").ap()
    decoder_layer(nc, *aps, out)
    r = run_bass_kernel_spmd(nc, [{f"in_{n}": a for n, a in arrays.items()}], core_ids=[0])
    return r.results[0]["out"].reshape(B, S, H)
```
